# Optimizing a Trainium2 kernel written in Bass

```python
import numpy as np
import jax
import jax.numpy as jnp

def _softmax(x, axis=-1):
    return jax.nn.softmax(x, axis=axis)

def _gelu(x):
    return jax.nn.gelu(x, approximate=True)

def _silu(x):
    return jax.nn.silu(x)

def _sigmoid(x):
    return jax.nn.sigmoid(x)

def _layernorm(x, axis=-1, eps=1e-05):
    m = jnp.mean(x, axis=axis, keepdims=True)
    v = jnp.var(x, axis=axis, keepdims=True)
    return (x - m) / jnp.sqrt(v + eps)

def _scatter_add(tgt, idx, src, axis=0):
    return tgt.at[idx].add(src)

def _segment_sum(src, seg, n):
    return jax.ops.segment_sum(src, seg, n)
kernel_name = 'mk_gnn_preln_d2_gnn_r32_5d701c'

def setup_inputs(seed: int=0):
    np.random.seed(seed)
    _w = jnp.asarray

    def _rec_inputs():
        import jax
        import jax.numpy as jnp
        _gk = jax.random.key(seed)
        x = -0.0005121 + 1.001 * jax.random.normal(jax.random.fold_in(_gk, 1), (3125, 160), jnp.float32)
        _s = jax.random.randint(jax.random.fold_in(_gk, 2), (25000,), 0, 3125, jnp.int32)
        _d = jax.random.randint(jax.random.fold_in(_gk, 3), (25000,), 0, 3125, jnp.int32)
        _loop = jnp.arange(3125, dtype=jnp.int32)
        src = jnp.concatenate([_s, _d, _loop])
        dst = jnp.concatenate([_d, _s, _loop])
        _o = jnp.argsort(dst, stable=True)
        src = src[_o]
        dst = dst[_o]
        edge_attr_16 = jax.random.uniform(jax.random.fold_in(_gk, 11), (53125, 16), jnp.float32, 0.0, 1)
        edge_attr_4 = 0.000898722 + 1.00012 * jax.random.normal(jax.random.fold_in(_gk, 12), (53125, 4), jnp.float32)
        node_vec1 = -0.00915711 + 0.999674 * jax.random.normal(jax.random.fold_in(_gk, 14), (3125, 1), jnp.float32)
        return (x, src, dst, edge_attr_16, edge_attr_4, node_vec1)
    x, src, dst, edge_attr_16, edge_attr_4, node_vec1 = _rec_inputs()

    def _L0_gnn_setup():
        import jax, jax.numpy as jnp
        import numpy as np
        N, E = (625, 10000)
        CS, CV = (64, 32)
        AS_, AV, H = (16, 8, 4)
        NB = 16
        SQRT3 = 1.7320508075688772
        SQRT2 = 1.4142135623730951
        EPS = 1e-05

        def _cg_tp(s, v, y0, y1, w_ss, w_sv, w_vs, w_vv0, w_vv1):
            out_s = jnp.concatenate([w_ss * s * y0[:, None], w_vv0 * (jnp.einsum('eci,ei->ec', v, y1) / SQRT3)], axis=-1)
            out_v = jnp.concatenate([(w_sv * s)[:, :, None] * y1[:, None, :], (w_vs * jnp.ones_like(v[..., 0]))[..., None] * v * y0[:, None, None], (w_vv1 * jnp.ones_like(v[..., 0]))[..., None] * (jnp.cross(v, y1[:, None, :]) / SQRT2)], axis=1)
            return (out_s, out_v)

        def _equiv_layernorm(s, v, gamma_s, beta_s, gamma_v):
            mu = jnp.mean(s, axis=-1, keepdims=True)
            var = jnp.var(s, axis=-1, keepdims=True)
            s_n = (s - mu) * jax.lax.rsqrt(var + EPS) * gamma_s + beta_s
            rms = jnp.sqrt(jnp.mean(jnp.sum(v * v, axis=-1), axis=-1, keepdims=True) + EPS)
            v_n = v / rms[..., None] * gamma_v[None, :, None]
            return (s_n, v_n)
        key = jax.random.key(seed)
        ks = jax.random.split(key, 26)

        def rn(k, shape, fan):
            return jax.random.normal(k, shape, jnp.float32) / np.sqrt(fan)
        D1S, D1V = (CS + CV, CS + 2 * CV)
        WN = 2 * CS + 3 * CV
        inp = {'node': jax.random.normal(ks[0], (N, CS + 3 * CV), jnp.float32), 'edge_index': jax.random.randint(ks[1], (2, E), 0, N, jnp.int64 if jax.config.jax_enable_x64 else jnp.int32), 'rbf': jax.random.uniform(ks[2], (E, NB), jnp.float32), 'rsh': jax.random.normal(ks[3], (E, 4), jnp.float32), 'gamma_s': jnp.ones((CS,), jnp.float32), 'beta_s': jnp.zeros((CS,), jnp.float32), 'gamma_v': jnp.ones((CV,), jnp.float32), 'Ws_src': rn(ks[4], (CS, CS), CS), 'Wv_src': rn(ks[5], (CV, CV), CV), 'Ws_dst': rn(ks[6], (CS, CS), CS), 'Wv_dst': rn(ks[7], (CV, CV), CV), 'W_rbf': rn(ks[8], (NB, WN), NB), 'W_alpha': rn(ks[9], (D1S, H * AS_), D1S), 'alpha_dot': rn(ks[10], (1, H, AS_), AS_), 'Ws_val': rn(ks[11], (D1S, CS), D1S), 'Wv_val': rn(ks[12], (D1V, CV), D1V), 'Wg': rn(ks[13], (CS, CV), CS), 'w2_ss': rn(ks[14], (CS,), 1), 'w2_sv': rn(ks[15], (CS,), 1), 'w2_vs': rn(ks[16], (CV,), 1), 'w2_vv0': rn(ks[17], (CV,), 1), 'w2_vv1': rn(ks[18], (CV,), 1), 'Ws_vlin': rn(ks[19], (D1S, H * AS_), D1S), 'Wv_vlin': rn(ks[20], (D1V, H * AV), D1V), 'Wps': rn(ks[21], (H * AS_, CS), H * AS_), 'Wpv': rn(ks[22], (H * AV, CV), H * AV)}
        return inp
    _L0_gnn_all = _L0_gnn_setup()
    _L0_gnn_in = {k: v for k, v in _L0_gnn_all.items() if k in ('gamma_s', 'beta_s', 'gamma_v', 'Ws_src', 'Wv_src', 'Ws_dst', 'Wv_dst', 'W_rbf', 'W_alpha', 'alpha_dot', 'Ws_val', 'Wv_val', 'Wg', 'w2_ss', 'w2_sv', 'w2_vs', 'w2_vv0', 'w2_vv1', 'Ws_vlin', 'Wv_vlin', 'Wps', 'Wpv')}
    del _L0_gnn_all

    def _L1_gnn_setup():
        import jax, jax.numpy as jnp
        import numpy as np
        MUL0, MUL1 = (64, 32)
        INV_SQRT3 = 1.0 / np.sqrt(3.0)

        def _split(x):
            return (x[:, :MUL0], x[:, MUL0:].reshape(x.shape[0], MUL1, 3))

        def _merge(o0, o1):
            return jnp.concatenate([o0, o1.reshape(o1.shape[0], -1)], axis=-1)

        def _tp(x0, x1, y0, y1, w000, w011, w101, w110):
            fan0 = x0.shape[1] * y0.shape[1] + x1.shape[1] * y1.shape[1]
            fan1 = x0.shape[1] * y1.shape[1] + x1.shape[1] * y0.shape[1]
            out0 = (jnp.einsum('eu,ev,uvw->ew', x0, y0, w000) + INV_SQRT3 * jnp.einsum('euk,evk,uvw->ew', x1, y1, w110)) / np.sqrt(fan0)
            out1 = (jnp.einsum('eu,evk,uvw->ewk', x0, y1, w011) + jnp.einsum('euk,ev,uvw->ewk', x1, y0, w101)) / np.sqrt(fan1)
            return (out0, out1)

        def _lin(x0, x1, w0, w1):
            return (x0 @ w0 / np.sqrt(x0.shape[1]), jnp.einsum('euk,uv->evk', x1, w1) / np.sqrt(x1.shape[1]))
        key = jax.random.key(seed)
        ks = jax.random.split(key, 20)
        N, E = (50000, 15625)
        inp = {'node_features': jax.random.normal(ks[0], (N, MUL0 + 3 * MUL1), dtype=jnp.float32), 'edge_index': jax.random.randint(ks[1], (2, E), 0, N, dtype=jnp.int64), 'edge_attr_tensor': jax.random.normal(ks[2], (E, 4), dtype=jnp.float32), 'node_attr_scalar_raw': jax.random.normal(ks[3], (N, 1), dtype=jnp.float32), 'wm000': jax.random.normal(ks[4], (MUL0, 1, MUL0), dtype=jnp.float32), 'wm011': jax.random.normal(ks[5], (MUL0, 1, MUL1), dtype=jnp.float32), 'wm101': jax.random.normal(ks[6], (MUL1, 1, MUL1), dtype=jnp.float32), 'wm110': jax.random.normal(ks[7], (MUL1, 1, MUL0), dtype=jnp.float32), 'lm0': jax.random.normal(ks[8], (MUL0, MUL0), dtype=jnp.float32), 'lm1': jax.random.normal(ks[9], (MUL1, MUL1), dtype=jnp.float32), 'wu000': jax.random.normal(ks[10], (MUL0, MUL0, MUL0), dtype=jnp.float32), 'wu011': jax.random.normal(ks[11], (MUL0, MUL1, MUL1), dtype=jnp.float32), 'wu101': jax.random.normal(ks[12], (MUL1, MUL0, MUL1), dtype=jnp.float32), 'wu110': jax.random.normal(ks[13], (MUL1, MUL1, MUL0), dtype=jnp.float32), 'lu0': jax.random.normal(ks[14], (MUL0, MUL0), dtype=jnp.float32), 'lu1': jax.random.normal(ks[15], (MUL1, MUL1), dtype=jnp.float32)}
        return inp
    _L1_gnn_all = _L1_gnn_setup()
    _L1_gnn_in = {k: v for k, v in _L1_gnn_all.items() if k in ('wm000', 'wm011', 'wm101', 'wm110', 'lm0', 'lm1', 'wu000', 'wu011', 'wu101', 'wu110', 'lu0', 'lu1')}
    del _L1_gnn_all
    return {'x': x, 'src': src, 'dst': dst, 'edge_attr_16': edge_attr_16, 'edge_attr_4': edge_attr_4, 'node_vec1': node_vec1, 'L0_gnn_gamma_s': _L0_gnn_in['gamma_s'], 'L0_gnn_beta_s': _L0_gnn_in['beta_s'], 'L0_gnn_gamma_v': _L0_gnn_in['gamma_v'], 'L0_gnn_Ws_src': _L0_gnn_in['Ws_src'], 'L0_gnn_Wv_src': _L0_gnn_in['Wv_src'], 'L0_gnn_Ws_dst': _L0_gnn_in['Ws_dst'], 'L0_gnn_Wv_dst': _L0_gnn_in['Wv_dst'], 'L0_gnn_W_rbf': _L0_gnn_in['W_rbf'], 'L0_gnn_W_alpha': _L0_gnn_in['W_alpha'], 'L0_gnn_alpha_dot': _L0_gnn_in['alpha_dot'], 'L0_gnn_Ws_val': _L0_gnn_in['Ws_val'], 'L0_gnn_Wv_val': _L0_gnn_in['Wv_val'], 'L0_gnn_Wg': _L0_gnn_in['Wg'], 'L0_gnn_w2_ss': _L0_gnn_in['w2_ss'], 'L0_gnn_w2_sv': _L0_gnn_in['w2_sv'], 'L0_gnn_w2_vs': _L0_gnn_in['w2_vs'], 'L0_gnn_w2_vv0': _L0_gnn_in['w2_vv0'], 'L0_gnn_w2_vv1': _L0_gnn_in['w2_vv1'], 'L0_gnn_Ws_vlin': _L0_gnn_in['Ws_vlin'], 'L0_gnn_Wv_vlin': _L0_gnn_in['Wv_vlin'], 'L0_gnn_Wps': _L0_gnn_in['Wps'], 'L0_gnn_Wpv': _L0_gnn_in['Wpv'], 'L1_gnn_wm000': _L1_gnn_in['wm000'], 'L1_gnn_wm011': _L1_gnn_in['wm011'], 'L1_gnn_wm101': _L1_gnn_in['wm101'], 'L1_gnn_wm110': _L1_gnn_in['wm110'], 'L1_gnn_lm0': _L1_gnn_in['lm0'], 'L1_gnn_lm1': _L1_gnn_in['lm1'], 'L1_gnn_wu000': _L1_gnn_in['wu000'], 'L1_gnn_wu011': _L1_gnn_in['wu011'], 'L1_gnn_wu101': _L1_gnn_in['wu101'], 'L1_gnn_wu110': _L1_gnn_in['wu110'], 'L1_gnn_lu0': _L1_gnn_in['lu0'], 'L1_gnn_lu1': _L1_gnn_in['lu1']}

def reference(x, src, dst, edge_attr_16, edge_attr_4, node_vec1, L0_gnn_gamma_s, L0_gnn_beta_s, L0_gnn_gamma_v, L0_gnn_Ws_src, L0_gnn_Wv_src, L0_gnn_Ws_dst, L0_gnn_Wv_dst, L0_gnn_W_rbf, L0_gnn_W_alpha, L0_gnn_alpha_dot, L0_gnn_Ws_val, L0_gnn_Wv_val, L0_gnn_Wg, L0_gnn_w2_ss, L0_gnn_w2_sv, L0_gnn_w2_vs, L0_gnn_w2_vv0, L0_gnn_w2_vv1, L0_gnn_Ws_vlin, L0_gnn_Wv_vlin, L0_gnn_Wps, L0_gnn_Wpv, L1_gnn_wm000, L1_gnn_wm011, L1_gnn_wm101, L1_gnn_wm110, L1_gnn_lm0, L1_gnn_lm1, L1_gnn_wu000, L1_gnn_wu011, L1_gnn_wu101, L1_gnn_wu110, L1_gnn_lu0, L1_gnn_lu1):
    import jax
    import jax.numpy as jnp

    def _L0_gnn_ref(node, rbf, rsh, gamma_s, beta_s, gamma_v, Ws_src, Wv_src, Ws_dst, Wv_dst, W_rbf, W_alpha, alpha_dot, Ws_val, Wv_val, Wg, w2_ss, w2_sv, w2_vs, w2_vv0, w2_vv1, Ws_vlin, Wv_vlin, Wps, Wpv, edge_index):
        import jax, jax.numpy as jnp
        import numpy as np
        N, E = (625, 10000)
        CS, CV = (64, 32)
        AS_, AV, H = (16, 8, 4)
        NB = 16
        SQRT3 = 1.7320508075688772
        SQRT2 = 1.4142135623730951
        EPS = 1e-05

        def _cg_tp(s, v, y0, y1, w_ss, w_sv, w_vs, w_vv0, w_vv1):
            out_s = jnp.concatenate([w_ss * s * y0[:, None], w_vv0 * (jnp.einsum('eci,ei->ec', v, y1) / SQRT3)], axis=-1)
            out_v = jnp.concatenate([(w_sv * s)[:, :, None] * y1[:, None, :], (w_vs * jnp.ones_like(v[..., 0]))[..., None] * v * y0[:, None, None], (w_vv1 * jnp.ones_like(v[..., 0]))[..., None] * (jnp.cross(v, y1[:, None, :]) / SQRT2)], axis=1)
            return (out_s, out_v)

        def _equiv_layernorm(s, v, gamma_s, beta_s, gamma_v):
            mu = jnp.mean(s, axis=-1, keepdims=True)
            var = jnp.var(s, axis=-1, keepdims=True)
            s_n = (s - mu) * jax.lax.rsqrt(var + EPS) * gamma_s + beta_s
            rms = jnp.sqrt(jnp.mean(jnp.sum(v * v, axis=-1), axis=-1, keepdims=True) + EPS)
            v_n = v / rms[..., None] * gamma_v[None, :, None]
            return (s_n, v_n)
        n = node.shape[0]
        e = rsh.shape[0]
        s = node[:, :CS]
        v = node[:, CS:].reshape(n, CV, 3)
        s_n, v_n = _equiv_layernorm(s, v, gamma_s, beta_s, gamma_v)
        src, dst = (edge_index[0], edge_index[1])
        msg_s = (s_n @ Ws_src)[src] + (s_n @ Ws_dst)[dst]
        msg_v = jnp.einsum('ncx,cd->ndx', v_n, Wv_src)[src] + jnp.einsum('ncx,cd->ndx', v_n, Wv_dst)[dst]
        y0, y1 = (rsh[:, 0], rsh[:, 1:4])
        w1 = rbf @ W_rbf
        m1_s, m1_v = _cg_tp(msg_s, msg_v, y0, y1, w1[:, :CS], w1[:, CS:2 * CS], w1[:, 2 * CS:2 * CS + CV], w1[:, 2 * CS + CV:2 * CS + 2 * CV], w1[:, 2 * CS + 2 * CV:])
        a = (m1_s @ W_alpha).reshape(e, H, AS_)
        a = jnp.where(a > 0, a, 0.2 * a)
        a = jnp.sum(a * alpha_dot, axis=-1, keepdims=True)
        amax = jax.ops.segment_max(a, dst, num_segments=n)
        amax = jnp.where(jnp.isfinite(amax), amax, 0.0)
        ex = jnp.exp(a - amax[dst])
        den = jax.ops.segment_sum(ex, dst, num_segments=n)
        alpha = ex / (den[dst] + 1e-16)
        val_s = m1_s @ Ws_val
        val_v = jnp.einsum('ecx,cd->edx', m1_v, Wv_val)
        val_v = val_v * jax.nn.sigmoid(val_s @ Wg)[..., None]
        val_s = jax.nn.sigmoid(val_s)
        m2_s, m2_v = _cg_tp(val_s, val_v, y0, y1, w2_ss, w2_sv, w2_vs, w2_vv0, w2_vv1)
        hs = (m2_s @ Ws_vlin).reshape(e, H, AS_)
        hv = jnp.einsum('ecx,cd->edx', m2_v, Wv_vlin).reshape(e, H, AV, 3)
        h = jnp.concatenate([hs, hv.reshape(e, H, AV * 3)], axis=-1)
        agg = jax.ops.segment_sum(alpha * h, dst, num_segments=n)
        agg_s = agg[:, :, :AS_].reshape(n, H * AS_)
        agg_v = agg[:, :, AS_:].reshape(n, H * AV, 3)
        out = node + jnp.concatenate([agg_s @ Wps, jnp.einsum('ncx,cd->ndx', agg_v, Wpv).reshape(n, CV * 3)], axis=-1)
        return out

    def _L1_gnn_ref(node_features, edge_index, edge_attr_tensor, node_attr_scalar_raw, wm000, wm011, wm101, wm110, lm0, lm1, wu000, wu011, wu101, wu110, lu0, lu1):
        import jax, jax.numpy as jnp
        import numpy as np
        MUL0, MUL1 = (64, 32)
        INV_SQRT3 = 1.0 / np.sqrt(3.0)

        def _split(x):
            return (x[:, :MUL0], x[:, MUL0:].reshape(x.shape[0], MUL1, 3))

        def _merge(o0, o1):
            return jnp.concatenate([o0, o1.reshape(o1.shape[0], -1)], axis=-1)

        def _tp(x0, x1, y0, y1, w000, w011, w101, w110):
            fan0 = x0.shape[1] * y0.shape[1] + x1.shape[1] * y1.shape[1]
            fan1 = x0.shape[1] * y1.shape[1] + x1.shape[1] * y0.shape[1]
            out0 = (jnp.einsum('eu,ev,uvw->ew', x0, y0, w000) + INV_SQRT3 * jnp.einsum('euk,evk,uvw->ew', x1, y1, w110)) / np.sqrt(fan0)
            out1 = (jnp.einsum('eu,evk,uvw->ewk', x0, y1, w011) + jnp.einsum('euk,ev,uvw->ewk', x1, y0, w101)) / np.sqrt(fan1)
            return (out0, out1)

        def _lin(x0, x1, w0, w1):
            return (x0 @ w0 / np.sqrt(x0.shape[1]), jnp.einsum('euk,uv->evk', x1, w1) / np.sqrt(x1.shape[1]))
        N = node_features.shape[0]
        row, col = (edge_index[0], edge_index[1])
        r_vec = edge_attr_tensor[:, :3]
        dist = edge_attr_tensor[:, 3:4]
        e0 = dist
        e1 = r_vec[:, None, :]
        xj0, xj1 = _split(node_features[col])
        m0, m1 = _tp(xj0, xj1, e0, e1, wm000, wm011, wm101, wm110)
        d0, d1 = _lin(xj0, xj1, lm0, lm1)
        msgs = _merge(m0 + d0, m1 + d1)
        agg = jax.ops.segment_sum(msgs, row, num_segments=N)
        a0, a1 = _split(agg)
        x0, x1 = _split(node_features)
        u0, u1 = _tp(x0, x1, a0, a1, wu000, wu011, wu101, wu110)
        ud0, ud1 = _lin(x0, x1, lu0, lu1)
        return node_features + _merge(u0 + ud0, u1 + ud1)
    edge_index = jnp.stack([src, dst])
    h = jnp.maximum(_layernorm(x, axis=-1), 0.0)
    x = x + _L0_gnn_ref(h, edge_attr_16, edge_attr_4, L0_gnn_gamma_s, L0_gnn_beta_s, L0_gnn_gamma_v, L0_gnn_Ws_src, L0_gnn_Wv_src, L0_gnn_Ws_dst, L0_gnn_Wv_dst, L0_gnn_W_rbf, L0_gnn_W_alpha, L0_gnn_alpha_dot, L0_gnn_Ws_val, L0_gnn_Wv_val, L0_gnn_Wg, L0_gnn_w2_ss, L0_gnn_w2_sv, L0_gnn_w2_vs, L0_gnn_w2_vv0, L0_gnn_w2_vv1, L0_gnn_Ws_vlin, L0_gnn_Wv_vlin, L0_gnn_Wps, L0_gnn_Wpv, edge_index)
    h = jnp.maximum(_layernorm(x, axis=-1), 0.0)
    x = x + _L1_gnn_ref(h, edge_index, edge_attr_4, node_vec1, L1_gnn_wm000, L1_gnn_wm011, L1_gnn_wm101, L1_gnn_wm110, L1_gnn_lm0, L1_gnn_lm1, L1_gnn_wu000, L1_gnn_wu011, L1_gnn_wu101, L1_gnn_wu110, L1_gnn_lu0, L1_gnn_lu1)
    return x

_drawn_inputs = setup_inputs


def setup_inputs(seed=0):
    import zlib

    import numpy as np

    out = dict(_drawn_inputs(seed))
    spreads = {'L0_gnn_gamma_s': (1.0, 0.2), 'L0_gnn_beta_s': (0.0, 0.638), 'L0_gnn_gamma_v': (1.0, 0.6)}
    factors = {'L0_gnn_w2_vv1': 3.222}
    for name, (base, spread) in spreads.items():
        noise = np.random.default_rng([zlib.crc32(name.encode()), seed]).standard_normal(out[name].shape)
        drawn = base * np.exp(spread * noise) if base else spread * noise
        out[name] = jnp.asarray(drawn.astype(out[name].dtype))
    for name, factor in factors.items():
        out[name] = (out[name] * factor).astype(out[name].dtype)
    return out
```

```python
from contextlib import ExitStack

import concourse.bass as bass
from concourse import mybir

F32 = mybir.dt.float32
I32 = mybir.dt.int32
ALU = mybir.AluOpType
ACT = mybir.ActivationFunctionType
AX = mybir.AxisListType

N, E = 3125, 53125
CS, CV = 64, 32
D = CS + 3 * CV
H = 4
NB = 16
P = 125
NT = N // P
ET = E // P
T = 4
G = -(-ET // T)
LEFT = ET - T * (G - 1)
W = T * P
ROWS = 26 * P
HS, HV = CS // H, 3 * CV // H
AC = D + 2 * H
PW = 544
LOW = -1.0e30
EPS = 1e-5
S2, S3 = 2.0 ** -0.5, 3.0 ** -0.5
R96 = 96.0 ** -0.5
K0, K1 = (CS * CS + CV * CV) ** -0.5, (2 * CS * CV) ** -0.5

O_IN, F_IN, L_IN, NEXT_D_IN = 0, (1, 2, 3, 4), (5, 6, 7, 8, 9), 10

V0, V1, SC, V2 = 0, 32, 64, 128


class Event:

    def __init__(self, sem, per):
        self.sem, self.per = sem, per

    def value(self, g, k=None):
        return g.number(self.per, self.per if k is None else k + 1)


class Pair:

    def __init__(self, sems, per):
        self.sems, self.per = sems, per


class Group:

    def __init__(self, i, off, stride=2):
        self.i, self.off, self.stride = i, off, stride
        self.b = off % 2

    def back(self, n):
        return Group(self.i, self.off - n, self.stride)

    def ahead(self, n):
        return self.back(-n)

    def number(self, per, plus=0):
        return self.i * (self.stride * per) + (self.off * per + plus)

    def pair(self, per):
        return self.i * per + (self.off // 2 + 1) * per

    def exists(self):
        return not (isinstance(self.i, int) and not 0 <= self.off < G)


def ring(g, use):
    return (g.b + use) % 2


def wait(eng, event, g, k=None):
    if not g.exists():
        return
    if isinstance(event, Pair):
        eng.wait_ge(event.sems[g.b], g.pair(event.per))
    else:
        eng.wait_ge(event.sem, event.value(g, k))


class Count:

    def __init__(self, sem, step=1):
        self.sem, self.step, self.n = sem, step, 0

    def __call__(self, ins):
        self.n += self.step
        ins.then_inc(self.sem, self.step)
        return self.n

    def wait(self, eng, n=None):
        eng.wait_ge(self.sem, self.n if n is None else n)


def build(nc, x, src, dst, edge16, edge4, w, out):
    ctx = ExitStack()
    with ctx:
        def sb(name, shape, dt=F32):
            return ctx.enter_context(nc.sbuf_tensor(name, shape, dt))

        def sem(name):
            return ctx.enter_context(nc.semaphore(name))

        def event(name, per=1):
            return Event(sem(name), per)

        def pair(name, per):
            return Pair([sem(f"{name}_even"), sem(f"{name}_odd")], per)

        def dram(name, shape, dt=F32):
            return nc.dram_tensor(name, shape, dt, kind="Internal").ap()

        src_rows = dram("src_rows", (N, D))
        dst_rows = dram("dst_rows", (ROWS, D))
        sums = [dram(f"sums{k}", (ROWS, AC)) for k in range(T)]
        proj_rows = dram("proj_rows", (N, PW))
        aggs = [dram(f"aggs{k}", (ROWS, D)) for k in range(T)]

        ps = ctx.enter_context(nc.psum_tensor("ps", [128, 8, 512], F32))

        xs = sb("xs", [P, NT, D])
        hs = sb("hs", [P, NT, D])
        ident = sb("ident", [128, 128])
        before = sb("before", [P, P])
        pcol = sb("pcol", [P, 1])
        pcol_i = sb("pcol_i", [P, 1], I32)
        room = sb("room", [128, 42000])
        cut = {"at": 0}

        def part(width, dt=F32):
            a = cut["at"]
            cut["at"] = a + width
            assert cut["at"] <= 42000, cut["at"]
            v = room[:, a:a + width]
            return v if dt == F32 else v.bitcast(dt)

        stage = part(NT * 2 * D)[0:P].rearrange("p (j c) -> p j c", j=NT)
        nn = part(NT * D)[0:P].rearrange("p (j c) -> p j c", j=NT)
        tmp = part(NT * D)[0:P].rearrange("p (j c) -> p j c", j=NT)
        stat = part(8 * NT)[0:P].rearrange("p (k j) -> p k j", k=8)
        nA = [part(128) for _ in range(2)]
        nB = [part(128) for _ in range(2)]
        gam = part(CS + CV + CS)
        wA = part(2 * D)
        wB = part(2 * D)
        init_row = part(26 * AC)[0:P].rearrange("p (j c) -> p j c", j=26)
        node_end = cut["at"]

        cut["at"] = 0
        e_src = [part(T, I32)[0:P] for _ in range(2)]
        e_dst = [part(T, I32)[0:P] for _ in range(2)]
        e_rbf = [part(T * NB)[0:P] for _ in range(2)]
        e_y = [part(T * 4)[0:P] for _ in range(2)]
        pad_dst = part(T, I32)[0:P]
        g_src = [part(T * D)[0:P] for _ in range(2)]
        g_dst = [part(T * D)[0:P] for _ in range(2)]
        outer = [part(T * 128)[0:P].rearrange("p (t c) -> p t c", t=T) for _ in range(2)]
        y_kept = [part(T * 4)[0:P] for _ in range(2)]
        dst_kept = [part(T, I32)[0:P] for _ in range(2)]
        dst_f = part(T)[0:P]
        feat = part(T * 256)[0:P].rearrange("p (t c) -> p t c", t=T)
        oT = part(W)
        fT = [part(W) for _ in range(4)]
        prod = [part(W) for _ in range(5)]
        xv = part(W)
        rl = part(W)
        sg = part(W)
        tg = part(W)[0:96]
        gv = part(W)[0:96]
        logit = part(T * H)[0:P].rearrange("p (t h) -> p t h", t=T)
        same = [part(W)[0:P].rearrange("p (t e) -> p t e", t=T) for _ in range(2)]
        apart = [part(W)[0:P].rearrange("p (t e) -> p t e", t=T) for _ in range(2)]
        early = part(W)[0:P].rearrange("p (t e) -> p t e", t=T)
        masked = [part(W)[0:P].rearrange("p (t e) -> p t e", t=T) for _ in range(2)]
        cnt = part(T)[0:P]
        away = part(T)[0:P]
        moved = part(T)[0:P]
        first = [part(T, I32)[0:P] for _ in range(2)]
        rows = [part(T * AC)[0:P].rearrange("p (t c) -> p t c", t=T) for _ in range(2)]
        gmax = part(T * H)[0:P].rearrange("p (t h) -> p t h", t=T)
        newmax = part(T * H)[0:P].rearrange("p (t h) -> p t h", t=T)
        shift = part(2 * T * H)[0:P].rearrange("p (k t h) -> p k t h", k=2, t=T)
        scale = part(2 * T * H)[0:P].rearrange("p (k t h) -> p k t h", k=2, t=T)
        ht = part(T * D)[0:P].rearrange("p (t c) -> p t c", t=T)
        vx = part(T * (D + H))[0:P].rearrange("p (t c) -> p t c", t=T)
        edge_end = cut["at"]
        cut["at"] = w_at = max(node_end, edge_end)
        wl_all = part(5 * 128)
        wL = [wl_all[:, k * 128:(k + 1) * 128] for k in range(5)]
        wX0, wX4 = part(128), part(128)
        wV = [part(32) for _ in range(3)]
        wV4 = part(96)
        wG = part(96)
        wLr = part(H)
        wUg, wUs = part(4 * D), part(4 * D)
        w2col = part(8)
        l0_end = cut["at"]


        inputs_loaded = sem("inputs_loaded")
        cleared = sem("cleared")
        weights_loaded = Count(sem("weights_loaded"), 16)
        dve_step, act_step, pool_step = sem("dve_step"), sem("act_step"), sem("pool_step")
        weights_scaled = sem("weights_scaled")
        var_ready, std_ready = sem("var_ready"), sem("std_ready")
        consts_made = sem("consts_made")
        nn_ready = sem("nn_ready")
        nodes_turned, turned_kept = sem("nodes_turned"), sem("turned_kept")
        projected, projection_kept = sem("projected"), sem("projection_kept")
        tables_stored = sem("tables_stored")
        edge_places_cleared = sem("edge_places_cleared")
        pad_copied = sem("pad_copied")
        settled = [sem("pool_settled"), sem("sync_settled")]

        edges_loaded = pair("edges_loaded", 64)
        nodes_gathered = pair("nodes_gathered", 2 * T * 16)
        rows_gathered = pair("rows_gathered", T * 16)
        rows_scattered = pair("rows_scattered", T * 16)
        outer_built = event("outer_built", 4)
        copies_made = event("copies_made", 3)
        feat_added, feat_dup = event("feat_added"), event("feat_dup", 2)
        outer_turned, outer_kept = event("outer_turned"), event("outer_kept")
        f_turned, f_kept = event("f_turned", 4), event("f_kept", 4)
        l_made, prod_made = event("l_made", 5), event("prod_made", 5)
        x_made, v_made, xv_kept = event("x_made"), event("v_made"), event("xv_kept", 3)
        g_made, tg_made, sg_made = event("g_made"), event("tg_made"), event("sg_made", 2)
        gv_made = event("gv_made")
        lg_made, lg_kept = event("lg_made"), event("lg_kept")
        d_made, same_made, masks_made = event("d_made"), event("same_made"), event("masks_made", 2)
        early_counted = event("early_counted")
        firsts_made = event("firsts_made", 4)
        a_made, a_masked, a_max = event("a_made", 4), event("a_masked", 4), event("a_max", 4)
        shift_made, exp_made = event("shift_made", 3), event("exp_made")
        u_made, t0_made, comb = event("u_made", 2 * T), event("t0_made", T), event("comb", 3 * T)
        vx_made, sm_made = event("vx_made", 3), event("sm_made", 2)
        rows_scaled, rows_added = event("rows_scaled", 3), event("rows_added", 3)

        def settle(eng, k):
            eng.sem_inc(settled[k], 1)

        def fold(ap):
            return ap.rearrange("(p t) c -> p (t c)", p=P)

        src_v, dst_v = src.rearrange("(p t) -> p t", p=P), dst.rearrange("(p t) -> p t", p=P)
        rbf_v, y_v = fold(edge16), fold(edge4)

        def norm(dve, dv, raw, res, c, root, relu, stat, tmp, var_ready, std_ready):
            bc = lambda k: stat[:, k, :].unsqueeze(2).broadcast_to([P, NT, c])
            dv(nc.vector.tensor_reduce(stat[:, 0, :], raw, AX.X, ALU.add))
            dv.wait(dve)
            dv(nc.vector.tensor_scalar(stat[:, 1, :], stat[:, 0, :], 1.0 / c, None, ALU.mult))
            dv.wait(dve)
            dv(nc.vector.tensor_tensor(res, raw, bc(1), ALU.subtract))
            dv.wait(dve)
            dv(nc.vector.tensor_tensor(tmp[:, :, 0:c], res, res, ALU.mult))
            dv.wait(dve)
            dv(nc.vector.tensor_reduce(stat[:, 2, :], tmp[:, :, 0:c], AX.X, ALU.add))
            dv.wait(dve)
            nc.vector.tensor_scalar(stat[:, 3, :], stat[:, 2, :], 1.0 / c, EPS, ALU.mult, ALU.add).then_inc(var_ready, 1)
            dve.wait_ge(std_ready, root)
            dv(nc.vector.reciprocal(stat[:, 5, :], stat[:, 4, :]))
            dv.wait(dve)
            dv(nc.vector.tensor_tensor(res, res, bc(5), ALU.mult))
            dv.wait(dve)
            if relu:
                dv(nc.vector.tensor_scalar(res, res, 0.0, None, ALU.max))
                dv.wait(dve)

        def root_of(act, root):
            act.wait_ge(var_ready, root)
            nc.scalar.activation(stat[:, 4, :], stat[:, 3, :], ACT.Sqrt).then_inc(std_ready, 1)

        def to_rows(dst_ap, vecs):
            v = vecs.rearrange("p j (c k) -> p j c k", k=3)
            return [(dst_ap[:, :, at:at + CV], v[:, :, :, k]) for k, at in enumerate((V0, V1, V2))]

        with nc.Block() as block:
            @block.sync
            def _(sp):
                sp.dma_start(xs[:, :, :], x.rearrange("(p j) c -> p j c", p=P)).then_inc(inputs_loaded, 16)
                sp.dma_start(gam[0:P, 0:CS], w["gamma_s"].partition_broadcast(P)).then_inc(inputs_loaded, 16)
                sp.dma_start(gam[0:P, CS:2 * CS], w["beta_s"].partition_broadcast(P)).then_inc(inputs_loaded, 16)
                sp.dma_start(gam[0:P, 2 * CS:2 * CS + CV], w["gamma_v"].partition_broadcast(P)).then_inc(inputs_loaded, 16)
                sp.wait_ge(cleared, 3)
                ld = lambda a, b: weights_loaded(sp.dma_start(a, b, allow_slow_non_contiguous=True))
                for k, (ws, wv) in enumerate(((w["Ws_src"], w["Wv_src"]), (w["Ws_dst"], w["Wv_dst"]))):
                    ld(wA[V0:V0 + 32, k * D + V0:k * D + V0 + 32], wv)
                    ld(wA[V1:V1 + 32, k * D + V1:k * D + V1 + 32], wv)
                    ld(wA[SC:SC + 64, k * D + SC:k * D + SC + 64], ws)
                    ld(wB[0:32, k * D + V2:k * D + V2 + 32], wv)
                Wr = w["W_rbf"]
                r_ss, r_sv = Wr[:, 0:64], Wr[:, 64:128]
                r_vs, r_vv0, r_vv1 = Wr[:, 128:160], Wr[:, 160:192], Wr[:, 192:224]
                lw = [[(0, 1, r_vv0), (32, 2, r_vv0), (64, 0, r_ss)],
                      [(0, 0, r_vs), (32, 3, r_vv1), (64, 1, r_sv)],
                      [(0, 0, r_vs), (32, 2, r_sv), (96, 1, r_vv1)],
                      [(0, 3, r_sv), (64, 0, r_vs), (96, 2, r_vv1)],
                      [(0, 2, r_vv1), (32, 3, r_vv1), (64, 1, r_vv1), (96, 3, r_vv0)]]
                for k in range(5):
                    for col, c, b in lw[k]:
                        ld(wL[k][16 * c:16 * c + 16, col:col + b.shape[1]], b)
                for col, m in ((0, w["W_alpha"]), (64, w["Ws_val"])):
                    ld(wX0[0:32, col:col + 64], m[64:96, :])
                    ld(wX0[32:64, col:col + 64], m[64:96, :])
                    ld(wX0[64:128, col:col + 64], m[0:64, :])
                    ld(wX4[96:128, col:col + 64], m[64:96, :])
                Wv = w["Wv_val"]
                for k, (s_at, vs_at, c_at) in enumerate(((64, 0, 32), (32, 0, 96), (0, 64, 96))):
                    ld(wV[k][s_at:s_at + 64, :], Wv[0:64, :])
                    ld(wV[k][vs_at:vs_at + 32, :], Wv[64:96, :])
                    ld(wV[k][c_at:c_at + 32, :], Wv[96:128, :])
                for k in range(3):
                    ld(wV4[32 * k:32 * k + 32, 32 * k:32 * k + 32], Wv[96:128, :])
                    ld(wG[64:128, 32 * k:32 * k + 32], w["Wg"])
                for h in range(H):
                    a = w["alpha_dot"][0, h, :].rearrange("(a o) -> a o", o=1)
                    ld(wLr[HS * h:HS * h + HS, h:h + 1], a)
                    ld(wLr[64 + HS * h:64 + HS * h + HS, h:h + 1], a)
                Wh, Wl = w["Wv_vlin"], w["Ws_vlin"]

                def hv_cols(t, r, c, j, m):
                    for h in range(H):
                        at = c * D + CS + h * HV + j * 8
                        ld(t[r:r + m.shape[0], at:at + 8], m[:, 8 * h:8 * h + 8])

                for j in range(3):
                    a, b = (j + 1) % 3, (j + 2) % 3
                    hv_cols(wUg, 32 * j, 0, j, Wh[64:96, :])
                    ld(wUg[32 * j:32 * j + 32, (1 + j) * D:(1 + j) * D + CS], Wl[64:96, :])
                    hv_cols(wUg, 32 * b, 1 + j, a, Wh[96:128, :])
                    hv_cols(wUg, 32 * a, 1 + j, b, Wh[96:128, :])
                    hv_cols(wUs, 64, 1 + j, j, Wh[0:64, :])
                    for k, name in enumerate(("w2_vs", "w2_vv0", "w2_vv1")):
                        ld(w2col[32 * j:32 * j + 32, k:k + 1], w[name].rearrange("(a o) -> a o", o=1))
                ld(wUs[64:128, 0:CS], Wl[0:64, :])
                for k, name in enumerate(("w2_ss", "w2_sv")):
                    ld(w2col[64:128, 3 + k:4 + k], w[name].rearrange("(a o) -> a o", o=1))
                sp.wait_ge(consts_made, 5)
                for k in range(T):
                    sp.dma_start(sums[k].rearrange("(p j) c -> p j c", p=P), init_row).then_inc(tables_stored, 16)
                sp.dma_start(dst_rows[N:ROWS, :], init_row[:, 0, 0:D]).then_inc(tables_stored, 16)
                sp.wait_ge(projection_kept, NT)
                sp.dma_start(src_rows.rearrange("(p j) c -> p j c", p=P), stage[:, :, 0:D]).then_inc(tables_stored, 16)
                sp.dma_start(dst_rows[0:N, :].rearrange("(p j) c -> p j c", p=P), stage[:, :, D:2 * D]).then_inc(tables_stored, 16)
                sp.wait_ge(tables_stored, 16 * (T + 3))
                sp.wait_ge(weights_loaded.sem, weights_loaded.n)

            @block.gpsimd
            def _(pool):
                nc.gpsimd.memset(room[:, w_at:l0_end], 0.0).then_inc(cleared, 1)
                nc.gpsimd.memset(wA, 0.0).then_inc(cleared, 1)
                nc.gpsimd.memset(wB, 0.0).then_inc(cleared, 1)
                nc.gpsimd.memset(ident[:, :], 0.0).then_inc(pool_step, 1)
                nc.gpsimd.memset(before[:, :], 1.0).then_inc(pool_step, 1)
                nc.gpsimd.memset(init_row[:, :, 0:D + H], 0.0).then_inc(consts_made, 1)
                nc.gpsimd.memset(init_row[:, :, D + H:AC], LOW).then_inc(consts_made, 1)
                nc.gpsimd.iota(pcol_i[:, :], pattern=[[0, 1]], base=N, channel_multiplier=1).then_inc(pool_step, 1)
                pool.wait_ge(pool_step, 3)
                nc.gpsimd.tensor_copy(pcol[:, :], pcol_i[:, :]).then_inc(consts_made, 1)
                nc.gpsimd.affine_select(out=ident[:, :], in_=ident[:, :], compare_op=ALU.not_equal, fill=1.0,
                                        base=0, pattern=[[-1, 128]], channel_multiplier=1).then_inc(consts_made, 1)
                nc.gpsimd.affine_select(out=before[:, :], in_=before[:, :], compare_op=ALU.is_gt, fill=0.0,
                                        base=0, pattern=[[-1, P]], channel_multiplier=1).then_inc(consts_made, 1)

            @block.vector
            def _(dve):
                dv = Count(dve_step)
                dve.wait_ge(inputs_loaded, 64)
                norm(dve, dv, xs[:, :, :], hs[:, :, :], D, 1, True, stat, tmp, var_ready, std_ready)
                sn = stage[:, :, 0:CS]
                norm(dve, dv, hs[:, :, 0:CS], sn, CS, 2, False, stat, tmp, var_ready, std_ready)
                row = lambda a, b: gam[0:P, a:b].unsqueeze(1).broadcast_to([P, NT, b - a])
                dv(nc.vector.tensor_tensor(sn, sn, row(0, CS), ALU.mult))
                dv.wait(dve)
                nc.vector.tensor_tensor(nn[:, :, SC:SC + CS], sn, row(CS, 2 * CS), ALU.add).then_inc(nn_ready, 1)
                vec = hs[:, :, CS:D]
                dv(nc.vector.tensor_tensor(tmp[:, :, 0:3 * CV], vec, vec, ALU.mult))
                dv.wait(dve)
                dv(nc.vector.tensor_reduce(stat[:, 2, :], tmp[:, :, 0:3 * CV], AX.X, ALU.add))
                dv.wait(dve)
                nc.vector.tensor_scalar(stat[:, 3, :], stat[:, 2, :], 1.0 / CV, EPS, ALU.mult, ALU.add).then_inc(var_ready, 1)
                dve.wait_ge(std_ready, 3)
                dv(nc.vector.reciprocal(stat[:, 5, :], stat[:, 4, :]))
                dv.wait(dve)
                dv(nc.vector.tensor_tensor(tmp[:, :, 0:3 * CV], vec,
                                           stat[:, 5, :].unsqueeze(2).broadcast_to([P, NT, 3 * CV]), ALU.mult))
                dv.wait(dve)
                for o, i in to_rows(nn, tmp[:, :, 0:3 * CV]):
                    nc.vector.tensor_tensor(o, i, row(2 * CS, 2 * CS + CV), ALU.mult).then_inc(nn_ready, 1)
                dve.wait_ge(weights_loaded.sem, weights_loaded.n)
                sc = []
                mul = lambda ap, f, g=None: sc.append(
                    nc.vector.tensor_scalar(ap, ap, f, g, ALU.mult, ALU.mult) if g is not None
                    else nc.vector.tensor_scalar(ap, ap, f, None, ALU.mult))
                mul(wX0[0:64, :], S3)
                mul(wX4[96:128, :], S3)
                for k, c_at in enumerate((32, 96, 96)):
                    mul(wV[k][c_at:c_at + 32, :], S2)
                mul(wV4[0:96, :], -S2)
                mul(wLr[0:64, :], 0.2)
                mul(wLr[64:128, :], 0.8)
                mul(wUs[64:128, 0:CS], w2col[64:128, 3:4], 0.5)
                mul(wUs[64:128, D:4 * D], w2col[64:128, 4:5], 0.5)
                mul(wUg[0:96, 0:D], w2col[0:96, 0:1], 0.5)
                for j in range(3):
                    a, b, at = (j + 1) % 3, (j + 2) % 3, (1 + j) * D
                    mul(wUg[32 * j:32 * j + 32, at:at + CS], w2col[32 * j:32 * j + 32, 1:2], 0.5 * S3)
                    mul(wUg[32 * b:32 * b + 32, at + CS:at + D], w2col[32 * b:32 * b + 32, 2:3], 0.5 * S2)
                    mul(wUg[32 * a:32 * a + 32, at + CS:at + D], w2col[32 * a:32 * a + 32, 2:3], -0.5 * S2)
                for ins in sc:
                    ins.then_inc(weights_scaled, 1)
                dve.wait_ge(weights_scaled, len(sc))

            @block.scalar
            def _(act):
                for r in (1, 2, 3):
                    root_of(act, r)
                act.wait_ge(weights_loaded.sem, weights_loaded.n)
                for j in range(NT):
                    b = j % 2
                    act.wait_ge(nodes_turned, 2 * j + 2)
                    if j >= 2:
                        act.wait_ge(projected, j - 1)
                    nc.scalar.activation(nA[b][:, 0:P], ps[:, b, 0:P], ACT.Copy).then_inc(turned_kept, 1)
                    nc.scalar.activation(nB[b][0:32, 0:P], ps[0:32, b, 128:128 + P], ACT.Copy).then_inc(turned_kept, 1)
                    act.wait_ge(projected, j + 1)
                    nc.scalar.activation(stage[:, j, :], ps[0:P, 2 + b, 0:2 * D], ACT.Copy).then_inc(projection_kept, 1)

            @block.tensor
            def _(pe):
                pe.wait_ge(consts_made, 5)
                pe.wait_ge(nn_ready, 4)
                pe.wait_ge(weights_loaded.sem, weights_loaded.n)
                for j in range(NT):
                    b = j % 2
                    if j >= 2:
                        pe.wait_ge(turned_kept, 2 * (j - 1))
                    nc.tensor.transpose(ps[:, b, 0:P], nn[:, j, 0:128], ident[0:P, 0:P]).then_inc(nodes_turned, 1)
                    nc.tensor.transpose(ps[0:32, b, 128:128 + P], nn[:, j, 128:D], ident[0:P, 0:P]).then_inc(nodes_turned, 1)
                    pe.wait_ge(turned_kept, 2 * j + 2)
                    if j >= 2:
                        pe.wait_ge(projection_kept, j - 1)
                    nc.tensor.matmul(ps[0:P, 2 + b, 0:2 * D], nA[b][:, 0:P], wA, start=True, stop=False)
                    nc.tensor.matmul(ps[0:P, 2 + b, 0:2 * D], nB[b][0:32, 0:P], wB[0:32, :],
                                     start=False, stop=True).then_inc(projected, 1)

        def steps(eng, body):
            for j in range(3):
                body(Group(0, j))
            with eng.Fori(0, (G - 5) // 2) as i:
                for u in range(2):
                    body(Group(i, u + 3))
            for j in range(G - 2, G + 1):
                body(Group(0, j))

        def halves(j):
            return j.exists(), j.back(1).exists()

        with nc.Block() as block:
            @block.sync
            def _(sp):
                def load_edges(g):
                    b, eds = g.b, edges_loaded.sems[g.b]
                    wait(sp, outer_built, g.back(2))
                    settle(sp, 1)
                    wait(sp, copies_made, g.back(2))
                    wait(sp, nodes_gathered, g.back(2))
                    settle(sp, 1)
                    last = isinstance(g.i, int) and g.off == G - 1
                    n = LEFT if last else T
                    if last:
                        sp.dma_start(e_dst[b][:, n:T], pad_dst[:, n:T]).then_inc(pad_copied, 16)
                        sp.wait_ge(pad_copied, 16)
                    sp.dma_start(e_src[b][:, 0:n], src_v[:, bass.ds(g.number(T), n)], allow_slow_non_contiguous=True).then_inc(eds, 16)
                    sp.dma_start(e_dst[b][:, 0:n], dst_v[:, bass.ds(g.number(T), n)], allow_slow_non_contiguous=True).then_inc(eds, 16)
                    sp.dma_start(e_rbf[b][:, 0:n * NB], rbf_v[:, bass.ds(g.number(T * NB), n * NB)]).then_inc(eds, 16)
                    sp.dma_start(e_y[b][:, 0:n * 4], y_v[:, bass.ds(g.number(T * 4), n * 4)]).then_inc(eds, 16)

                sp.wait_ge(edge_places_cleared, 4)
                for g in range(4):
                    load_edges(Group(0, g))
                with sp.Fori(0, (G - 5) // 2) as i:
                    for u in range(2):
                        load_edges(Group(i, u + 4))
                load_edges(Group(0, G - 1))

            @block.gpsimd
            def _(pool):
                nc.gpsimd.memset(outer[0], 0.0).then_inc(edge_places_cleared, 1)
                nc.gpsimd.memset(outer[1], 0.0).then_inc(edge_places_cleared, 1)
                nc.gpsimd.memset(sg, 0.0).then_inc(edge_places_cleared, 1)
                nc.gpsimd.memset(pad_dst, N).then_inc(edge_places_cleared, 1)
                pool.wait_ge(edge_places_cleared, 4)

                def gather(g):
                    b = g.b
                    wait(pool, edges_loaded, g)
                    wait(pool, feat_added, g.back(2))
                    settle(pool, 0)
                    for t in range(T):
                        nc.gpsimd.indirect_dma_start(g_src[b][:, t * D:(t + 1) * D], None, src_rows,
                                                     bass.IndirectOffsetOnAxis(ap=e_src[b][:, t:t + 1], axis=0)
                                                     ).then_inc(nodes_gathered.sems[b], 16)
                        nc.gpsimd.indirect_dma_start(g_dst[b][:, t * D:(t + 1) * D], None, dst_rows,
                                                     bass.IndirectOffsetOnAxis(ap=e_dst[b][:, t:t + 1], axis=0)
                                                     ).then_inc(nodes_gathered.sems[b], 16)
                    wait(pool, outer_turned, g.back(2))
                    y = e_y[b].rearrange("p (t c) -> p t c", c=4)
                    for c in range(4):
                        nc.gpsimd.tensor_tensor(outer[b][:, :, NB * c:NB * c + NB],
                                                e_rbf[b].rearrange("p (t r) -> p t r", r=NB),
                                                y[:, :, c:c + 1].broadcast_to([P, T, NB]),
                                                ALU.mult).then_inc(outer_built.sem, 1)

                def read_tables(g):
                    wait(pool, copies_made, g)
                    wait(pool, rows_scattered, g.back(1))
                    settle(pool, 0)
                    for t in range(T):
                        nc.gpsimd.indirect_dma_start(rows[g.b][:, t, :], None, sums[t],
                                                     bass.IndirectOffsetOnAxis(ap=dst_kept[g.b][:, t:t + 1], axis=0)
                                                     ).then_inc(rows_gathered.sems[g.b], 16)

                def write_tables(g):
                    b, rw = g.b, rows[g.b]
                    wait(pool, rows_gathered, g)
                    wait(pool, exp_made, g)
                    for a, n in ((0, HS), (CS, HV), (D, 1)):
                        v = rw[:, :, a:a + H * n].rearrange("p t (h a) -> p t h a", h=H)
                        nc.gpsimd.tensor_tensor(v, v, scale[:, 0, :, :].unsqueeze(3).broadcast_to([P, T, H, n]),
                                                ALU.mult).then_inc(rows_scaled.sem, 1)
                    wait(pool, rows_added, g)
                    wait(pool, firsts_made, g)
                    settle(pool, 0)
                    for t in range(T):
                        nc.gpsimd.indirect_dma_start(sums[t], bass.IndirectOffsetOnAxis(ap=first[b][:, t:t + 1], axis=0),
                                                     rw[:, t, :], None, bounds_check=N - 1, oob_is_err=False
                                                     ).then_inc(rows_scattered.sems[b], 16)

                def body(m):
                    read_tables(m)
                    if m.ahead(3).exists():
                        gather(m.ahead(3))
                    write_tables(m)

                for g in range(3):
                    gather(Group(0, g))
                body(Group(0, 0))
                with pool.Fori(0, (G - 5) // 2) as i:
                    for u in range(2):
                        body(Group(i, u + 1))
                for g in range(G - 4, G):
                    body(Group(0, g))
                wait(pool, rows_scattered, Group(0, G - 2))
                wait(pool, rows_scattered, Group(0, G - 1))

            @block.vector
            def _(dve):
                def take(j):
                    b = j.b
                    wait(dve, edges_loaded, j)
                    wait(dve, rows_gathered, j.back(2))
                    wait(dve, d_made, j.back(1))
                    wait(dve, firsts_made, j.back(1))
                    nc.vector.tensor_copy(dst_f, e_dst[b]).then_inc(copies_made.sem, 1)
                    nc.vector.tensor_copy(dst_kept[b], e_dst[b]).then_inc(copies_made.sem, 1)
                    wait(dve, comb, j.back(2))
                    wait(dve, t0_made, j.back(2))
                    nc.vector.tensor_copy(y_kept[b], e_y[b]).then_inc(copies_made.sem, 1)
                    wait(dve, nodes_gathered, j)
                    wait(dve, f_turned, j.back(1))
                    nc.vector.tensor_tensor(feat[:, :, 0:D], g_src[b].rearrange("p (t c) -> p t c", t=T),
                                            g_dst[b].rearrange("p (t c) -> p t c", t=T),
                                            ALU.add).then_inc(feat_added.sem, 1)

                def masks(j):
                    b = j.b
                    wait(dve, d_made, j)
                    wait(dve, sm_made, j.back(2))
                    col = dst_f.unsqueeze(2).broadcast_to([P, T, P])
                    nc.vector.tensor_tensor(same[b], ps[0:P, ring(j.back(1), NEXT_D_IN), 0:W].rearrange("p (t e) -> p t e", t=T), col,
                                            ALU.is_equal).then_inc(same_made.sem, 1)
                    wait(dve, early_counted, j.back(1))
                    wait(dve, same_made, j)
                    nc.vector.tensor_tensor(early, same[b], before[:, :].unsqueeze(1).broadcast_to([P, T, P]),
                                            ALU.mult).then_inc(masks_made.sem, 1)
                    wait(dve, a_masked, j.back(2))
                    nc.vector.tensor_scalar(apart[b], same[b], -LOW, LOW, ALU.mult, ALU.add).then_inc(masks_made.sem, 1)
                    wait(dve, masks_made, j, 0)
                    nc.vector.tensor_reduce(cnt, early, AX.X, ALU.add).then_inc(early_counted.sem, 1)
                    nc.vector.tensor_scalar(away, dst_f, -1.0, pcol[:, 0:1], ALU.mult, ALU.add).then_inc(firsts_made.sem, 1)
                    wait(dve, early_counted, j)
                    nc.vector.tensor_scalar(cnt, cnt, 0.5, None, ALU.is_gt).then_inc(firsts_made.sem, 1)
                    wait(dve, firsts_made, j, 1)
                    nc.vector.tensor_tensor(moved, away, cnt, ALU.mult).then_inc(firsts_made.sem, 1)
                    wait(dve, firsts_made, j, 2)
                    wait(dve, rows_scattered, j.back(2))
                    nc.vector.tensor_tensor(first[b], moved, dst_f, ALU.add).then_inc(firsts_made.sem, 1)

                def only_same(g, h):
                    wait(dve, a_made, g, h)
                    wait(dve, masks_made, g)
                    if h >= 2:
                        wait(dve, a_max, g, h - 2)
                    else:
                        wait(dve, a_max, g.back(1))
                    nc.vector.tensor_tensor(masked[h % 2], ps[0:P, 6 + h % 2, 0:W].rearrange("p (t e) -> p t e", t=T),
                                            apart[g.b], ALU.add).then_inc(a_masked.sem, 1)

                def largest(g, h):
                    wait(dve, a_masked, g, h)
                    nc.vector.tensor_reduce(gmax[:, :, h], masked[h % 2], AX.X, ALU.max).then_inc(a_max.sem, 1)

                def combine(g, t, c):
                    if c != 3:
                        wait(dve, u_made, g, 2 * t + c // 2)
                    if c == 1:
                        wait(dve, t0_made, g, t)
                    else:
                        wait(dve, comb, g, 3 * t + c - 2)
                    nc.vector.scalar_tensor_tensor(
                        ht[:, t, :], ps[0:P, 4 + c // 2, (c % 2) * D:(c % 2 + 1) * D],
                        y_kept[g.b][:, 4 * t + c:4 * t + c + 1], ht[:, t, :],
                        ALU.mult, ALU.add).then_inc(comb.sem, 1)

                def product(j, k):
                    wait(dve, l_made, j, k)
                    f = (0, 0, 1, 2, 3)[k]
                    wait(dve, f_kept, j, f)
                    nc.vector.tensor_tensor(prod[k], ps[:, ring(j, L_IN[k]), 0:W], fT[f], ALU.mult).then_inc(prod_made.sem, 1)

                def body(j):
                    new, old = halves(j)
                    g = j.back(1)
                    if old:
                        for f, *k in ((only_same, 0), (only_same, 1), (largest, 0), (only_same, 2), (largest, 1),
                                      (only_same, 3), (combine, 0, 1), (largest, 2), (combine, 0, 2), (largest, 3),
                                      (combine, 0, 3), (combine, 1, 1), (combine, 1, 2), (combine, 1, 3)):
                            f(g, *k)
                        wait(dve, rows_gathered, g)
                        wait(dve, a_max, g)
                        wait(dve, rows_added, g.back(1))
                        old_max = rows[g.b][:, :, D + H:AC]
                        nc.vector.tensor_tensor(newmax, gmax, old_max, ALU.max).then_inc(shift_made.sem, 1)
                        combine(g, 2, 1)
                        wait(dve, shift_made, g, 0)
                        wait(dve, exp_made, g.back(1))
                        nc.vector.tensor_tensor(shift[:, 0], old_max, newmax, ALU.subtract).then_inc(shift_made.sem, 1)
                        combine(g, 2, 2)
                        wait(dve, lg_kept, g)
                        nc.vector.tensor_tensor(shift[:, 1], logit, newmax, ALU.subtract).then_inc(shift_made.sem, 1)
                        combine(g, 2, 3)
                        for c in range(1, 4):
                            combine(g, 3, c)
                    if new:
                        wait(dve, x_made, j.back(1))
                        wait(dve, v_made, j.back(1))
                        product(j, 0)
                    if old:
                        wait(dve, comb, g)
                        wait(dve, exp_made, g)
                        wait(dve, sm_made, g.back(1))
                        ex = scale[:, 1, :, :]
                        for a, n in ((0, HS), (CS, HV)):
                            nc.vector.tensor_tensor(
                                vx[:, :, a:a + H * n].rearrange("p t (h a) -> p t h a", h=H),
                                ht[:, :, a:a + H * n].rearrange("p t (h a) -> p t h a", h=H),
                                ex.unsqueeze(3).broadcast_to([P, T, H, n]), ALU.mult).then_inc(vx_made.sem, 1)
                        nc.vector.tensor_copy(vx[:, :, D:D + H], ex).then_inc(vx_made.sem, 1)
                    if new:
                        for k in range(1, 5):
                            product(j, k)
                    if old:
                        wait(dve, rows_scaled, g)
                        for k in range(2):
                            wait(dve, sm_made, g, k)
                            r = rows[g.b][:, 2 * k:2 * k + 2, 0:D + H]
                            nc.vector.tensor_tensor(r, r, ps[0:P, 6 + k, 0:2 * (D + H)].rearrange("p (t c) -> p t c", t=2),
                                                    ALU.add).then_inc(rows_added.sem, 1)
                        wait(dve, shift_made, g)
                        nc.vector.tensor_copy(rows[g.b][:, :, D + H:AC], newmax).then_inc(rows_added.sem, 1)
                    if j.ahead(1).exists():
                        take(j.ahead(1))
                        masks(j.ahead(1))
                    if new:
                        wait(dve, tg_made, j)
                        wait(dve, v_made, j)
                        wait(dve, u_made, j.back(1))
                        nc.vector.scalar_tensor_tensor(gv[:, :], tg[:, :], 1.0, ps[0:96, 3, 0:W],
                                                       ALU.add, ALU.mult).then_inc(gv_made.sem, 1)

                take(Group(0, 0))
                masks(Group(0, 0))
                steps(dve, body)

            @block.scalar
            def _(act):
                def keep(out_, in_, ev):
                    nc.scalar.activation(out_, in_, ACT.Copy).then_inc(ev.sem, 1)

                def double(j):
                    wait(act, feat_added, j)
                    wait(act, f_turned, j.back(1))
                    keep(feat[:, :, D:D + 64], feat[:, :, V0:V0 + 64], feat_dup)
                    keep(feat[:, :, D + 64:D + 96], feat[:, :, V2:V2 + 32], feat_dup)

                act.wait_ge(edge_places_cleared, 4)

                def body(j):
                    new, old = halves(j)
                    g = j.back(1)
                    if new:
                        wait(act, outer_turned, j)
                        wait(act, l_made, j.back(1))
                        keep(oT, ps[:, ring(j, O_IN), 0:W], outer_kept)
                        for k in range(4):
                            wait(act, f_turned, j, k)
                            wait(act, prod_made, j.back(1))
                            keep(fT[k], ps[:, ring(j, F_IN[k]), 0:W], f_kept)
                    if old:
                        wait(act, vx_made, g.back(1))
                        for t in range(T):
                            wait(act, u_made, g, 2 * t)
                            nc.scalar.activation(ht[:, t, :], ps[0:P, 4, 0:D], ACT.Copy,
                                                 scale=y_kept[g.b][:, 4 * t:4 * t + 1]).then_inc(t0_made.sem, 1)
                            if t == 2:
                                wait(act, shift_made, g)
                                wait(act, rows_scaled, g.back(1))
                                nc.scalar.activation(scale, shift, ACT.Exp).then_inc(exp_made.sem, 1)
                    if new:
                        wait(act, x_made, j)
                        wait(act, lg_made, j.back(1))
                        wait(act, g_made, j.back(1))
                        wait(act, sg_made, j.back(1))
                        keep(xv[64:128, :], ps[64:128, 2, 0:W], xv_kept)
                        keep(rl[0:64, :], ps[0:64, 2, 0:W], xv_kept)
                        nc.scalar.activation(rl[64:128, :], ps[0:64, 2, 0:W], ACT.Relu).then_inc(xv_kept.sem, 1)
                        wait(act, xv_kept, j, 0)
                        wait(act, u_made, j.back(1))
                        nc.scalar.activation(sg[64:128, :], xv[64:128, :], ACT.Tanh, scale=0.5).then_inc(sg_made.sem, 1)
                        wait(act, g_made, j)
                        wait(act, gv_made, j.back(1))
                        nc.scalar.activation(tg[:, :], ps[0:96, 4, 0:W], ACT.Tanh, scale=0.5).then_inc(tg_made.sem, 1)
                        wait(act, sg_made, j, 0)
                        nc.scalar.activation(sg[64:128, :], sg[64:128, :], ACT.Copy, bias=1.0).then_inc(sg_made.sem, 1)
                    if j.ahead(1).exists():
                        double(j.ahead(1))
                    if new:
                        wait(act, lg_made, j)
                        wait(act, shift_made, j.back(1))
                        wait(act, a_made, j.back(1))
                        keep(logit, ps[0:P, 7, 0:T * H].rearrange("p (t h) -> p t h", t=T), lg_kept)

                double(Group(0, 0))
                steps(act, body)

            @block.tensor
            def _(pe):
                tr = nc.tensor.transpose
                mm = nc.tensor.matmul
                idP = ident[0:P, 0:P]

                def destinations(j):
                    wait(pe, copies_made, j)
                    wait(pe, prod_made, j.back(1), 3)
                    for t in range(T):
                        ins = tr(ps[0:P, ring(j.back(1), NEXT_D_IN), t * P:(t + 1) * P],
                                 dst_f[:, t:t + 1].broadcast_to([P, P]), idP)
                    ins.then_inc(d_made.sem, 1)

                def over_edges(g, h):
                    bank = 6 + h % 2
                    if h >= 2:
                        wait(pe, a_masked, g, h - 2)
                    elif h == 0:
                        wait(pe, lg_kept, g)
                        wait(pe, rows_added, g.back(1), 0)
                    for t in range(T):
                        ins = tr(ps[0:P, bank, t * P:(t + 1) * P], logit[:, t, h:h + 1].broadcast_to([P, P]), idP)
                    ins.then_inc(a_made.sem, 1)

                def vector_linear(g, t, k):
                    e = slice(t * P, (t + 1) * P)
                    if k == 0:
                        wait(pe, comb, g, 3 * (t - 1)) if t else wait(pe, comb, g.back(1))
                        mm(ps[0:P, 4, 0:2 * D], gv[:, e], wUg[0:96, 0:2 * D], start=True, stop=True)
                        mm(ps[0:P, 4, 0:CS], sg[:, e], wUs[:, 0:CS], start=False, stop=True, skip_group_check=True)
                        mm(ps[0:P, 4, D + CS:2 * D], sg[:, e], wUs[:, D + CS:2 * D], start=False, stop=True,
                           skip_group_check=True).then_inc(u_made.sem, 1)
                    else:
                        if t:
                            wait(pe, comb, g, 3 * (t - 1) + 2)
                        mm(ps[0:P, 5, 0:2 * D], gv[:, e], wUg[0:96, 2 * D:4 * D], start=True, stop=True)
                        mm(ps[0:P, 5, CS:D], sg[:, e], wUs[:, 2 * D + CS:3 * D], start=False, stop=True, skip_group_check=True)
                        mm(ps[0:P, 5, D + CS:2 * D], sg[:, e], wUs[:, 3 * D + CS:4 * D], start=False, stop=True,
                           skip_group_check=True).then_inc(u_made.sem, 1)

                def body(j):
                    new, old = halves(j)
                    g = j.back(1)
                    if new:
                        wait(pe, outer_built, j)
                        wait(pe, prod_made, j.back(1))
                        for t in range(T):
                            ins = tr(ps[:, ring(j, O_IN), t * P:(t + 1) * P], outer[j.b][:, t, :], idP)
                        ins.then_inc(outer_turned.sem, 1)
                        wait(pe, feat_added, j)
                        for k, a in enumerate((0, 32, 64, 128)):
                            if k == 0:
                                wait(pe, same_made, j)
                            elif k == 1:
                                wait(pe, outer_kept, j)
                            else:
                                wait(pe, f_kept, j, k - 2)
                            if k == 2:
                                wait(pe, feat_dup, j)
                            for t in range(T):
                                ins = tr(ps[:, ring(j, F_IN[k]), t * P:(t + 1) * P], feat[:, t, a:a + 128], idP)
                            ins.then_inc(f_turned.sem, 1)
                            if old:
                                over_edges(g, k)
                    elif old:
                        for h in range(H):
                            over_edges(g, h)
                    if old:
                        wait(pe, gv_made, g)
                        wait(pe, sg_made, g)
                        for t in range(T):
                            vector_linear(g, t, 0)
                            vector_linear(g, t, 1)
                    if new:
                        wait(pe, outer_kept, j)
                        for k in range(5):
                            wait(pe, *((f_kept, j, 2 + k) if k < 2 else (prod_made, j, k - 2)))
                            mm(ps[:, ring(j, L_IN[k]), 0:W], wL[k], oT, start=True, stop=True).then_inc(l_made.sem, 1)
                    if old:
                        wait(pe, vx_made, g)
                        for k in range(2):
                            wait(pe, a_masked, g, 2 + k)
                            for t in range(2):
                                ins = mm(ps[0:P, 6 + k, t * (D + H):(t + 1) * (D + H)], same[g.b][:, 2 * k + t, :],
                                         vx[:, 2 * k + t, :], start=True, stop=True)
                            ins.then_inc(sm_made.sem, 1)
                    if new:
                        wait(pe, xv_kept, j.back(1))
                        wait(pe, prod_made, j)
                        mm(ps[:, 2, 0:W], wX0, prod[0], start=True, stop=False)
                        mm(ps[:, 2, 0:W], wX4, prod[4], start=False, stop=True).then_inc(x_made.sem, 1)
                        wait(pe, gv_made, j.back(1))
                        mm(ps[0:96, 3, 0:W], wV4, prod[4], start=True, stop=True)
                        for k in range(3):
                            ins = mm(ps[32 * k:32 * k + 32, 3, 0:W], wV[k], prod[1 + k], start=False, stop=True,
                                     skip_group_check=True)
                        ins.then_inc(v_made.sem, 1)
                        if j.ahead(1).exists():
                            destinations(j.ahead(1))
                        wait(pe, xv_kept, j, 0)
                        wait(pe, comb, j.back(1))
                        mm(ps[0:96, 4, 0:W], wG[64:128, :], xv[64:128, :], start=True, stop=True).then_inc(g_made.sem, 1)
                        wait(pe, xv_kept, j)
                        wait(pe, rows_added, j.back(1), 1)
                        for t in range(T):
                            ins = mm(ps[0:P, 7, t * H:(t + 1) * H], rl[:, t * P:(t + 1) * P], wLr, start=True, stop=True)
                        ins.then_inc(lg_made.sem, 1)

                pe.wait_ge(edge_places_cleared, 4)
                destinations(Group(0, 0))
                steps(pe, body)

        cut["at"] = 0
        tabs = [part(NT * AC)[0:P].rearrange("p (j c) -> p j c", j=NT) for _ in range(T)]
        top = part(NT * H)[0:P].rearrange("p (j h) -> p j h", j=NT)
        nn3 = part(NT * D)[0:P].rearrange("p (j c) -> p j c", j=NT)
        stage3 = part(4 * PW)[0:P].rearrange("p (j c) -> p j c", j=4)
        aA, aB = [part(128) for _ in range(2)], [part(128) for _ in range(2)]
        w3_at = cut["at"]
        wPs, wPv = part(D), part(D)
        wMA, wMB = part(PW), part(PW)
        w3_end = cut["at"]
        zeros = part(26 * D)[0:P]
        total = tabs[0][:, 0:NT, :]
        scratch = tabs[1][:, 0:NT, 0:D]
        weights3_loaded = Count(sem("weights3_loaded"), 16)
        cleared3, scaled3 = sem("cleared3"), sem("scaled3")
        tabs_loaded = sem("tabs_loaded")
        dve3, act3, pool3 = sem("dve3"), sem("act3"), sem("pool3")
        tab_shift, tab_exp, tab_scaled = sem("tab_shift"), sem("tab_exp"), sem("tab_scaled")
        agg_ready, agg_turned, agg_kept = sem("agg_ready"), sem("agg_turned"), sem("agg_kept")
        out_made, out_kept = sem("out_made"), sem("out_kept")
        h1_ready, h1_turned, h1_kept = sem("h1_ready"), sem("h1_turned"), sem("h1_kept")
        proj_made, proj_kept, proj_stored = sem("proj_made"), sem("proj_kept"), [sem(f"proj_stored{k}") for k in range(4)]
        aggs_cleared = sem("aggs_cleared")
        stat_at = cut["at"]
        stat3 = part(8 * NT)[0:P].rearrange("p (k j) -> p k j", k=8)
        var3, std3 = sem("var3"), sem("std3")

        P_ONE, P_DIST, P_DIR, P_VEC = 0, D, 2 * D, 2 * D + 3 * CS

        def turn(pe, j, source, turned, kept):
            b = j % 2
            if j >= 2:
                pe.wait_ge(kept, 2 * (j - 1))
            nc.tensor.transpose(ps[:, b, 0:P], source[:, j, 0:128], ident[0:P, 0:P]).then_inc(turned, 1)
            nc.tensor.transpose(ps[0:32, b, 128:128 + P], source[:, j, 128:D], ident[0:P, 0:P]).then_inc(turned, 1)
            pe.wait_ge(kept, 2 * j + 2)

        def keep_turned(act, j, turned, kept, used):
            b = j % 2
            act.wait_ge(turned, 2 * j + 2)
            if j >= 2:
                act.wait_ge(used, j - 1)
            nc.scalar.activation(aA[b][:, 0:P], ps[:, b, 0:P], ACT.Copy).then_inc(kept, 1)
            nc.scalar.activation(aB[b][0:32, 0:P], ps[0:32, b, 128:128 + P], ACT.Copy).then_inc(kept, 1)

        with nc.Block() as block:
            @block.sync
            def _(sp):
                for k in range(T):
                    sp.dma_start(tabs[k], sums[k][0:N, :].rearrange("(p j) c -> p j c", p=P)).then_inc(tabs_loaded, 16)
                sp.wait_ge(cleared3, 2)
                ld = lambda a, b: weights3_loaded(sp.dma_start(a, b, allow_slow_non_contiguous=True))
                ld(wPs[0:CS, 0:CS], w["Wps"])
                for h in range(H):
                    for k in range(3):
                        r = CS + h * HV + k * 8
                        for a, n, t, base in ((r, 8, wPs, 0),) if r + 8 <= 128 else ((r - 128, 8, wPv, 0),):
                            ld(t[a:a + n, CS + k * CV:CS + (k + 1) * CV], w["Wpv"][8 * h:8 * h + 8, :])
                m = {n: w[n].rearrange("u o w -> (u o) w") for n in ("wm000", "wm011", "wm101", "wm110")}
                ld(wMA[SC:SC + CS, P_ONE:P_ONE + CS], w["lm0"])
                ld(wMA[SC:SC + CS, P_DIST:P_DIST + CS], m["wm000"])
                ld(wMA[SC:SC + CS, P_VEC:P_VEC + CV], m["wm011"])
                for k, (t, r) in enumerate(((wMA, V0), (wMA, V1), (wMB, 0))):
                    ld(t[r:r + CV, P_ONE + CS + k * CV:P_ONE + CS + (k + 1) * CV], w["lm1"])
                    ld(t[r:r + CV, P_DIST + CS + k * CV:P_DIST + CS + (k + 1) * CV], m["wm101"])
                    ld(t[r:r + CV, P_DIR + k * CS:P_DIR + (k + 1) * CS], m["wm110"])
                for k in range(T):
                    sp.dma_start(aggs[k].rearrange("(p j) c -> p (j c)", p=P), zeros).then_inc(aggs_cleared, 16)
                rows_v = proj_rows.rearrange("(p j) c -> p j c", p=P)
                for j in range(NT):
                    sp.wait_ge(proj_kept, 2 * j + 2)
                    sp.dma_start(rows_v[:, j, :], stage3[:, j % 4, :]).then_inc(proj_stored[j % 4], 16)
                for k in range(4):
                    sp.wait_ge(proj_stored[k], 16 * len(range(k, NT, 4)))
                sp.wait_ge(aggs_cleared, 16 * T)
                sp.wait_ge(weights3_loaded.sem, weights3_loaded.n)

            @block.gpsimd
            def _(pool):
                nc.gpsimd.memset(room[:, w3_at:w3_end], 0.0).then_inc(cleared3, 1)
                nc.gpsimd.memset(zeros, 0.0).then_inc(cleared3, 1)

            @block.vector
            def _(dve):
                dv = Count(dve3)
                dve.wait_ge(tabs_loaded, 16 * T)
                mx = [tabs[k][:, 0:NT, D + H:AC] for k in range(T)]
                dv(nc.vector.tensor_tensor(top, mx[0], mx[1], ALU.max))
                for k in (2, 3):
                    dv.wait(dve)
                    dv(nc.vector.tensor_tensor(top, top, mx[k], ALU.max))
                dv.wait(dve)
                for k in range(T):
                    nc.vector.tensor_tensor(mx[k], mx[k], top, ALU.subtract).then_inc(tab_shift, 1)
                dve.wait_ge(tab_exp, T)
                for k in range(T):
                    for h in range(H):
                        f = tabs[k][:, 0:NT, D + H + h:D + H + h + 1]
                        for a, n in ((h * HS, HS), (CS + h * HV, HV), (D + h, 1)):
                            v = tabs[k][:, 0:NT, a:a + n]
                            dv(nc.vector.tensor_tensor(v, v, f.broadcast_to([P, NT, n]), ALU.mult))
                dv.wait(dve)
                for k in range(1, T):
                    dv(nc.vector.tensor_tensor(total[:, :, 0:D + H], total[:, :, 0:D + H], tabs[k][:, 0:NT, 0:D + H], ALU.add))
                    dv.wait(dve)
                den = total[:, :, D:D + H]
                dv(nc.vector.tensor_scalar(den, den, 1e-16, None, ALU.add))
                dv.wait(dve)
                dv(nc.vector.reciprocal(top, den))
                dv.wait(dve)
                for h in range(H):
                    f = top[:, :, h:h + 1]
                    for a, n in ((h * HS, HS), (CS + h * HV, HV)):
                        v = total[:, :, a:a + n]
                        dv(nc.vector.tensor_tensor(v, v, f.broadcast_to([P, NT, n]), ALU.mult))
                dv.wait(dve)
                nc.vector.tensor_copy(nn3, total[:, :, 0:D]).then_inc(agg_ready, 1)
                dv(nc.vector.tensor_tensor(xs[:, :, :], xs[:, :, :], hs[:, :, :], ALU.add))
                dv.wait(dve)
                for j in range(NT):
                    dve.wait_ge(out_made, j + 1)
                    b = 4 + j % 2
                    v = xs[:, j, CS:D].rearrange("p (c k) -> p k c", k=3)
                    nc.vector.tensor_tensor(xs[:, j, 0:CS], xs[:, j, 0:CS], ps[0:P, b, 0:CS], ALU.add).then_inc(out_kept, 1)
                    nc.vector.tensor_tensor(v, v, ps[0:P, b, CS:D].rearrange("p (k c) -> p k c", k=3),
                                            ALU.add).then_inc(out_kept, 1)
                dve.wait_ge(out_kept, 2 * NT)
                dve.wait_ge(agg_turned, 2 * NT)
                norm(dve, dv, xs[:, :, :], hs[:, :, :], D, 1, True, stat3, scratch, var3, std3)
                nc.vector.tensor_copy(nn3[:, :, SC:SC + CS], hs[:, :, 0:CS]).then_inc(h1_ready, 1)
                for o, i in to_rows(nn3, hs[:, :, CS:D]):
                    nc.vector.tensor_copy(o, i).then_inc(h1_ready, 1)
                dve.wait_ge(weights3_loaded.sem, weights3_loaded.n)
                nc.vector.tensor_scalar(wMA[0:64, P_ONE:P_ONE + D], wMA[0:64, P_ONE:P_ONE + D], 32.0 ** -0.5, None, ALU.mult).then_inc(scaled3, 1)
                nc.vector.tensor_scalar(wMA[64:128, P_ONE:P_ONE + D], wMA[64:128, P_ONE:P_ONE + D], 0.125, None, ALU.mult).then_inc(scaled3, 1)
                nc.vector.tensor_scalar(wMB[0:32, P_ONE:P_ONE + D], wMB[0:32, P_ONE:P_ONE + D], 32.0 ** -0.5, None, ALU.mult).then_inc(scaled3, 1)
                for t, n in ((wMA, 128), (wMB, 32)):
                    for a, b, f in ((P_DIST, P_DIR, R96), (P_DIR, P_VEC, R96 * S3), (P_VEC, PW, R96)):
                        nc.vector.tensor_scalar(t[0:n, a:b], t[0:n, a:b], f, None, ALU.mult).then_inc(scaled3, 1)

            @block.scalar
            def _(act):
                act.wait_ge(tab_shift, T)
                for k in range(T):
                    m = tabs[k][:, 0:NT, D + H:AC]
                    nc.scalar.activation(m, m, ACT.Exp).then_inc(tab_exp, 1)
                for j in range(NT):
                    keep_turned(act, j, agg_turned, agg_kept, out_made)
                act.wait_ge(out_made, NT)
                act.wait_ge(var3, 1)
                nc.scalar.activation(stat3[:, 4, :], stat3[:, 3, :], ACT.Sqrt).then_inc(std3, 1)
                for j in range(NT):
                    b = j % 2
                    keep_turned(act, j, h1_turned, h1_kept, proj_made)
                    act.wait_ge(proj_made, j + 1)
                    if j >= 4:
                        act.wait_ge(proj_stored[j % 4], 16 * (j // 4))
                    nc.scalar.activation(stage3[:, j % 4, 0:320], ps[0:P, 4 + 2 * b, 0:320], ACT.Copy).then_inc(proj_kept, 1)
                    nc.scalar.activation(stage3[:, j % 4, 320:PW], ps[0:P, 5 + 2 * b, 0:PW - 320], ACT.Copy).then_inc(proj_kept, 1)

            @block.tensor
            def _(pe):
                pe.wait_ge(agg_ready, 1)
                pe.wait_ge(weights3_loaded.sem, weights3_loaded.n)
                for j in range(NT):
                    turn(pe, j, nn3, agg_turned, agg_kept)
                    if j >= 2:
                        pe.wait_ge(out_kept, 2 * (j - 1))
                    b = j % 2
                    o = ps[0:P, 4 + b, 0:D]
                    nc.tensor.matmul(o, aA[b][:, 0:P], wPs, start=True, stop=False)
                    nc.tensor.matmul(o, aB[b][0:32, 0:P], wPv[0:32, :], start=False, stop=True).then_inc(out_made, 1)
                pe.wait_ge(h1_ready, 4)
                pe.wait_ge(scaled3, 9)
                pe.wait_ge(out_kept, 2 * NT)
                pe.wait_ge(agg_kept, 2 * NT)
                for j in range(NT):
                    turn(pe, j, nn3, h1_turned, h1_kept)
                    if j >= 2:
                        pe.wait_ge(proj_kept, 2 * (j - 1))
                    b = j % 2
                    for k, (a, e) in enumerate(((0, 320), (320, PW))):
                        o = ps[0:P, 4 + 2 * b + k, 0:e - a]
                        nc.tensor.matmul(o, aA[b][:, 0:P], wMA[:, a:e], start=True, stop=False)
                        last = nc.tensor.matmul(o, aB[b][0:32, 0:P], wMB[0:32, a:e], start=False, stop=True)
                    last.then_inc(proj_made, 1)

        cut["at"] = 0
        m_src = [part(T, I32)[0:P] for _ in range(2)]
        m_first = [part(T, I32)[0:P] for _ in range(2)]
        m_early = part(W)[0:P].rearrange("p (t e) -> p t e", t=T)
        m_cnt, m_away, m_moved = part(T)[0:P], part(T)[0:P], part(T)[0:P]
        m_dst = [part(T, I32)[0:P] for _ in range(2)]
        m_y = [part(T * 4)[0:P] for _ in range(2)]
        m_src_f = [part(T)[0:P] for _ in range(2)]
        m_pad = part(T, I32)[0:P]
        m_rows = [part(T * PW)[0:P].rearrange("p (t c) -> p t c", t=T) for _ in range(2)]
        m_same = [part(W)[0:P].rearrange("p (t e) -> p t e", t=T) for _ in range(2)]
        m_edge = [part(T * D)[0:P].rearrange("p (t c) -> p t c", t=T) for _ in range(2)]
        m_vec = part(T * 3 * CV)[0:P].rearrange("p (t k c) -> p t k c", t=T, k=3)
        m_msg = [part(T * D)[0:P].rearrange("p (t c) -> p t c", t=T) for _ in range(2)]
        m_loaded = pair("m_loaded", 48)
        m_gathered, m_scattered = pair("m_gathered", 16 * T), pair("m_scattered", 16 * T)
        m_pad_made, m_pad_copied = sem("m_pad_made"), sem("m_pad_copied")
        m_copied, m_turned, m_masked = event("m_copied"), event("m_turned"), event("m_masked")
        m_early_made, m_counted, m_firsts_made = event("m_early_made"), event("m_counted"), event("m_firsts_made", 4)
        m_combined = event("m_combined", 4 * T + 2)
        m_summed, m_kept = event("m_summed", 2), event("m_kept", 2)

        with nc.Block() as block:
            @block.sync
            def _(sp):
                def load(g):
                    b, eds = g.b, m_loaded.sems[g.b]
                    wait(sp, m_copied, g.back(2))
                    settle(sp, 1)
                    wait(sp, m_combined, g.back(2))
                    settle(sp, 1)
                    wait(sp, m_gathered, g.back(2))
                    settle(sp, 1)
                    last = isinstance(g.i, int) and g.off == G - 1
                    n = LEFT if last else T
                    if last:
                        sp.dma_start(m_src[b][:, n:T], m_pad[:, n:T]).then_inc(m_pad_copied, 16)
                        sp.wait_ge(m_pad_copied, 16)
                    sp.dma_start(m_src[b][:, 0:n], src_v[:, bass.ds(g.number(T), n)], allow_slow_non_contiguous=True).then_inc(eds, 16)
                    sp.dma_start(m_dst[b][:, 0:n], dst_v[:, bass.ds(g.number(T), n)], allow_slow_non_contiguous=True).then_inc(eds, 16)
                    sp.dma_start(m_y[b][:, 0:n * 4], y_v[:, bass.ds(g.number(T * 4), n * 4)]).then_inc(eds, 16)

                sp.wait_ge(m_pad_made, 1)
                for g in range(2):
                    load(Group(0, g))
                with sp.Fori(0, (G - 3) // 2) as i:
                    for u in range(2):
                        load(Group(i, u + 2))
                load(Group(0, G - 1))

            @block.gpsimd
            def _(pool):
                nc.gpsimd.memset(m_pad, N).then_inc(m_pad_made, 1)

                def gather(g):
                    b = g.b
                    wait(pool, m_loaded, g)
                    wait(pool, m_combined, g.back(2))
                    settle(pool, 0)
                    for t in range(T):
                        nc.gpsimd.indirect_dma_start(m_rows[b][:, t, :], None, proj_rows,
                                                     bass.IndirectOffsetOnAxis(ap=m_dst[b][:, t:t + 1], axis=0)
                                                     ).then_inc(m_gathered.sems[b], 16)

                def add(g):
                    b = g.b
                    wait(pool, m_kept, g)
                    wait(pool, m_firsts_made, g)
                    wait(pool, m_scattered, g.back(1))
                    settle(pool, 0)
                    for t in range(T):
                        nc.gpsimd.indirect_dma_start(aggs[t], bass.IndirectOffsetOnAxis(ap=m_first[b][:, t:t + 1], axis=0),
                                                     m_msg[b][:, t, :], None, compute_op=ALU.add
                                                     ).then_inc(m_scattered.sems[b], 16)

                gather(Group(0, 0))
                gather(Group(0, 1))
                gather(Group(0, 2))
                add(Group(0, 0))
                with pool.Fori(0, (G - 3) // 2) as i:
                    for u in range(2):
                        gather(Group(i, u + 3))
                        add(Group(i, u + 1))
                for g in range(G - 2, G):
                    add(Group(0, g))
                wait(pool, m_scattered, Group(0, G - 2))
                wait(pool, m_scattered, Group(0, G - 1))

            @block.vector
            def _(dve):
                def copy_src(j):
                    b = j.b
                    wait(dve, m_loaded, j)
                    wait(dve, m_turned, j.back(2))
                    wait(dve, m_firsts_made, j.back(2))
                    nc.vector.tensor_copy(m_src_f[b], m_src[b]).then_inc(m_copied.sem, 1)

                def masks(j):
                    b = j.b
                    wait(dve, m_turned, j)
                    wait(dve, m_copied, j)
                    wait(dve, m_summed, j.back(2))
                    wait(dve, m_early_made, j.back(2))
                    nc.vector.tensor_tensor(m_same[b], ps[0:P, b, 0:W].rearrange("p (t e) -> p t e", t=T),
                                            m_src_f[b].unsqueeze(2).broadcast_to([P, T, P]), ALU.is_equal).then_inc(m_masked.sem, 1)
                    wait(dve, m_firsts_made, j.back(1))
                    nc.vector.tensor_scalar(m_away, m_src_f[b], -1.0, pcol[:, 0:1], ALU.mult, ALU.add).then_inc(m_firsts_made.sem, 1)
                    wait(dve, m_masked, j)
                    wait(dve, m_counted, j.back(1))
                    nc.vector.tensor_tensor(m_early, m_same[b], before[:, :].unsqueeze(1).broadcast_to([P, T, P]),
                                            ALU.mult).then_inc(m_early_made.sem, 1)
                    wait(dve, m_early_made, j)
                    nc.vector.tensor_reduce(m_cnt, m_early, AX.X, ALU.add).then_inc(m_counted.sem, 1)
                    wait(dve, m_counted, j)
                    nc.vector.tensor_scalar(m_cnt, m_cnt, 0.5, None, ALU.is_gt).then_inc(m_firsts_made.sem, 1)
                    wait(dve, m_firsts_made, j, 1)
                    nc.vector.tensor_tensor(m_moved, m_away, m_cnt, ALU.mult).then_inc(m_firsts_made.sem, 1)
                    wait(dve, m_firsts_made, j, 2)
                    wait(dve, m_scattered, j.back(2))
                    nc.vector.tensor_tensor(m_first[b], m_moved, m_src_f[b], ALU.add).then_inc(m_firsts_made.sem, 1)

                def messages(g):
                    b = g.b
                    y, r, o = m_y[b], m_rows[b], m_edge[b]
                    wait(dve, m_gathered, g)
                    wait(dve, m_summed, g.back(2))
                    for t in range(T):
                        nc.vector.scalar_tensor_tensor(o[:, t, :], r[:, t, P_DIST:P_DIST + D], y[:, 4 * t + 3:4 * t + 4],
                                                       r[:, t, P_ONE:P_ONE + D], ALU.mult, ALU.add).then_inc(m_combined.sem, 1)
                    wait(dve, m_combined, g.back(1))
                    nc.vector.tensor_tensor(m_vec, r[:, :, P_VEC:PW].unsqueeze(2).broadcast_to([P, T, 3, CV]),
                                            y.rearrange("p (t c) -> p t c", c=4)[:, :, 0:3].unsqueeze(3).broadcast_to([P, T, 3, CV]),
                                            ALU.mult).then_inc(m_combined.sem, 1)
                    for k in range(3):
                        for t in range(T):
                            wait(dve, m_combined, g, t if k == 0 else T + 1 + T * (k - 1) + t)
                            v = o[:, t, 0:CS]
                            nc.vector.scalar_tensor_tensor(v, r[:, t, P_DIR + k * CS:P_DIR + (k + 1) * CS],
                                                           y[:, 4 * t + k:4 * t + k + 1], v, ALU.mult, ALU.add
                                                           ).then_inc(m_combined.sem, 1)
                    v = o[:, :, CS:D].rearrange("p t (k c) -> p t k c", k=3)
                    nc.vector.tensor_tensor(v, v, m_vec, ALU.add).then_inc(m_combined.sem, 1)

                def body(j):
                    new, old = halves(j)
                    if new:
                        copy_src(j)
                    if old:
                        messages(j.back(1))
                    if new:
                        masks(j)

                steps(dve, body)

            @block.tensor
            def _(pe):
                def body(j):
                    new, old = halves(j)
                    if new:
                        wait(pe, m_copied, j)
                        wait(pe, m_masked, j.back(2))
                        for t in range(T):
                            ins = nc.tensor.transpose(ps[0:P, j.b, t * P:(t + 1) * P],
                                                      m_src_f[j.b][:, t:t + 1].broadcast_to([P, P]), ident[0:P, 0:P])
                        ins.then_inc(m_turned.sem, 1)
                    if old:
                        g = j.back(1)
                        b = g.b
                        wait(pe, m_masked, g)
                        wait(pe, m_combined, g)
                        for t in range(T):
                            if t % 2 == 0:
                                wait(pe, m_kept, g.back(2), t // 2)
                            ins = nc.tensor.matmul(ps[0:P, 2 + 2 * b + t // 2, (t % 2) * D:(t % 2 + 1) * D],
                                                   m_same[b][:, t, :], m_edge[b][:, t, :], start=True, stop=True)
                            if t % 2:
                                ins.then_inc(m_summed.sem, 1)

                steps(pe, body)

            @block.scalar
            def _(act):
                def body(j):
                    new, old = halves(j)
                    if not old:
                        return
                    g = j.back(1)
                    wait(act, m_scattered, g.back(2))
                    for k in range(2):
                        wait(act, m_summed, g, k)
                        nc.scalar.activation(m_msg[g.b][:, 2 * k:2 * k + 2, :],
                                             ps[0:P, 2 + 2 * g.b + k, 0:2 * D].rearrange("p (t c) -> p t c", t=2),
                                             ACT.Copy).then_inc(m_kept.sem, 1)

                steps(act, body)

        cut["at"] = 0
        YC = 2048
        agg = part(NT * D)[0:P].rearrange("p (j c) -> p j c", j=NT)
        slot_at = cut["at"]
        tab5 = [part(NT * D)[0:P].rearrange("p (j c) -> p j c", j=NT) for _ in range(3)]
        cut["at"] = slot_at
        slots0 = part(NT * 5 * CS)[0:P].rearrange("p (j s w) -> p j s w", j=NT, s=5)
        slots1 = part(NT * 2 * 3 * CV)[0:P].rearrange("p (j s w) -> p j s w", j=NT, s=6)
        lin = part(NT * D)[0:P].rearrange("p (j c) -> p j c", j=NT)
        wy_at = cut["at"]
        wYs, wY0, wY1 = part(2 * YC + CV * CV), part(2 * YC), part(2 * YC)
        wLA, wLB = part(D), part(D)
        wy_end = cut["at"]
        zbuf = [part(YC)[0:P] for _ in range(3)]
        tile = part(D)[0:P]
        hA, hB = part(128), part(128)
        cleared5, scaled5, aggs_loaded = sem("cleared5"), sem("scaled5"), sem("aggs_loaded")
        weights5_loaded = Count(sem("weights5_loaded"), 16)
        dve5, agg_summed = sem("dve5"), sem("agg_summed")
        CH = 9
        tile_kept, turned5, turned5_kept = event("tile_kept", 4), event("turned5", 2), event("turned5_kept", 2)
        y_made, lin_made, lin_kept = event("y_made", CH), event("lin_made"), event("lin_kept")
        NQ = 11
        z_made, z_halved, z_summed = event("z_made", NQ), event("z_halved", NQ), event("z_summed", NQ)
        stored = sem("stored")
        products = ([(0, 0, 32, CS, 0, 0), (1, 32, 32, CS, 0, 1)]
                    + [(2, CS + k * CV, CV, CV, 1, k) for k in range(3)]
                    + [(3 + k, CS + k * CV, CV, CS, 0, 2 + k) for k in range(3)]
                    + [(6 + k, 0, CS, CV, 1, 3 + k) for k in range(3)])
        last_of = {c: max(q for q, p in enumerate(products) if p[0] == c) for c in range(CH)}

        def tiles(eng, body):
            body(Group(0, 0, 1))
            with eng.Fori(0, NT - 1) as i:
                body(Group(i, 1, 1))

        with nc.Block() as block:
            @block.sync
            def _(sp):
                for k in range(T):
                    sp.dma_start(([agg] + tab5)[k], aggs[k][0:N, :].rearrange("(p j) c -> p j c", p=P)).then_inc(aggs_loaded, 16)
                sp.wait_ge(cleared5, 2)
                ld = lambda a, b: weights5_loaded(sp.dma_start(a, b))
                ld(wYs[SC:SC + CS, 0:2 * YC], w["wu000"].rearrange("u v w -> u (v w)"))
                ld(wYs[SC:SC + CS, 2 * YC:2 * YC + CV * CV], w["wu011"].rearrange("u v w -> u (v w)"))
                for t, r in ((wY0, V0), (wY1, V1)):
                    ld(t[r:r + CV, 0:YC], w["wu110"].rearrange("u v w -> u (v w)"))
                    ld(t[r:r + CV, YC:2 * YC], w["wu101"].rearrange("u v w -> u (v w)"))
                ld(wLA[SC:SC + CS, 0:CS], w["lu0"])
                for k, (t, r) in enumerate(((wLA, V0), (wLA, V1), (wLB, 0))):
                    ld(t[r:r + CV, CS + k * CV:CS + (k + 1) * CV], w["lu1"])
                sp.wait_ge(z_summed.sem, NQ * NT + 1)
                sp.dma_start(out.rearrange("(p j) c -> p j c", p=P), xs[:, :, :]).then_inc(stored, 16)
                sp.wait_ge(stored, 16)

            @block.gpsimd
            def _(pool):
                nc.gpsimd.memset(room[:, wy_at:wy_end], 0.0).then_inc(cleared5, 1)
                nc.gpsimd.memset(hB, 0.0).then_inc(cleared5, 1)

                def body(j):
                    for q, (c, _, v, n, _, _) in enumerate(products):
                        z, half = zbuf[q % 3], v * n // 2
                        wait(pool, z_made, j, q)
                        nc.gpsimd.tensor_tensor(z[:, 0:half], z[:, 0:half], z[:, half:2 * half], ALU.add).then_inc(z_halved.sem, 1)

                tiles(pool, body)

            @block.vector
            def _(dve):
                dv = Count(dve5)
                dve.wait_ge(aggs_loaded, 16 * T)
                for k in range(3):
                    dv(nc.vector.tensor_tensor(agg, agg, tab5[k], ALU.add))
                    dv.wait(dve)
                nc.vector.tensor_tensor(xs[:, :, :], xs[:, :, :], hs[:, :, :], ALU.add).then_inc(agg_summed, 1)
                dve.wait_ge(agg_summed, 1)

                def total(j, q):
                    c, _, v, n, tab, s = products[q]
                    wait(dve, z_halved, j, q)
                    o = (slots0, slots1)[tab]
                    o = o[:, bass.ds(j.number(1), 1), s, 0:n]
                    nc.vector.tensor_reduce(o, zbuf[q % 3][:, 0:v * n // 2].rearrange("p (v w) -> p w v", w=n).unsqueeze(1),
                                            AX.X, ALU.add).then_inc(z_summed.sem, 1)

                def body(j):
                    for q, (c, a, v, n, _, _) in enumerate(products):
                        wait(dve, y_made, j, c)
                        if q < 3:
                            before_q = max(p for p in range(NQ) if p % 3 == q % 3)
                            wait(dve, z_summed, j.back(1), before_q)
                        else:
                            wait(dve, z_summed, j, q - 3)
                        p0 = ps[0:P, :, :].rearrange("p b c -> p (b c)")[:, (c % 2) * YC:(c % 2) * YC + v * n]
                        f = agg[:, bass.ds(j.number(1), 1), a:a + v].rearrange("p o v -> p (o v)")
                        nc.vector.tensor_tensor(zbuf[q % 3][:, 0:v * n].rearrange("p (v w) -> p v w", w=n),
                                                p0.rearrange("p (v w) -> p v w", w=n),
                                                f.unsqueeze(2).broadcast_to([P, v, n]), ALU.mult).then_inc(z_made.sem, 1)
                        if q >= 1:
                            total(j, q - 1)
                    total(j, NQ - 1)

                tiles(dve, body)
                dve.wait_ge(z_summed.sem, NQ * NT)
                dve.wait_ge(lin_kept.sem, NT)
                s = xs[:, :, 0:CS]
                v = xs[:, :, CS:D].rearrange("p j (c k) -> p j c k", k=3)
                dv(nc.vector.tensor_tensor(s, s, lin[:, :, 0:CS], ALU.add))
                for k in range(3):
                    dv(nc.vector.tensor_tensor(v[:, :, :, k], v[:, :, :, k], lin[:, :, CS + k * CV:CS + (k + 1) * CV], ALU.add))
                dv.wait(dve)
                for i in range(5):
                    dv(nc.vector.tensor_tensor(s, s, slots0[:, :, i, :], ALU.add))
                    if i < 2:
                        for k in range(3):
                            dv(nc.vector.tensor_tensor(v[:, :, :, k], v[:, :, :, k], slots1[:, :, 3 * i + k, :], ALU.add))
                    dv.wait(dve)
                nc.vector.tensor_copy(agg[:, 0, 0:1], agg[:, 0, 1:2]).then_inc(z_summed.sem, 1)

            @block.scalar
            def _(act):
                act.wait_ge(weights5_loaded.sem, weights5_loaded.n)
                n = 0
                for t, a, e, f in ((wYs, 0, 2 * YC, K0), (wYs, 2 * YC, 2 * YC + CV * CV, K1), (wY0, 0, YC, K0 * S3),
                                   (wY0, YC, 2 * YC, K1), (wY1, 0, YC, K0 * S3), (wY1, YC, 2 * YC, K1)):
                    nc.scalar.mul(t[:, a:e], t[:, a:e], f).then_inc(scaled5, 1)
                for t, r, f in ((wLA[64:128, :], 0, 0.125), (wLA[0:64, :], 0, 32.0 ** -0.5), (wLB, 0, 32.0 ** -0.5)):
                    nc.scalar.mul(t, t, f).then_inc(scaled5, 1)
                act.wait_ge(cleared5, 2)

                def body(j):
                    wait(act, turned5, j.back(1))
                    row = hs[:, bass.ds(j.number(1), 1), :].rearrange("p o c -> p (o c)")
                    nc.scalar.activation(tile[:, SC:SC + CS], row[:, 0:CS], ACT.Copy).then_inc(tile_kept.sem, 1)
                    v = row[:, CS:D].rearrange("p (c k) -> p k c", k=3)
                    for k, at in enumerate((V0, V1, V2)):
                        nc.scalar.activation(tile[:, at:at + CV], v[:, k, :], ACT.Copy).then_inc(tile_kept.sem, 1)
                    wait(act, turned5, j)
                    wait(act, lin_made, j.back(1))
                    nc.scalar.activation(hA[:, 0:P], ps[:, 7, 256:256 + P], ACT.Copy).then_inc(turned5_kept.sem, 1)
                    nc.scalar.activation(hB[0:32, 0:P], ps[0:32, 7, 384:384 + P], ACT.Copy).then_inc(turned5_kept.sem, 1)
                    wait(act, lin_made, j)
                    nc.scalar.activation(lin[:, bass.ds(j.number(1), 1), :], ps[0:P, 4:5, 0:D], ACT.Copy).then_inc(lin_kept.sem, 1)

                act.wait_ge(agg_summed, 1)
                tiles(act, body)

            @block.tensor
            def _(pe):
                pe.wait_ge(scaled5, 9)
                pe.wait_ge(cleared5, 2)

                def body(j):
                    wait(pe, tile_kept, j)
                    wait(pe, z_made, j.back(1), last_of[7])
                    wait(pe, lin_kept, j.back(1))
                    nc.tensor.transpose(ps[:, 7, 256:256 + P], tile[:, 0:128], ident[0:P, 0:P]).then_inc(turned5.sem, 1)
                    nc.tensor.transpose(ps[0:32, 7, 384:384 + P], tile[:, 128:D], ident[0:P, 0:P]).then_inc(turned5.sem, 1)
                    wait(pe, turned5_kept, j)
                    for c in range(CH):
                        if c < 2:
                            wait(pe, z_made, j.back(1), last_of[8 - c] if c == 0 else last_of[7])
                        else:
                            wait(pe, z_made, j, last_of[c - 2])
                        left, wt, at, n = ((hA, wYs, 0, YC), (hA, wYs, YC, YC), (hA, wYs, 2 * YC, CV * CV),
                                           (hA, wY0, 0, YC), (hA, wY1, 0, YC), (hB, wY0, 0, YC),
                                           (hA, wY0, YC, YC), (hA, wY1, YC, YC), (hB, wY0, YC, YC))[c]
                        for k in range(n // 512):
                            ins = nc.tensor.matmul(ps[0:P, 4 * (c % 2) + k, :], left[:, 0:P], wt[:, at + 512 * k:at + 512 * (k + 1)],
                                                   start=True, stop=True)
                        ins.then_inc(y_made.sem, 1)
                    wait(pe, z_made, j, last_of[7])
                    nc.tensor.matmul(ps[0:P, 4, 0:D], hA[:, 0:P], wLA, start=True, stop=False)
                    nc.tensor.matmul(ps[0:P, 4, 0:D], hB[:, 0:P], wLB, start=False, stop=True).then_inc(lin_made.sem, 1)

                tiles(pe, body)


WEIGHTS = {
    "L0_gnn_": ["gamma_s", "beta_s", "gamma_v", "Ws_src", "Wv_src", "Ws_dst", "Wv_dst", "W_rbf", "W_alpha",
                "alpha_dot", "Ws_val", "Wv_val", "Wg", "w2_ss", "w2_sv", "w2_vs", "w2_vv0", "w2_vv1",
                "Ws_vlin", "Wv_vlin", "Wps", "Wpv"],
    "L1_gnn_": ["wm000", "wm011", "wm101", "wm110", "lm0", "lm1", "wu000", "wu011", "wu101", "wu110", "lu0", "lu1"],
}


def kernel(**inputs):
    import numpy as np
    import concourse.bacc as bacc
    from concourse.bass_utils import run_bass_kernel_spmd

    nc = bacc.Bacc("TRN2", target_bir_lowering=False, num_devices=1)
    arrays = {}

    def given(name):
        a = np.ascontiguousarray(inputs[name])
        arrays[f"in_{name}"] = a
        return nc.dram_tensor(f"in_{name}", a.shape, mybir.dt.from_np(a.dtype), kind="ExternalInput").ap()

    args = [given(n) for n in ("x", "src", "dst", "edge_attr_16", "edge_attr_4")]
    weights = {n: given(prefix + n) for prefix, names in WEIGHTS.items() for n in names}
    out = nc.dram_tensor("out_x", (N, D), F32, kind="ExternalOutput").ap()
    build(nc, *args, weights, out)
    r = run_bass_kernel_spmd(nc, [arrays], core_ids=[0])
    return r.results[0]["out_x"]
```

```python
from contextlib import ExitStack

import concourse.bass as bass
from concourse import mybir

F32 = mybir.dt.float32
I32 = mybir.dt.int32
ALU = mybir.AluOpType
ACT = mybir.ActivationFunctionType
AX = mybir.AxisListType

N, E = 3125, 53125
CS, CV = 64, 32
D = CS + 3 * CV
H = 4
NB = 16
P = 125
NT = N // P
ET = E // P
T = 4
G = -(-ET // T)
LEFT = ET - T * (G - 1)
W = T * P
ROWS = 26 * P
AC = D + 2 * H
PW = 544
LOW = -1.0e30
EPS = 1e-5
S2, S3 = 2.0 ** -0.5, 3.0 ** -0.5
R96 = 96.0 ** -0.5
K0, K1 = (CS * CS + CV * CV) ** -0.5, (2 * CS * CV) ** -0.5

O_BANK, F_BANK, L_BANK, D_BANK = 0, (1, 0, 1, 0), (5, 1, 0, 5, 0), 1

V0, V1, SC, V2 = 0, 32, 64, 128
HEADS = ((V0, CV // H), (V1, CV // H), (SC, CS // H), (V2, CV // H))
HW = D + 2 * CV
RUNS = ((V2, 3 * CV), (V1, 2 * CV + CS), (SC, 2 * CV + CS), (V0, 2 * CV + CS))
U_AT = (0, 96, 224, 352)
UW = 480
SUMS = [(2 * p + t, c) for p in range(T // 2) for c in range(4) for t in range(2)]
SUM_NO = {s: n for n, s in enumerate(SUMS)}
U_BANK = (3, 4, 3, 4)


class Event:

    def __init__(self, sem, per):
        self.sem, self.per = sem, per

    def value(self, g, k=None):
        return g.number(self.per, self.per if k is None else k + 1)


class Pair:

    def __init__(self, sems, per):
        self.sems, self.per = sems, per


class Group:

    def __init__(self, i, off, stride=2):
        self.i, self.off, self.stride = i, off, stride
        self.b = off % 2

    def back(self, n):
        return Group(self.i, self.off - n, self.stride)

    def ahead(self, n):
        return self.back(-n)

    def number(self, per, plus=0):
        return self.i * (self.stride * per) + (self.off * per + plus)

    def pair(self, per):
        return self.i * per + (self.off // 2 + 1) * per

    def exists(self):
        return not (isinstance(self.i, int) and not 0 <= self.off < G)


def wait(eng, event, g, k=None):
    if not g.exists():
        return
    if isinstance(event, Pair):
        eng.wait_ge(event.sems[g.b], g.pair(event.per))
    else:
        eng.wait_ge(event.sem, event.value(g, k))


class Count:

    def __init__(self, sem, step=1):
        self.sem, self.step, self.n = sem, step, 0

    def __call__(self, ins):
        self.n += self.step
        ins.then_inc(self.sem, self.step)
        return self.n

    def wait(self, eng, n=None):
        eng.wait_ge(self.sem, self.n if n is None else n)


def build(nc, x, src, dst, edge16, edge4, w, out):
    ctx = ExitStack()
    with ctx:
        def sb(name, shape, dt=F32):
            return ctx.enter_context(nc.sbuf_tensor(name, shape, dt))

        def sem(name):
            return ctx.enter_context(nc.semaphore(name))

        def event(name, per=1):
            return Event(sem(name), per)

        def pair(name, per):
            return Pair([sem(f"{name}_even"), sem(f"{name}_odd")], per)

        def dram(name, shape, dt=F32):
            return nc.dram_tensor(name, shape, dt, kind="Internal").ap()

        src_rows = dram("src_rows", (N, D))
        dst_rows = dram("dst_rows", (ROWS, D))
        sums = [dram(f"sums{k}", (ROWS, AC)) for k in range(T)]
        proj_rows = dram("proj_rows", (N, PW))
        aggs = [dram(f"aggs{k}", (ROWS, D)) for k in range(T)]

        ps = ctx.enter_context(nc.psum_tensor("ps", [128, 8, 512], F32))

        xs = sb("xs", [P, NT, D])
        hs = sb("hs", [P, NT, D])
        ident = sb("ident", [128, 128])
        before = sb("before", [P, P])
        pcol = sb("pcol", [P, 1])
        pcol_i = sb("pcol_i", [P, 1], I32)
        room = sb("room", [128, 42000])
        cut = {"at": 0}

        def part(width, dt=F32):
            a = cut["at"]
            cut["at"] = a + width
            assert cut["at"] <= 42000, cut["at"]
            v = room[:, a:a + width]
            return v if dt == F32 else v.bitcast(dt)

        stage = part(NT * 2 * D)[0:P].rearrange("p (j c) -> p j c", j=NT)
        nn = part(NT * D)[0:P].rearrange("p (j c) -> p j c", j=NT)
        tmp = part(NT * D)[0:P].rearrange("p (j c) -> p j c", j=NT)
        stat = part(8 * NT)[0:P].rearrange("p (k j) -> p k j", k=8)
        nA = [part(128) for _ in range(2)]
        nB = [part(128) for _ in range(2)]
        gam = part(CS + CV + CS)
        wA = part(2 * D)
        wB = part(2 * D)
        init_row = part(26 * AC)[0:P].rearrange("p (j c) -> p j c", j=26)
        node_end = cut["at"]

        cut["at"] = 0
        e_src = [part(T, I32)[0:P] for _ in range(2)]
        e_dst = [part(T, I32)[0:P] for _ in range(2)]
        e_rbf = [part(T * NB)[0:P] for _ in range(2)]
        e_y = [part(T * 4)[0:P] for _ in range(2)]
        pad_dst = part(T, I32)[0:P]
        g_src = [part(T * D)[0:P] for _ in range(2)]
        g_dst = [part(T * D)[0:P] for _ in range(2)]
        outer = [part(T * 128)[0:P].rearrange("p (t c) -> p t c", t=T) for _ in range(2)]
        y_kept = [part(T * 4)[0:P] for _ in range(2)]
        dst_kept = [part(T, I32)[0:P] for _ in range(2)]
        dst_f = part(T)[0:P]
        feat = part(T * 256)[0:P].rearrange("p (t c) -> p t c", t=T)
        oT = part(W)
        fT = [part(W) for _ in range(4)]
        prod = [part(W) for _ in range(5)]
        xv = part(W)
        rl = part(W)
        sg = part(W)
        tg = part(W)[0:96]
        gv = part(W)[0:96]
        logit = part(T * H)[0:P].rearrange("p (t h) -> p t h", t=T)
        same = [part(W)[0:P].rearrange("p (t e) -> p t e", t=T) for _ in range(2)]
        apart = [part(W)[0:P].rearrange("p (t e) -> p t e", t=T) for _ in range(2)]
        early = part(W)[0:P].rearrange("p (t e) -> p t e", t=T)
        masked = [part(W)[0:P].rearrange("p (t e) -> p t e", t=T) for _ in range(2)]
        cnt = part(T)[0:P]
        away = part(T)[0:P]
        moved = part(T)[0:P]
        first = [part(T, I32)[0:P] for _ in range(2)]
        rows = [part(T * AC)[0:P].rearrange("p (t c) -> p t c", t=T) for _ in range(2)]
        gmax = part(T * H)[0:P].rearrange("p (t h) -> p t h", t=T)
        newmax = part(T * H)[0:P].rearrange("p (t h) -> p t h", t=T)
        shift = part(2 * T * H)[0:P].rearrange("p (k t h) -> p k t h", k=2, t=T)
        scale = part(2 * T * H)[0:P].rearrange("p (k t h) -> p k t h", k=2, t=T)
        ht = part(T * HW)[0:P].rearrange("p (t c) -> p t c", t=T)
        vx = part(T * (D + H))[0:P].rearrange("p (t c) -> p t c", t=T)
        edge_end = cut["at"]
        cut["at"] = w_at = max(node_end, edge_end)
        wl_all = part(5 * 128)
        wL = [wl_all[:, k * 128:(k + 1) * 128] for k in range(5)]
        wX0, wX4 = part(128), part(128)
        wV = [part(32) for _ in range(3)]
        wV4 = part(96)
        wG = part(96)
        wLr = part(H)
        wUg, wUs = part(UW), part(CS + CV)
        w2col = part(8)
        l0_end = cut["at"]


        inputs_loaded = sem("inputs_loaded")
        cleared = sem("cleared")
        weights_loaded = Count(sem("weights_loaded"), 16)
        dve_step, act_step, pool_step = sem("dve_step"), sem("act_step"), sem("pool_step")
        weights_scaled = sem("weights_scaled")
        var_ready, std_ready = sem("var_ready"), sem("std_ready")
        consts_made = sem("consts_made")
        nn_ready = sem("nn_ready")
        nodes_turned, turned_kept = sem("nodes_turned"), sem("turned_kept")
        projected, projection_kept = sem("projected"), sem("projection_kept")
        tables_stored = sem("tables_stored")
        edge_places_cleared = sem("edge_places_cleared")
        pad_copied = sem("pad_copied")
        settled = [sem("pool_settled"), sem("sync_settled")]

        edges_loaded = pair("edges_loaded", 64)
        nodes_gathered = pair("nodes_gathered", 2 * T * 16)
        rows_gathered = pair("rows_gathered", T * 16)
        rows_scattered = pair("rows_scattered", T * 16)
        outer_built = event("outer_built", 4)
        copies_made = event("copies_made", 3)
        feat_added, feat_dup = event("feat_added"), event("feat_dup", 2)
        outer_turned, outer_kept = event("outer_turned"), event("outer_kept")
        f_turned, f_kept = event("f_turned", 4), event("f_kept", 4)
        l_made, prod_made = event("l_made", 5), event("prod_made", 5)
        x_made, v_made, xv_kept = event("x_made"), event("v_made"), event("xv_kept", 3)
        g_made, tg_made, sg_made = event("g_made"), event("tg_made"), event("sg_made", 2)
        gv_made = event("gv_made")
        lg_made, lg_kept = event("lg_made"), event("lg_kept")
        d_made, same_made, masks_made = event("d_made"), event("same_made"), event("masks_made", 2)
        early_counted = event("early_counted")
        firsts_made = event("firsts_made", 4)
        a_made, a_masked, a_max = event("a_made", 4), event("a_masked", 4), event("a_max", 4)
        shift_made, exp_made = event("shift_made", 3), event("exp_made")
        us_made, u_made, zeroed = event("us_made"), event("u_made", T), event("zeroed")
        t0_made, comb, folded = event("t0_made", 4 * T), event("comb", 4 * T), event("folded")
        vx_made, sm_made = event("vx_made", 5), event("sm_made", 2)
        rows_scaled, rows_added = event("rows_scaled", 5), event("rows_added", 3)

        def settle(eng, k):
            eng.sem_inc(settled[k], 1)

        def fold(ap):
            return ap.rearrange("(p t) c -> p (t c)", p=P)

        src_v, dst_v = src.rearrange("(p t) -> p t", p=P), dst.rearrange("(p t) -> p t", p=P)
        rbf_v, y_v = fold(edge16), fold(edge4)

        def norm(dve, dv, raw, res, c, root, relu, stat, tmp, var_ready, std_ready):
            bc = lambda k: stat[:, k, :].unsqueeze(2).broadcast_to([P, NT, c])
            dv(nc.vector.tensor_reduce(stat[:, 0, :], raw, AX.X, ALU.add))
            dv.wait(dve)
            dv(nc.vector.tensor_scalar(stat[:, 1, :], stat[:, 0, :], 1.0 / c, None, ALU.mult))
            dv.wait(dve)
            dv(nc.vector.tensor_tensor(res, raw, bc(1), ALU.subtract))
            dv.wait(dve)
            dv(nc.vector.tensor_tensor(tmp[:, :, 0:c], res, res, ALU.mult))
            dv.wait(dve)
            dv(nc.vector.tensor_reduce(stat[:, 2, :], tmp[:, :, 0:c], AX.X, ALU.add))
            dv.wait(dve)
            nc.vector.tensor_scalar(stat[:, 3, :], stat[:, 2, :], 1.0 / c, EPS, ALU.mult, ALU.add).then_inc(var_ready, 1)
            dve.wait_ge(std_ready, root)
            dv(nc.vector.reciprocal(stat[:, 5, :], stat[:, 4, :]))
            dv.wait(dve)
            dv(nc.vector.tensor_tensor(res, res, bc(5), ALU.mult))
            dv.wait(dve)
            if relu:
                dv(nc.vector.tensor_scalar(res, res, 0.0, None, ALU.max))
                dv.wait(dve)

        def root_of(act, root):
            act.wait_ge(var_ready, root)
            nc.scalar.activation(stat[:, 4, :], stat[:, 3, :], ACT.Sqrt).then_inc(std_ready, 1)

        def to_rows(dst_ap, vecs):
            v = vecs.rearrange("p j (c k) -> p j c k", k=3)
            return [(dst_ap[:, :, at:at + CV], v[:, :, :, k]) for k, at in enumerate((V0, V1, V2))]

        with nc.Block() as block:
            @block.sync
            def _(sp):
                sp.dma_start(xs[:, :, :], x.rearrange("(p j) c -> p j c", p=P)).then_inc(inputs_loaded, 16)
                sp.dma_start(gam[0:P, 0:CS], w["gamma_s"].partition_broadcast(P)).then_inc(inputs_loaded, 16)
                sp.dma_start(gam[0:P, CS:2 * CS], w["beta_s"].partition_broadcast(P)).then_inc(inputs_loaded, 16)
                sp.dma_start(gam[0:P, 2 * CS:2 * CS + CV], w["gamma_v"].partition_broadcast(P)).then_inc(inputs_loaded, 16)
                sp.wait_ge(cleared, 3)
                ld = lambda a, b: weights_loaded(sp.dma_start(a, b, allow_slow_non_contiguous=True))
                for k, (ws, wv) in enumerate(((w["Ws_src"], w["Wv_src"]), (w["Ws_dst"], w["Wv_dst"]))):
                    ld(wA[V0:V0 + 32, k * D + V0:k * D + V0 + 32], wv)
                    ld(wA[V1:V1 + 32, k * D + V1:k * D + V1 + 32], wv)
                    ld(wA[SC:SC + 64, k * D + SC:k * D + SC + 64], ws)
                    ld(wB[0:32, k * D + V2:k * D + V2 + 32], wv)
                Wr = w["W_rbf"]
                r_ss, r_sv = Wr[:, 0:64], Wr[:, 64:128]
                r_vs, r_vv0, r_vv1 = Wr[:, 128:160], Wr[:, 160:192], Wr[:, 192:224]
                lw = [[(0, 1, r_vv0), (32, 2, r_vv0), (64, 0, r_ss)],
                      [(0, 0, r_vs), (32, 3, r_vv1), (64, 1, r_sv)],
                      [(0, 0, r_vs), (32, 2, r_sv), (96, 1, r_vv1)],
                      [(0, 3, r_sv), (64, 0, r_vs), (96, 2, r_vv1)],
                      [(0, 2, r_vv1), (32, 3, r_vv1), (64, 1, r_vv1), (96, 3, r_vv0)]]
                for k in range(5):
                    for col, c, b in lw[k]:
                        ld(wL[k][16 * c:16 * c + 16, col:col + b.shape[1]], b)
                for col, m in ((0, w["W_alpha"]), (64, w["Ws_val"])):
                    ld(wX0[0:32, col:col + 64], m[64:96, :])
                    ld(wX0[32:64, col:col + 64], m[64:96, :])
                    ld(wX0[64:128, col:col + 64], m[0:64, :])
                    ld(wX4[96:128, col:col + 64], m[64:96, :])
                Wv = w["Wv_val"]
                for k, (s_at, vs_at, c_at) in enumerate(((64, 0, 32), (32, 0, 96), (0, 64, 96))):
                    ld(wV[k][s_at:s_at + 64, :], Wv[0:64, :])
                    ld(wV[k][vs_at:vs_at + 32, :], Wv[64:96, :])
                    ld(wV[k][c_at:c_at + 32, :], Wv[96:128, :])
                for k in range(3):
                    ld(wV4[32 * k:32 * k + 32, 32 * k:32 * k + 32], Wv[96:128, :])
                    ld(wG[64:128, 32 * k:32 * k + 32], w["Wg"])
                for h in range(H):
                    a = w["alpha_dot"][0, h, :].rearrange("(a o) -> a o", o=1)
                    for r in (0, CS):
                        ld(wLr[r + h * CS // H:r + (h + 1) * CS // H, h:h + 1], a)
                Wh, Wl = w["Wv_vlin"], w["Ws_vlin"]

                for k, to in ((2, 0), (0, 1), (1, 2)):
                    ld(wUg[32 * k:32 * k + 32, to * CV:(to + 1) * CV], Wh[64:96, :])
                for j, (s_at, plus, minus) in enumerate(((32, 0, 96), (0, 64, 96), (64, 0, 32))):
                    a, b, at = (j + 1) % 3, (j + 2) % 3, U_AT[1 + j]
                    ld(wUg[32 * j:32 * j + 32, at + s_at:at + s_at + CS], Wl[64:96, :])
                    ld(wUg[32 * b:32 * b + 32, at + plus:at + plus + CV], Wh[96:128, :])
                    ld(wUg[32 * a:32 * a + 32, at + minus:at + minus + CV], Wh[96:128, :])
                    for k, name in enumerate(("w2_vs", "w2_vv0", "w2_vv1")):
                        ld(w2col[32 * j:32 * j + 32, k:k + 1], w[name].rearrange("(a o) -> a o", o=1))
                ld(wUs[64:128, 0:CS], Wl[0:64, :])
                ld(wUs[64:128, CS:CS + CV], Wh[0:64, :])
                for k, name in enumerate(("w2_ss", "w2_sv")):
                    ld(w2col[64:128, 3 + k:4 + k], w[name].rearrange("(a o) -> a o", o=1))
                sp.wait_ge(consts_made, 5)
                for k in range(T):
                    sp.dma_start(sums[k].rearrange("(p j) c -> p j c", p=P), init_row).then_inc(tables_stored, 16)
                sp.dma_start(dst_rows[N:ROWS, :], init_row[:, 0, 0:D]).then_inc(tables_stored, 16)
                sp.wait_ge(projection_kept, NT)
                sp.dma_start(src_rows.rearrange("(p j) c -> p j c", p=P), stage[:, :, 0:D]).then_inc(tables_stored, 16)
                sp.dma_start(dst_rows[0:N, :].rearrange("(p j) c -> p j c", p=P), stage[:, :, D:2 * D]).then_inc(tables_stored, 16)
                sp.wait_ge(tables_stored, 16 * (T + 3))
                sp.wait_ge(weights_loaded.sem, weights_loaded.n)

            @block.gpsimd
            def _(pool):
                nc.gpsimd.memset(room[:, w_at:l0_end], 0.0).then_inc(cleared, 1)
                nc.gpsimd.memset(wA, 0.0).then_inc(cleared, 1)
                nc.gpsimd.memset(wB, 0.0).then_inc(cleared, 1)
                nc.gpsimd.memset(ident[:, :], 0.0).then_inc(pool_step, 1)
                nc.gpsimd.memset(before[:, :], 1.0).then_inc(pool_step, 1)
                nc.gpsimd.memset(init_row[:, :, 0:D + H], 0.0).then_inc(consts_made, 1)
                nc.gpsimd.memset(init_row[:, :, D + H:AC], LOW).then_inc(consts_made, 1)
                nc.gpsimd.iota(pcol_i[:, :], pattern=[[0, 1]], base=N, channel_multiplier=1).then_inc(pool_step, 1)
                pool.wait_ge(pool_step, 3)
                nc.gpsimd.tensor_copy(pcol[:, :], pcol_i[:, :]).then_inc(consts_made, 1)
                nc.gpsimd.affine_select(out=ident[:, :], in_=ident[:, :], compare_op=ALU.not_equal, fill=1.0,
                                        base=0, pattern=[[-1, 128]], channel_multiplier=1).then_inc(consts_made, 1)
                nc.gpsimd.affine_select(out=before[:, :], in_=before[:, :], compare_op=ALU.is_gt, fill=0.0,
                                        base=0, pattern=[[-1, P]], channel_multiplier=1).then_inc(consts_made, 1)

            @block.vector
            def _(dve):
                dv = Count(dve_step)
                dve.wait_ge(inputs_loaded, 64)
                norm(dve, dv, xs[:, :, :], hs[:, :, :], D, 1, True, stat, tmp, var_ready, std_ready)
                sn = stage[:, :, 0:CS]
                norm(dve, dv, hs[:, :, 0:CS], sn, CS, 2, False, stat, tmp, var_ready, std_ready)
                row = lambda a, b: gam[0:P, a:b].unsqueeze(1).broadcast_to([P, NT, b - a])
                dv(nc.vector.tensor_tensor(sn, sn, row(0, CS), ALU.mult))
                dv.wait(dve)
                nc.vector.tensor_tensor(nn[:, :, SC:SC + CS], sn, row(CS, 2 * CS), ALU.add).then_inc(nn_ready, 1)
                vec = hs[:, :, CS:D]
                dv(nc.vector.tensor_tensor(tmp[:, :, 0:3 * CV], vec, vec, ALU.mult))
                dv.wait(dve)
                dv(nc.vector.tensor_reduce(stat[:, 2, :], tmp[:, :, 0:3 * CV], AX.X, ALU.add))
                dv.wait(dve)
                nc.vector.tensor_scalar(stat[:, 3, :], stat[:, 2, :], 1.0 / CV, EPS, ALU.mult, ALU.add).then_inc(var_ready, 1)
                dve.wait_ge(std_ready, 3)
                dv(nc.vector.reciprocal(stat[:, 5, :], stat[:, 4, :]))
                dv.wait(dve)
                dv(nc.vector.tensor_tensor(tmp[:, :, 0:3 * CV], vec,
                                           stat[:, 5, :].unsqueeze(2).broadcast_to([P, NT, 3 * CV]), ALU.mult))
                dv.wait(dve)
                for o, i in to_rows(nn, tmp[:, :, 0:3 * CV]):
                    nc.vector.tensor_tensor(o, i, row(2 * CS, 2 * CS + CV), ALU.mult).then_inc(nn_ready, 1)
                dve.wait_ge(weights_loaded.sem, weights_loaded.n)
                sc = []
                mul = lambda ap, f, g=None: sc.append(
                    nc.vector.tensor_scalar(ap, ap, f, g, ALU.mult, ALU.mult) if g is not None
                    else nc.vector.tensor_scalar(ap, ap, f, None, ALU.mult))
                mul(wX0[0:64, :], S3)
                mul(wX4[96:128, :], S3)
                for k, c_at in enumerate((32, 96, 96)):
                    mul(wV[k][c_at:c_at + 32, :], S2)
                mul(wV4[0:96, :], -S2)
                mul(wLr[0:64, :], 0.2)
                mul(wLr[64:128, :], 0.8)
                mul(wUs[64:128, 0:CS], w2col[64:128, 3:4], 0.5)
                mul(wUs[64:128, CS:CS + CV], w2col[64:128, 4:5], 0.5)
                mul(wUg[0:96, 0:96], w2col[0:96, 0:1], 0.5)
                for j, (s_at, plus, minus) in enumerate(((32, 0, 96), (0, 64, 96), (64, 0, 32))):
                    a, b, at = (j + 1) % 3, (j + 2) % 3, U_AT[1 + j]
                    for r, c, n, k, f in ((j, s_at, CS, 1, 0.5 * S3), (b, plus, CV, 2, 0.5 * S2), (a, minus, CV, 2, -0.5 * S2)):
                        mul(wUg[32 * r:32 * r + 32, at + c:at + c + n], w2col[32 * r:32 * r + 32, k:k + 1], f)
                for ins in sc:
                    ins.then_inc(weights_scaled, 1)
                dve.wait_ge(weights_scaled, len(sc))

            @block.scalar
            def _(act):
                for r in (1, 2, 3):
                    root_of(act, r)
                act.wait_ge(weights_loaded.sem, weights_loaded.n)

                def keep_turned(j):
                    b = j % 2
                    act.wait_ge(nodes_turned, 2 * j + 2)
                    if j >= 2:
                        act.wait_ge(projected, j - 1)
                    nc.scalar.activation(nA[b][:, 0:P], ps[:, b, 0:P], ACT.Copy).then_inc(turned_kept, 1)
                    nc.scalar.activation(nB[b][0:32, 0:P], ps[0:32, b, 128:128 + P], ACT.Copy).then_inc(turned_kept, 1)

                keep_turned(0)
                for j in range(NT):
                    b = j % 2
                    if j + 1 < NT:
                        keep_turned(j + 1)
                    act.wait_ge(projected, j + 1)
                    nc.scalar.activation(stage[:, j, :], ps[0:P, 2 + b, 0:2 * D], ACT.Copy).then_inc(projection_kept, 1)

            @block.tensor
            def _(pe):
                pe.wait_ge(consts_made, 5)
                pe.wait_ge(nn_ready, 4)
                pe.wait_ge(weights_loaded.sem, weights_loaded.n)

                def turn(j):
                    b = j % 2
                    if j >= 2:
                        pe.wait_ge(turned_kept, 2 * (j - 1))
                    nc.tensor.transpose(ps[:, b, 0:P], nn[:, j, 0:128], ident[0:P, 0:P]).then_inc(nodes_turned, 1)
                    nc.tensor.transpose(ps[0:32, b, 128:128 + P], nn[:, j, 128:D], ident[0:P, 0:P]).then_inc(nodes_turned, 1)

                turn(0)
                for j in range(NT):
                    b = j % 2
                    if j + 1 < NT:
                        turn(j + 1)
                    pe.wait_ge(turned_kept, 2 * j + 2)
                    if j >= 2:
                        pe.wait_ge(projection_kept, j - 1)
                    nc.tensor.matmul(ps[0:P, 2 + b, 0:2 * D], nA[b][:, 0:P], wA, start=True, stop=False)
                    nc.tensor.matmul(ps[0:P, 2 + b, 0:2 * D], nB[b][0:32, 0:P], wB[0:32, :],
                                     start=False, stop=True).then_inc(projected, 1)

        def steps(eng, body):
            for j in range(3):
                body(Group(0, j))
            with eng.Fori(0, (G - 5) // 2) as i:
                for u in range(2):
                    body(Group(i, u + 3))
            for j in range(G - 2, G + 1):
                body(Group(0, j))

        def halves(j):
            return j.exists(), j.back(1).exists()

        with nc.Block() as block:
            @block.sync
            def _(sp):
                def load_edges(g):
                    b, eds = g.b, edges_loaded.sems[g.b]
                    wait(sp, outer_built, g.back(2))
                    settle(sp, 1)
                    wait(sp, copies_made, g.back(2))
                    wait(sp, nodes_gathered, g.back(2))
                    settle(sp, 1)
                    last = isinstance(g.i, int) and g.off == G - 1
                    n = LEFT if last else T
                    if last:
                        sp.dma_start(e_dst[b][:, n:T], pad_dst[:, n:T]).then_inc(pad_copied, 16)
                        sp.wait_ge(pad_copied, 16)
                    sp.dma_start(e_src[b][:, 0:n], src_v[:, bass.ds(g.number(T), n)], allow_slow_non_contiguous=True).then_inc(eds, 16)
                    sp.dma_start(e_dst[b][:, 0:n], dst_v[:, bass.ds(g.number(T), n)], allow_slow_non_contiguous=True).then_inc(eds, 16)
                    sp.dma_start(e_rbf[b][:, 0:n * NB], rbf_v[:, bass.ds(g.number(T * NB), n * NB)]).then_inc(eds, 16)
                    sp.dma_start(e_y[b][:, 0:n * 4], y_v[:, bass.ds(g.number(T * 4), n * 4)]).then_inc(eds, 16)

                sp.wait_ge(edge_places_cleared, 4)
                for g in range(4):
                    load_edges(Group(0, g))
                with sp.Fori(0, (G - 5) // 2) as i:
                    for u in range(2):
                        load_edges(Group(i, u + 4))
                load_edges(Group(0, G - 1))

            @block.gpsimd
            def _(pool):
                nc.gpsimd.memset(outer[0], 0.0).then_inc(edge_places_cleared, 1)
                nc.gpsimd.memset(outer[1], 0.0).then_inc(edge_places_cleared, 1)
                nc.gpsimd.memset(sg, 0.0).then_inc(edge_places_cleared, 1)
                nc.gpsimd.memset(pad_dst, N).then_inc(edge_places_cleared, 1)
                pool.wait_ge(edge_places_cleared, 4)

                def gather(g, first, last):
                    b = g.b
                    if first == 0:
                        wait(pool, edges_loaded, g)
                        wait(pool, feat_added, g.back(2))
                        settle(pool, 0)
                    for t in range(first, last):
                        nc.gpsimd.indirect_dma_start(g_src[b][:, t * D:(t + 1) * D], None, src_rows,
                                                     bass.IndirectOffsetOnAxis(ap=e_src[b][:, t:t + 1], axis=0)
                                                     ).then_inc(nodes_gathered.sems[b], 16)
                        nc.gpsimd.indirect_dma_start(g_dst[b][:, t * D:(t + 1) * D], None, dst_rows,
                                                     bass.IndirectOffsetOnAxis(ap=e_dst[b][:, t:t + 1], axis=0)
                                                     ).then_inc(nodes_gathered.sems[b], 16)

                def radial(g):
                    b = g.b
                    wait(pool, outer_turned, g.back(2))
                    wait(pool, edges_loaded, g)
                    y = e_y[b].rearrange("p (t c) -> p t c", c=4)
                    for c in range(4):
                        nc.gpsimd.tensor_tensor(outer[b][:, :, NB * c:NB * c + NB],
                                                e_rbf[b].rearrange("p (t r) -> p t r", r=NB),
                                                y[:, :, c:c + 1].broadcast_to([P, T, NB]),
                                                ALU.mult).then_inc(outer_built.sem, 1)

                def read_tables(g):
                    wait(pool, copies_made, g)
                    wait(pool, rows_scattered, g.back(1))
                    settle(pool, 0)
                    for t in range(T):
                        nc.gpsimd.indirect_dma_start(rows[g.b][:, t, :], None, sums[t],
                                                     bass.IndirectOffsetOnAxis(ap=dst_kept[g.b][:, t:t + 1], axis=0)
                                                     ).then_inc(rows_gathered.sems[g.b], 16)

                def write_tables(g):
                    b, rw = g.b, rows[g.b]
                    wait(pool, rows_gathered, g)
                    wait(pool, exp_made, g)
                    for a, n in HEADS + ((D, 1),):
                        v = rw[:, :, a:a + H * n].rearrange("p t (h a) -> p t h a", h=H)
                        nc.gpsimd.tensor_tensor(v, v, scale[:, 0, :, :].unsqueeze(3).broadcast_to([P, T, H, n]),
                                                ALU.mult).then_inc(rows_scaled.sem, 1)
                    wait(pool, rows_added, g)
                    wait(pool, firsts_made, g)
                    settle(pool, 0)
                    for t in range(T):
                        nc.gpsimd.indirect_dma_start(sums[t], bass.IndirectOffsetOnAxis(ap=first[b][:, t:t + 1], axis=0),
                                                     rw[:, t, :], None, bounds_check=N - 1, oob_is_err=False
                                                     ).then_inc(rows_scattered.sems[b], 16)

                def body(m):
                    n = m.ahead(3)
                    if n.exists():
                        gather(n, 0, 1)
                    read_tables(m)
                    if n.exists():
                        gather(n, 1, T)
                        radial(n)
                    write_tables(m)

                for g in range(3):
                    gather(Group(0, g), 0, T)
                    radial(Group(0, g))
                body(Group(0, 0))
                with pool.Fori(0, (G - 5) // 2) as i:
                    for u in range(2):
                        body(Group(i, u + 1))
                for g in range(G - 4, G):
                    body(Group(0, g))
                wait(pool, rows_scattered, Group(0, G - 2))
                wait(pool, rows_scattered, Group(0, G - 1))

            @block.vector
            def _(dve):
                def take(j):
                    b = j.b
                    wait(dve, edges_loaded, j)
                    wait(dve, rows_gathered, j.back(2))
                    wait(dve, d_made, j.back(1))
                    wait(dve, firsts_made, j.back(1))
                    nc.vector.tensor_copy(dst_f, e_dst[b]).then_inc(copies_made.sem, 1)
                    nc.vector.tensor_copy(dst_kept[b], e_dst[b]).then_inc(copies_made.sem, 1)

                def features(j):
                    b = j.b
                    wait(dve, comb, j.back(2))
                    wait(dve, t0_made, j.back(2))
                    nc.vector.tensor_copy(y_kept[b], e_y[b]).then_inc(copies_made.sem, 1)
                    wait(dve, nodes_gathered, j)
                    wait(dve, f_turned, j.back(1))
                    nc.vector.tensor_tensor(feat[:, :, 0:D], g_src[b].rearrange("p (t c) -> p t c", t=T),
                                            g_dst[b].rearrange("p (t c) -> p t c", t=T),
                                            ALU.add).then_inc(feat_added.sem, 1)

                def same_destination(j):
                    b = j.b
                    wait(dve, d_made, j)
                    wait(dve, sm_made, j.back(2))
                    col = dst_f.unsqueeze(2).broadcast_to([P, T, P])
                    nc.vector.tensor_tensor(same[b], ps[0:P, D_BANK, 0:W].rearrange("p (t e) -> p t e", t=T), col,
                                            ALU.is_equal).then_inc(same_made.sem, 1)

                def masks(j):
                    b = j.b
                    wait(dve, early_counted, j.back(1))
                    wait(dve, same_made, j)
                    nc.vector.tensor_tensor(early, same[b], before[:, :].unsqueeze(1).broadcast_to([P, T, P]),
                                            ALU.mult).then_inc(masks_made.sem, 1)
                    wait(dve, a_masked, j.back(2))
                    nc.vector.tensor_scalar(apart[b], same[b], -LOW, LOW, ALU.mult, ALU.add).then_inc(masks_made.sem, 1)

                def firsts(j):
                    wait(dve, masks_made, j, 0)
                    nc.vector.tensor_reduce(cnt, early, AX.X, ALU.add).then_inc(early_counted.sem, 1)
                    nc.vector.tensor_scalar(away, dst_f, -1.0, pcol[:, 0:1], ALU.mult, ALU.add).then_inc(firsts_made.sem, 1)
                    wait(dve, early_counted, j)
                    nc.vector.tensor_scalar(cnt, cnt, 0.5, None, ALU.is_gt).then_inc(firsts_made.sem, 1)
                    wait(dve, firsts_made, j, 1)
                    nc.vector.tensor_tensor(moved, away, cnt, ALU.mult).then_inc(firsts_made.sem, 1)

                def table_rows(j):
                    wait(dve, firsts_made, j, 2)
                    wait(dve, rows_scattered, j.back(2))
                    nc.vector.tensor_tensor(first[j.b], moved, dst_f, ALU.add).then_inc(firsts_made.sem, 1)

                def only_same(g, h):
                    wait(dve, a_made, g, h)
                    wait(dve, masks_made, g)
                    if h >= 2:
                        wait(dve, a_max, g, h - 2)
                    else:
                        wait(dve, a_max, g.back(1))
                    nc.vector.tensor_tensor(masked[h % 2], ps[0:P, 6 + h % 2, 0:W].rearrange("p (t e) -> p t e", t=T),
                                            apart[g.b], ALU.add).then_inc(a_masked.sem, 1)

                def largest(g, h):
                    wait(dve, a_masked, g, h)
                    nc.vector.tensor_reduce(gmax[:, :, h], masked[h % 2], AX.X, ALU.max).then_inc(a_max.sem, 1)

                def combine(g, t, c):
                    if c == 0:
                        wait(dve, u_made, g, t)
                        wait(dve, t0_made, g, 4 * t + 3)
                    else:
                        wait(dve, comb, g, SUM_NO[t, c - 1])
                    if c == 1:
                        wait(dve, zeroed, g)
                    at, n = RUNS[c]
                    nc.vector.scalar_tensor_tensor(
                        ht[:, t, at:at + n], ps[0:P, U_BANK[t], U_AT[c]:U_AT[c] + n],
                        y_kept[g.b][:, 4 * t + c:4 * t + c + 1], ht[:, t, at:at + n],
                        ALU.mult, ALU.add).then_inc(comb.sem, 1)

                def product(j, k):
                    wait(dve, l_made, j, k)
                    f = (0, 0, 1, 2, 3)[k]
                    wait(dve, f_kept, j, f)
                    nc.vector.tensor_tensor(prod[k], ps[:, L_BANK[k], 0:W], fT[f], ALU.mult).then_inc(prod_made.sem, 1)

                def new_maxima(g, step):
                    old_max = rows[g.b][:, :, D + H:AC]
                    if step == 0:
                        wait(dve, rows_gathered, g)
                        wait(dve, a_max, g)
                        wait(dve, rows_added, g.back(1))
                        nc.vector.tensor_tensor(newmax, gmax, old_max, ALU.max).then_inc(shift_made.sem, 1)
                    elif step == 1:
                        wait(dve, shift_made, g, 0)
                        wait(dve, exp_made, g.back(1))
                        nc.vector.tensor_tensor(shift[:, 0], old_max, newmax, ALU.subtract).then_inc(shift_made.sem, 1)
                    else:
                        wait(dve, lg_kept, g)
                        nc.vector.tensor_tensor(shift[:, 1], logit, newmax, ALU.subtract).then_inc(shift_made.sem, 1)

                def weigh(g):
                    wait(dve, folded, g)
                    wait(dve, exp_made, g)
                    wait(dve, sm_made, g.back(1))
                    ex = scale[:, 1, :, :]
                    for a, n in HEADS:
                        nc.vector.tensor_tensor(
                            vx[:, :, a:a + H * n].rearrange("p t (h a) -> p t h a", h=H),
                            ht[:, :, a:a + H * n].rearrange("p t (h a) -> p t h a", h=H),
                            ex.unsqueeze(3).broadcast_to([P, T, H, n]), ALU.mult).then_inc(vx_made.sem, 1)
                    nc.vector.tensor_copy(vx[:, :, D:D + H], ex).then_inc(vx_made.sem, 1)

                def add_rows(g):
                    wait(dve, rows_scaled, g)
                    for k in range(2):
                        wait(dve, sm_made, g, k)
                        r = rows[g.b][:, 2 * k:2 * k + 2, 0:D + H]
                        nc.vector.tensor_tensor(r, r, ps[0:P, 6 + k, 0:2 * (D + H)].rearrange("p (t c) -> p t c", t=2),
                                                ALU.add).then_inc(rows_added.sem, 1)
                    wait(dve, shift_made, g)
                    nc.vector.tensor_copy(rows[g.b][:, :, D + H:AC], newmax).then_inc(rows_added.sem, 1)

                def body(j):
                    new, old = halves(j)
                    g, n = j.back(1), j.ahead(1)
                    if old:
                        only_same(g, 0)
                        only_same(g, 1)
                        largest(g, 0)
                        only_same(g, 2)
                        largest(g, 1)
                        only_same(g, 3)
                        wait(dve, vx_made, g.back(1))
                        nc.vector.memset(ht[:, :, V0:V0 + 2 * CV], 0.0).then_inc(zeroed.sem, 1)
                        largest(g, 2)
                        largest(g, 3)
                    if new:
                        wait(dve, x_made, j.back(1))
                        wait(dve, v_made, j.back(1))
                        for k in range(3):
                            product(j, k)
                    if old:
                        for t, c in SUMS[0:8]:
                            combine(g, t, c)
                    if new:
                        table_rows(j)
                        product(j, 3)
                        product(j, 4)
                    if n.exists():
                        take(n)
                    if old:
                        for t, c in SUMS[8:13]:
                            combine(g, t, c)
                        for k in range(3):
                            new_maxima(g, k)
                            combine(g, *SUMS[13 + k])
                        wait(dve, comb, g)
                        v = ht[:, :, V0:V0 + 2 * CV]
                        nc.vector.tensor_tensor(v, v, ht[:, :, D:HW], ALU.add).then_inc(folded.sem, 1)
                    if n.exists():
                        features(n)
                    if old:
                        weigh(g)
                    if new:
                        wait(dve, tg_made, j)
                        wait(dve, v_made, j)
                        wait(dve, u_made, j.back(1))
                        nc.vector.scalar_tensor_tensor(gv[:, :], tg[:, :], 1.0, ps[0:96, 5, 0:W],
                                                       ALU.add, ALU.mult).then_inc(gv_made.sem, 1)
                    if old:
                        add_rows(g)
                    if n.exists():
                        same_destination(n)
                        masks(n)
                    if n.exists():
                        firsts(n)

                take(Group(0, 0))
                features(Group(0, 0))
                same_destination(Group(0, 0))
                masks(Group(0, 0))
                firsts(Group(0, 0))
                steps(dve, body)

            @block.scalar
            def _(act):
                def keep(out_, in_, ev):
                    nc.scalar.activation(out_, in_, ACT.Copy).then_inc(ev.sem, 1)

                def double(j):
                    wait(act, feat_added, j)
                    wait(act, f_turned, j.back(1))
                    keep(feat[:, :, D:D + 64], feat[:, :, V0:V0 + 64], feat_dup)
                    keep(feat[:, :, D + 64:D + 96], feat[:, :, V2:V2 + 32], feat_dup)

                act.wait_ge(edge_places_cleared, 4)

                def body(j):
                    new, old = halves(j)
                    g = j.back(1)
                    if new:
                        wait(act, outer_turned, j)
                        wait(act, l_made, j.back(1))
                        keep(oT, ps[:, O_BANK, 0:W], outer_kept)
                        for k in range(4):
                            wait(act, f_turned, j, k)
                            wait(act, prod_made, j.back(1))
                            keep(fT[k], ps[:, F_BANK[k], 0:W], f_kept)
                    if old:
                        wait(act, vx_made, g.back(1))
                        wait(act, us_made, g)
                        for t in range(T):
                            for c, to, at, n in ((0, SC, 0, CS), (1, D, CS, CV), (2, D + CV, CS, CV), (3, V2, CS, CV)):
                                nc.scalar.activation(ht[:, t, to:to + n], ps[0:P, 2, t * 96 + at:t * 96 + at + n], ACT.Copy,
                                                     scale=y_kept[g.b][:, 4 * t + c:4 * t + c + 1]).then_inc(t0_made.sem, 1)
                    if new:
                        wait(act, x_made, j)
                        wait(act, lg_made, j.back(1))
                        wait(act, g_made, j.back(1))
                        wait(act, sg_made, j.back(1))
                        keep(xv[64:128, :], ps[64:128, 2, 0:W], xv_kept)
                    if old:
                        wait(act, shift_made, g)
                        wait(act, rows_scaled, g.back(1))
                        nc.scalar.activation(scale, shift, ACT.Exp).then_inc(exp_made.sem, 1)
                    if new:
                        keep(rl[0:64, :], ps[0:64, 2, 0:W], xv_kept)
                        nc.scalar.activation(rl[64:128, :], ps[0:64, 2, 0:W], ACT.Relu).then_inc(xv_kept.sem, 1)
                        wait(act, xv_kept, j, 0)
                        wait(act, us_made, j.back(1))
                        nc.scalar.activation(sg[64:128, :], xv[64:128, :], ACT.Tanh, scale=0.5).then_inc(sg_made.sem, 1)
                        wait(act, g_made, j)
                        wait(act, gv_made, j.back(1))
                        nc.scalar.activation(tg[:, :], ps[0:96, 6, 0:W], ACT.Tanh, scale=0.5).then_inc(tg_made.sem, 1)
                        wait(act, lg_made, j)
                        wait(act, shift_made, j.back(1))
                        wait(act, a_made, j.back(1))
                        keep(logit, ps[0:P, 7, 0:T * H].rearrange("p (t h) -> p t h", t=T), lg_kept)
                        wait(act, sg_made, j, 0)
                        nc.scalar.activation(sg[64:128, :], sg[64:128, :], ACT.Copy, bias=1.0).then_inc(sg_made.sem, 1)
                    if j.ahead(1).exists():
                        double(j.ahead(1))

                double(Group(0, 0))
                steps(act, body)

            @block.tensor
            def _(pe):
                tr = nc.tensor.transpose
                mm = nc.tensor.matmul
                idP = ident[0:P, 0:P]

                def destinations(j):
                    wait(pe, copies_made, j, 0)
                    wait(pe, prod_made, j.back(1), 1)
                    for t in range(T):
                        ins = tr(ps[0:P, D_BANK, t * P:(t + 1) * P],
                                 dst_f[:, t:t + 1].broadcast_to([P, P]), idP)
                    ins.then_inc(d_made.sem, 1)

                def over_edges(g, h):
                    bank = 6 + h % 2
                    if h >= 2:
                        wait(pe, a_masked, g, h - 2)
                    else:
                        if h == 0:
                            wait(pe, lg_kept, g)
                        wait(pe, rows_added, g.back(1), h)
                    for t in range(T):
                        ins = tr(ps[0:P, bank, t * P:(t + 1) * P], logit[:, t, h:h + 1].broadcast_to([P, P]), idP)
                    ins.then_inc(a_made.sem, 1)

                def weights_of(j, k):
                    if k == 0:
                        wait(pe, gv_made, j.back(1))
                    elif k < 3:
                        wait(pe, f_kept, j, 1 + k)
                    else:
                        wait(pe, prod_made, j, (0, 2)[k - 3])
                    mm(ps[:, L_BANK[k], 0:W], wL[k], oT, start=True, stop=True).then_inc(l_made.sem, 1)

                def scalars_terms(g):
                    wait(pe, sg_made, g)
                    for t in range(T):
                        ins = mm(ps[0:P, 2, t * 96:(t + 1) * 96], sg[:, t * P:(t + 1) * P], wUs, start=True, stop=True)
                    ins.then_inc(us_made.sem, 1)

                def vectors_terms(g, t):
                    if t == 0:
                        wait(pe, gv_made, g)
                        wait(pe, comb, g.back(1))
                    if t >= 2:
                        wait(pe, comb, g, SUM_NO[t - 2, 3])
                    mm(ps[0:P, U_BANK[t], 0:UW], gv[:, t * P:(t + 1) * P], wUg[0:96, :], start=True, stop=True).then_inc(u_made.sem, 1)

                def body(j):
                    new, old = halves(j)
                    g = j.back(1)
                    if new:
                        wait(pe, outer_built, j)
                        wait(pe, prod_made, j.back(1))
                        for t in range(T):
                            ins = tr(ps[:, O_BANK, t * P:(t + 1) * P], outer[j.b][:, t, :], idP)
                        ins.then_inc(outer_turned.sem, 1)
                    if old:
                        over_edges(g, 0)
                    if new:
                        wait(pe, feat_added, j)
                        for k, a in enumerate((0, 32, 64, 128)):
                            if k == 1 and old:
                                over_edges(g, 1)
                            if k == 2 and old:
                                scalars_terms(g)
                            if k == 0:
                                wait(pe, same_made, j)
                            elif k == 1:
                                wait(pe, outer_kept, j)
                            else:
                                wait(pe, f_kept, j, k - 2)
                            if k == 2:
                                wait(pe, feat_dup, j)
                            for t in range(T):
                                ins = tr(ps[:, F_BANK[k], t * P:(t + 1) * P], feat[:, t, a:a + 128], idP)
                            ins.then_inc(f_turned.sem, 1)
                    elif old:
                        over_edges(g, 1)
                        scalars_terms(g)
                    if old:
                        over_edges(g, 2)
                    if new:
                        wait(pe, outer_kept, j)
                        weights_of(j, 0)
                    if old:
                        over_edges(g, 3)
                    if new:
                        weights_of(j, 1)
                        weights_of(j, 2)
                    if old:
                        vectors_terms(g, 0)
                        vectors_terms(g, 1)
                    if new:
                        weights_of(j, 3)
                        weights_of(j, 4)
                    if old:
                        vectors_terms(g, 2)
                        vectors_terms(g, 3)
                    if j.ahead(1).exists():
                        destinations(j.ahead(1))
                    if new:
                        wait(pe, t0_made, j.back(1))
                        wait(pe, prod_made, j)
                        mm(ps[:, 2, 0:W], wX0, prod[0], start=True, stop=False)
                        mm(ps[:, 2, 0:W], wX4, prod[4], start=False, stop=True).then_inc(x_made.sem, 1)
                        mm(ps[0:96, 5, 0:W], wV4, prod[4], start=True, stop=True)
                        for k in range(3):
                            ins = mm(ps[32 * k:32 * k + 32, 5, 0:W], wV[k], prod[1 + k], start=False, stop=True,
                                     skip_group_check=True)
                        ins.then_inc(v_made.sem, 1)
                        wait(pe, xv_kept, j, 0)
                        wait(pe, a_masked, j.back(1))
                        mm(ps[0:96, 6, 0:W], wG[64:128, :], xv[64:128, :], start=True, stop=True).then_inc(g_made.sem, 1)
                        wait(pe, xv_kept, j)
                        for t in range(T):
                            ins = mm(ps[0:P, 7, t * H:(t + 1) * H], rl[:, t * P:(t + 1) * P], wLr, start=True, stop=True)
                        ins.then_inc(lg_made.sem, 1)
                    if old:
                        wait(pe, vx_made, g)
                        for k in range(2):
                            if new:
                                wait(pe, *((tg_made, j), (lg_kept, j))[k])
                            else:
                                wait(pe, a_masked, g, 2 + k)
                            for t in range(2):
                                ins = mm(ps[0:P, 6 + k, t * (D + H):(t + 1) * (D + H)], same[g.b][:, 2 * k + t, :],
                                         vx[:, 2 * k + t, :], start=True, stop=True)
                            ins.then_inc(sm_made.sem, 1)

                pe.wait_ge(edge_places_cleared, 4)
                destinations(Group(0, 0))
                steps(pe, body)

        cut["at"] = 0
        tabs = [part(NT * AC)[0:P].rearrange("p (j c) -> p j c", j=NT) for _ in range(T)]
        top = part(NT * H)[0:P].rearrange("p (j h) -> p j h", j=NT)
        nn3 = part(NT * D)[0:P].rearrange("p (j c) -> p j c", j=NT)
        stage3 = part(4 * PW)[0:P].rearrange("p (j c) -> p j c", j=4)
        aA, aB = [part(128) for _ in range(2)], [part(128) for _ in range(2)]
        w3_at = cut["at"]
        wPs, wPv = part(D), part(D)
        wMA, wMB = part(PW), part(PW)
        w3_end = cut["at"]
        zeros = part(26 * D)[0:P]
        total = tabs[0][:, 0:NT, :]
        scratch = tabs[1][:, 0:NT, 0:D]
        weights3_loaded = Count(sem("weights3_loaded"), 16)
        cleared3, scaled3 = sem("cleared3"), sem("scaled3")
        tabs_loaded = sem("tabs_loaded")
        dve3, act3, pool3 = sem("dve3"), sem("act3"), sem("pool3")
        tab_shift, tab_exp, tab_scaled = sem("tab_shift"), sem("tab_exp"), sem("tab_scaled")
        agg_ready, agg_turned, agg_kept = sem("agg_ready"), sem("agg_turned"), sem("agg_kept")
        out_made, out_kept = sem("out_made"), sem("out_kept")
        h1_ready, h1_turned, h1_kept = sem("h1_ready"), sem("h1_turned"), sem("h1_kept")
        proj_made, proj_kept, proj_stored = sem("proj_made"), sem("proj_kept"), [sem(f"proj_stored{k}") for k in range(4)]
        aggs_cleared = sem("aggs_cleared")
        stat_at = cut["at"]
        stat3 = part(8 * NT)[0:P].rearrange("p (k j) -> p k j", k=8)
        var3, std3 = sem("var3"), sem("std3")

        P_ONE, P_DIST, P_DIR, P_VEC = 0, D, 2 * D, 2 * D + 3 * CS

        def turn(pe, j, source, turned, kept):
            b = j % 2
            if j >= 2:
                pe.wait_ge(kept, 2 * (j - 1))
            nc.tensor.transpose(ps[:, b, 0:P], source[:, j, 0:128], ident[0:P, 0:P]).then_inc(turned, 1)
            nc.tensor.transpose(ps[0:32, b, 128:128 + P], source[:, j, 128:D], ident[0:P, 0:P]).then_inc(turned, 1)

        def keep_turned(act, j, turned, kept, used):
            b = j % 2
            act.wait_ge(turned, 2 * j + 2)
            if j >= 2:
                act.wait_ge(used, j - 1)
            nc.scalar.activation(aA[b][:, 0:P], ps[:, b, 0:P], ACT.Copy).then_inc(kept, 1)
            nc.scalar.activation(aB[b][0:32, 0:P], ps[0:32, b, 128:128 + P], ACT.Copy).then_inc(kept, 1)

        with nc.Block() as block:
            @block.sync
            def _(sp):
                for k in range(T):
                    sp.dma_start(tabs[k], sums[k][0:N, :].rearrange("(p j) c -> p j c", p=P)).then_inc(tabs_loaded, 16)
                sp.wait_ge(cleared3, 2)
                ld = lambda a, b: weights3_loaded(sp.dma_start(a, b, allow_slow_non_contiguous=True))
                ld(wPs[SC:SC + CS, 0:CS], w["Wps"])
                for k, (t, r) in enumerate(((wPs, V0), (wPs, V1), (wPv, 0))):
                    ld(t[r:r + CV, CS + k * CV:CS + (k + 1) * CV], w["Wpv"])
                m = {n: w[n].rearrange("u o w -> (u o) w") for n in ("wm000", "wm011", "wm101", "wm110")}
                ld(wMA[SC:SC + CS, P_ONE:P_ONE + CS], w["lm0"])
                ld(wMA[SC:SC + CS, P_DIST:P_DIST + CS], m["wm000"])
                ld(wMA[SC:SC + CS, P_VEC:P_VEC + CV], m["wm011"])
                for k, (t, r) in enumerate(((wMA, V0), (wMA, V1), (wMB, 0))):
                    ld(t[r:r + CV, P_ONE + CS + k * CV:P_ONE + CS + (k + 1) * CV], w["lm1"])
                    ld(t[r:r + CV, P_DIST + CS + k * CV:P_DIST + CS + (k + 1) * CV], m["wm101"])
                    ld(t[r:r + CV, P_DIR + k * CS:P_DIR + (k + 1) * CS], m["wm110"])
                for k in range(T):
                    sp.dma_start(aggs[k].rearrange("(p j) c -> p (j c)", p=P), zeros).then_inc(aggs_cleared, 16)
                rows_v = proj_rows.rearrange("(p j) c -> p j c", p=P)
                for j in range(NT):
                    sp.wait_ge(proj_kept, 2 * j + 2)
                    sp.dma_start(rows_v[:, j, :], stage3[:, j % 4, :]).then_inc(proj_stored[j % 4], 16)
                for k in range(4):
                    sp.wait_ge(proj_stored[k], 16 * len(range(k, NT, 4)))
                sp.wait_ge(aggs_cleared, 16 * T)
                sp.wait_ge(weights3_loaded.sem, weights3_loaded.n)

            @block.gpsimd
            def _(pool):
                nc.gpsimd.memset(room[:, w3_at:w3_end], 0.0).then_inc(cleared3, 1)
                nc.gpsimd.memset(zeros, 0.0).then_inc(cleared3, 1)

            @block.vector
            def _(dve):
                dv = Count(dve3)
                dve.wait_ge(tabs_loaded, 16 * T)
                mx = [tabs[k][:, 0:NT, D + H:AC] for k in range(T)]
                dv(nc.vector.tensor_tensor(top, mx[0], mx[1], ALU.max))
                for k in (2, 3):
                    dv.wait(dve)
                    dv(nc.vector.tensor_tensor(top, top, mx[k], ALU.max))
                dv.wait(dve)
                for k in range(T):
                    nc.vector.tensor_tensor(mx[k], mx[k], top, ALU.subtract).then_inc(tab_shift, 1)
                dve.wait_ge(tab_exp, T)
                for k in range(T):
                    for h in range(H):
                        f = tabs[k][:, 0:NT, D + H + h:D + H + h + 1]
                        for a, n in HEADS + ((D, 1),):
                            v = tabs[k][:, 0:NT, a + h * n:a + (h + 1) * n]
                            dv(nc.vector.tensor_tensor(v, v, f.broadcast_to([P, NT, n]), ALU.mult))
                dv.wait(dve)
                for k in range(1, T):
                    dv(nc.vector.tensor_tensor(total[:, :, 0:D + H], total[:, :, 0:D + H], tabs[k][:, 0:NT, 0:D + H], ALU.add))
                    dv.wait(dve)
                den = total[:, :, D:D + H]
                dv(nc.vector.tensor_scalar(den, den, 1e-16, None, ALU.add))
                dv.wait(dve)
                dv(nc.vector.reciprocal(top, den))
                dv.wait(dve)
                for h in range(H):
                    f = top[:, :, h:h + 1]
                    for a, n in HEADS:
                        v = total[:, :, a + h * n:a + (h + 1) * n]
                        dv(nc.vector.tensor_tensor(v, v, f.broadcast_to([P, NT, n]), ALU.mult))
                dv.wait(dve)
                nc.vector.tensor_copy(nn3, total[:, :, 0:D]).then_inc(agg_ready, 1)
                dv(nc.vector.tensor_tensor(xs[:, :, :], xs[:, :, :], hs[:, :, :], ALU.add))
                dv.wait(dve)
                for j in range(NT):
                    dve.wait_ge(out_made, j + 1)
                    b = 4 + j % 2
                    v = xs[:, j, CS:D].rearrange("p (c k) -> p k c", k=3)
                    nc.vector.tensor_tensor(xs[:, j, 0:CS], xs[:, j, 0:CS], ps[0:P, b, 0:CS], ALU.add).then_inc(out_kept, 1)
                    nc.vector.tensor_tensor(v, v, ps[0:P, b, CS:D].rearrange("p (k c) -> p k c", k=3),
                                            ALU.add).then_inc(out_kept, 1)
                dve.wait_ge(out_kept, 2 * NT)
                dve.wait_ge(agg_turned, 2 * NT)
                norm(dve, dv, xs[:, :, :], hs[:, :, :], D, 1, True, stat3, scratch, var3, std3)
                nc.vector.tensor_copy(nn3[:, :, SC:SC + CS], hs[:, :, 0:CS]).then_inc(h1_ready, 1)
                for o, i in to_rows(nn3, hs[:, :, CS:D]):
                    nc.vector.tensor_copy(o, i).then_inc(h1_ready, 1)
                dve.wait_ge(weights3_loaded.sem, weights3_loaded.n)
                nc.vector.tensor_scalar(wMA[0:64, P_ONE:P_ONE + D], wMA[0:64, P_ONE:P_ONE + D], 32.0 ** -0.5, None, ALU.mult).then_inc(scaled3, 1)
                nc.vector.tensor_scalar(wMA[64:128, P_ONE:P_ONE + D], wMA[64:128, P_ONE:P_ONE + D], 0.125, None, ALU.mult).then_inc(scaled3, 1)
                nc.vector.tensor_scalar(wMB[0:32, P_ONE:P_ONE + D], wMB[0:32, P_ONE:P_ONE + D], 32.0 ** -0.5, None, ALU.mult).then_inc(scaled3, 1)
                for t, n in ((wMA, 128), (wMB, 32)):
                    for a, b, f in ((P_DIST, P_DIR, R96), (P_DIR, P_VEC, R96 * S3), (P_VEC, PW, R96)):
                        nc.vector.tensor_scalar(t[0:n, a:b], t[0:n, a:b], f, None, ALU.mult).then_inc(scaled3, 1)

            @block.scalar
            def _(act):
                act.wait_ge(tab_shift, T)
                for k in range(T):
                    m = tabs[k][:, 0:NT, D + H:AC]
                    nc.scalar.activation(m, m, ACT.Exp).then_inc(tab_exp, 1)
                for j in range(NT):
                    keep_turned(act, j, agg_turned, agg_kept, out_made)
                act.wait_ge(out_made, NT)
                act.wait_ge(var3, 1)
                nc.scalar.activation(stat3[:, 4, :], stat3[:, 3, :], ACT.Sqrt).then_inc(std3, 1)
                keep_turned(act, 0, h1_turned, h1_kept, proj_made)
                for j in range(NT):
                    b = j % 2
                    if j + 1 < NT:
                        keep_turned(act, j + 1, h1_turned, h1_kept, proj_made)
                    act.wait_ge(proj_made, j + 1)
                    if j >= 4:
                        act.wait_ge(proj_stored[j % 4], 16 * (j // 4))
                    nc.scalar.activation(stage3[:, j % 4, 0:320], ps[0:P, 4 + 2 * b, 0:320], ACT.Copy).then_inc(proj_kept, 1)
                    nc.scalar.activation(stage3[:, j % 4, 320:PW], ps[0:P, 5 + 2 * b, 0:PW - 320], ACT.Copy).then_inc(proj_kept, 1)

            @block.tensor
            def _(pe):
                pe.wait_ge(agg_ready, 1)
                pe.wait_ge(weights3_loaded.sem, weights3_loaded.n)
                turn(pe, 0, nn3, agg_turned, agg_kept)
                for j in range(NT):
                    if j + 1 < NT:
                        turn(pe, j + 1, nn3, agg_turned, agg_kept)
                    pe.wait_ge(agg_kept, 2 * j + 2)
                    if j >= 2:
                        pe.wait_ge(out_kept, 2 * (j - 1))
                    b = j % 2
                    o = ps[0:P, 4 + b, 0:D]
                    nc.tensor.matmul(o, aA[b][:, 0:P], wPs, start=True, stop=False)
                    nc.tensor.matmul(o, aB[b][0:32, 0:P], wPv[0:32, :], start=False, stop=True).then_inc(out_made, 1)
                pe.wait_ge(h1_ready, 4)
                pe.wait_ge(scaled3, 9)
                pe.wait_ge(out_kept, 2 * NT)
                pe.wait_ge(agg_kept, 2 * NT)
                turn(pe, 0, nn3, h1_turned, h1_kept)
                for j in range(NT):
                    if j + 1 < NT:
                        turn(pe, j + 1, nn3, h1_turned, h1_kept)
                    pe.wait_ge(h1_kept, 2 * j + 2)
                    if j >= 2:
                        pe.wait_ge(proj_kept, 2 * (j - 1))
                    b = j % 2
                    for k, (a, e) in enumerate(((0, 320), (320, PW))):
                        o = ps[0:P, 4 + 2 * b + k, 0:e - a]
                        nc.tensor.matmul(o, aA[b][:, 0:P], wMA[:, a:e], start=True, stop=False)
                        last = nc.tensor.matmul(o, aB[b][0:32, 0:P], wMB[0:32, a:e], start=False, stop=True)
                    last.then_inc(proj_made, 1)

        cut["at"] = 0
        m_src = [part(T, I32)[0:P] for _ in range(2)]
        m_first = [part(T, I32)[0:P] for _ in range(2)]
        m_early = part(W)[0:P].rearrange("p (t e) -> p t e", t=T)
        m_cnt, m_away, m_moved = part(T)[0:P], part(T)[0:P], part(T)[0:P]
        m_dst = [part(T, I32)[0:P] for _ in range(2)]
        m_y = [part(T * 4)[0:P] for _ in range(2)]
        m_src_f = [part(T)[0:P] for _ in range(2)]
        m_pad = part(T, I32)[0:P]
        m_rows = [part(T * PW)[0:P].rearrange("p (t c) -> p t c", t=T) for _ in range(2)]
        m_same = [part(W)[0:P].rearrange("p (t e) -> p t e", t=T) for _ in range(2)]
        m_edge = [part(T * D)[0:P].rearrange("p (t c) -> p t c", t=T) for _ in range(2)]
        m_vec = part(T * 3 * CV)[0:P].rearrange("p (t k c) -> p t k c", t=T, k=3)
        m_msg = [part(T * D)[0:P].rearrange("p (t c) -> p t c", t=T) for _ in range(2)]
        m_loaded = pair("m_loaded", 48)
        m_gathered, m_scattered = pair("m_gathered", 16 * T), pair("m_scattered", 16 * T)
        m_pad_made, m_pad_copied = sem("m_pad_made"), sem("m_pad_copied")
        m_copied, m_turned, m_masked = event("m_copied"), event("m_turned"), event("m_masked")
        m_early_made, m_counted, m_firsts_made = event("m_early_made"), event("m_counted"), event("m_firsts_made", 4)
        m_combined = event("m_combined", 4 * T + 2)
        m_summed, m_kept = event("m_summed", 2), event("m_kept", 2)

        with nc.Block() as block:
            @block.sync
            def _(sp):
                def load(g):
                    b, eds = g.b, m_loaded.sems[g.b]
                    wait(sp, m_copied, g.back(2))
                    settle(sp, 1)
                    wait(sp, m_combined, g.back(2))
                    settle(sp, 1)
                    wait(sp, m_gathered, g.back(2))
                    settle(sp, 1)
                    last = isinstance(g.i, int) and g.off == G - 1
                    n = LEFT if last else T
                    if last:
                        sp.dma_start(m_src[b][:, n:T], m_pad[:, n:T]).then_inc(m_pad_copied, 16)
                        sp.wait_ge(m_pad_copied, 16)
                    sp.dma_start(m_src[b][:, 0:n], src_v[:, bass.ds(g.number(T), n)], allow_slow_non_contiguous=True).then_inc(eds, 16)
                    sp.dma_start(m_dst[b][:, 0:n], dst_v[:, bass.ds(g.number(T), n)], allow_slow_non_contiguous=True).then_inc(eds, 16)
                    sp.dma_start(m_y[b][:, 0:n * 4], y_v[:, bass.ds(g.number(T * 4), n * 4)]).then_inc(eds, 16)

                sp.wait_ge(m_pad_made, 1)
                for g in range(2):
                    load(Group(0, g))
                with sp.Fori(0, (G - 3) // 2) as i:
                    for u in range(2):
                        load(Group(i, u + 2))
                load(Group(0, G - 1))

            @block.gpsimd
            def _(pool):
                nc.gpsimd.memset(m_pad, N).then_inc(m_pad_made, 1)

                def gather(g):
                    b = g.b
                    wait(pool, m_loaded, g)
                    wait(pool, m_combined, g.back(2))
                    settle(pool, 0)
                    for t in range(T):
                        nc.gpsimd.indirect_dma_start(m_rows[b][:, t, :], None, proj_rows,
                                                     bass.IndirectOffsetOnAxis(ap=m_dst[b][:, t:t + 1], axis=0)
                                                     ).then_inc(m_gathered.sems[b], 16)

                def add(g):
                    b = g.b
                    wait(pool, m_kept, g)
                    wait(pool, m_firsts_made, g)
                    wait(pool, m_scattered, g.back(1))
                    settle(pool, 0)
                    for t in range(T):
                        nc.gpsimd.indirect_dma_start(aggs[t], bass.IndirectOffsetOnAxis(ap=m_first[b][:, t:t + 1], axis=0),
                                                     m_msg[b][:, t, :], None, compute_op=ALU.add
                                                     ).then_inc(m_scattered.sems[b], 16)

                gather(Group(0, 0))
                gather(Group(0, 1))
                gather(Group(0, 2))
                add(Group(0, 0))
                with pool.Fori(0, (G - 3) // 2) as i:
                    for u in range(2):
                        gather(Group(i, u + 3))
                        add(Group(i, u + 1))
                for g in range(G - 2, G):
                    add(Group(0, g))
                wait(pool, m_scattered, Group(0, G - 2))
                wait(pool, m_scattered, Group(0, G - 1))

            @block.vector
            def _(dve):
                def copy_src(j):
                    b = j.b
                    wait(dve, m_loaded, j)
                    wait(dve, m_turned, j.back(2))
                    wait(dve, m_firsts_made, j.back(2))
                    nc.vector.tensor_copy(m_src_f[b], m_src[b]).then_inc(m_copied.sem, 1)

                def masks(j):
                    b = j.b
                    wait(dve, m_turned, j)
                    wait(dve, m_copied, j)
                    wait(dve, m_summed, j.back(2))
                    wait(dve, m_early_made, j.back(2))
                    nc.vector.tensor_tensor(m_same[b], ps[0:P, b, 0:W].rearrange("p (t e) -> p t e", t=T),
                                            m_src_f[b].unsqueeze(2).broadcast_to([P, T, P]), ALU.is_equal).then_inc(m_masked.sem, 1)
                    wait(dve, m_firsts_made, j.back(1))
                    nc.vector.tensor_scalar(m_away, m_src_f[b], -1.0, pcol[:, 0:1], ALU.mult, ALU.add).then_inc(m_firsts_made.sem, 1)
                    wait(dve, m_masked, j)
                    wait(dve, m_counted, j.back(1))
                    nc.vector.tensor_tensor(m_early, m_same[b], before[:, :].unsqueeze(1).broadcast_to([P, T, P]),
                                            ALU.mult).then_inc(m_early_made.sem, 1)
                    wait(dve, m_early_made, j)
                    nc.vector.tensor_reduce(m_cnt, m_early, AX.X, ALU.add).then_inc(m_counted.sem, 1)
                    wait(dve, m_counted, j)
                    nc.vector.tensor_scalar(m_cnt, m_cnt, 0.5, None, ALU.is_gt).then_inc(m_firsts_made.sem, 1)
                    wait(dve, m_firsts_made, j, 1)
                    nc.vector.tensor_tensor(m_moved, m_away, m_cnt, ALU.mult).then_inc(m_firsts_made.sem, 1)

                def table_rows(j):
                    wait(dve, m_firsts_made, j, 2)
                    wait(dve, m_scattered, j.back(2))
                    nc.vector.tensor_tensor(m_first[j.b], m_moved, m_src_f[j.b], ALU.add).then_inc(m_firsts_made.sem, 1)

                def messages(g):
                    b = g.b
                    y, r, o = m_y[b], m_rows[b], m_edge[b]
                    wait(dve, m_gathered, g)
                    wait(dve, m_summed, g.back(2))
                    for t in range(T):
                        nc.vector.scalar_tensor_tensor(o[:, t, :], r[:, t, P_DIST:P_DIST + D], y[:, 4 * t + 3:4 * t + 4],
                                                       r[:, t, P_ONE:P_ONE + D], ALU.mult, ALU.add).then_inc(m_combined.sem, 1)
                    wait(dve, m_combined, g.back(1))
                    nc.vector.tensor_tensor(m_vec, r[:, :, P_VEC:PW].unsqueeze(2).broadcast_to([P, T, 3, CV]),
                                            y.rearrange("p (t c) -> p t c", c=4)[:, :, 0:3].unsqueeze(3).broadcast_to([P, T, 3, CV]),
                                            ALU.mult).then_inc(m_combined.sem, 1)
                    for k in range(3):
                        for t in range(T):
                            wait(dve, m_combined, g, t if k == 0 else T + 1 + T * (k - 1) + t)
                            v = o[:, t, 0:CS]
                            nc.vector.scalar_tensor_tensor(v, r[:, t, P_DIR + k * CS:P_DIR + (k + 1) * CS],
                                                           y[:, 4 * t + k:4 * t + k + 1], v, ALU.mult, ALU.add
                                                           ).then_inc(m_combined.sem, 1)
                    v = o[:, :, CS:D].rearrange("p t (k c) -> p t k c", k=3)
                    nc.vector.tensor_tensor(v, v, m_vec, ALU.add).then_inc(m_combined.sem, 1)

                def body(j):
                    new, old = halves(j)
                    if new:
                        copy_src(j)
                    if old:
                        messages(j.back(1))
                        table_rows(j.back(1))
                    if new:
                        masks(j)

                steps(dve, body)

            @block.tensor
            def _(pe):
                def body(j):
                    new, old = halves(j)
                    if new:
                        wait(pe, m_copied, j)
                        wait(pe, m_masked, j.back(2))
                        for t in range(T):
                            ins = nc.tensor.transpose(ps[0:P, j.b, t * P:(t + 1) * P],
                                                      m_src_f[j.b][:, t:t + 1].broadcast_to([P, P]), ident[0:P, 0:P])
                        ins.then_inc(m_turned.sem, 1)
                    if old:
                        g = j.back(1)
                        b = g.b
                        wait(pe, m_masked, g)
                        wait(pe, m_combined, g)
                        for t in range(T):
                            if t % 2 == 0:
                                wait(pe, m_kept, g.back(2), t // 2)
                            ins = nc.tensor.matmul(ps[0:P, 2 + 2 * b + t // 2, (t % 2) * D:(t % 2 + 1) * D],
                                                   m_same[b][:, t, :], m_edge[b][:, t, :], start=True, stop=True)
                            if t % 2:
                                ins.then_inc(m_summed.sem, 1)

                steps(pe, body)

            @block.scalar
            def _(act):
                def body(j):
                    new, old = halves(j)
                    if not old:
                        return
                    g = j.back(1)
                    wait(act, m_scattered, g.back(2))
                    for k in range(2):
                        wait(act, m_summed, g, k)
                        nc.scalar.activation(m_msg[g.b][:, 2 * k:2 * k + 2, :],
                                             ps[0:P, 2 + 2 * g.b + k, 0:2 * D].rearrange("p (t c) -> p t c", t=2),
                                             ACT.Copy).then_inc(m_kept.sem, 1)

                steps(act, body)

        cut["at"] = 0
        Q0, Q1 = CS * CS, CV * CV
        CHUNKS = (Q0 + Q1) // 128
        QUADS = CHUNKS // 4
        YW = 2 * CV * CV
        x0a0 = part(NT * 2 * CS)[0:P].rearrange("p (j c) -> p j c", j=NT)
        a1x1 = part(NT * 6 * CV)[0:P].rearrange("p (j k c) -> p j k c", j=NT, k=3)
        x1 = part(NT * 3 * CV)[0:P].rearrange("p (j c) -> p j c", j=NT)
        w5_at = cut["at"]
        wQ, wY = part(CHUNKS * CS), part(YW)
        wLA, wLB = part(D), part(D)
        w5_end = cut["at"]
        both = part(CS)
        outs = part(NT * D)[0:P].rearrange("p (j c) -> p j c", j=NT)
        slots = part(NT * 3 * CV)[0:P].rearrange("p (j k w) -> p j k w", j=NT, k=3)
        catT, x1T, sumT = part(P), part(P), part(P)
        cat_tile, x1_tile = part(2 * CS)[0:P], part(3 * CV)[0:P]
        qT = [part(W) for _ in range(3)]
        tabs_at = cut["at"]
        q = part(Q0 + Q1)[0:P]
        q_part = [part(Q1)[0:P] for _ in range(2)]
        zbuf = [part(YW)[0:P] for _ in range(2)]
        cut["at"] = tabs_at
        tab5 = [part(NT * D)[0:P].rearrange("p (j c) -> p j c", j=NT) for _ in range(T)]
        cleared5, scaled5, aggs_loaded = sem("cleared5"), sem("scaled5"), sem("aggs_loaded")
        weights5_loaded = Count(sem("weights5_loaded"), 16)
        dve5, x_copied, both_made, cats_made = sem("dve5"), sem("x_copied"), sem("both_made"), sem("cats_made")
        tile_taken = event("tile_taken", 2)
        cat_turned, cat_kept, y_made = event("cat_turned", 2), event("cat_kept", 2), event("y_made")
        q000_made, q_started, q_rest, q110_made = event("q000_made", 2), event("q_started"), event("q_rest", 3), event("q110_made")
        q_turned, q_kept, q_used = event("q_turned", QUADS), event("q_kept", QUADS), event("q_used", QUADS)
        sum_kept, tile_made, tile_kept = event("sum_kept"), event("tile_made"), event("tile_kept")
        z_made, z_halved, z_summed = event("z_made", 3), event("z_halved", 3), event("z_summed", 3)
        stored = sem("stored")

        def tiles(eng, body):
            body(Group(0, 0, 1))
            with eng.Fori(0, NT - 1) as i:
                body(Group(i, 1, 1))

        def of(array, j, *at):
            v = array[(slice(None), bass.ds(j.number(1), 1)) + at]
            return v.rearrange("p o c -> p (o c)")

        def outer_product(left, right):
            m, n = left.shape[-1], right.shape[-1]
            return left.unsqueeze(2).broadcast_to([P, m, n]), right.unsqueeze(1).broadcast_to([P, m, n])

        with nc.Block() as block:
            @block.sync
            def _(sp):
                for k in range(T):
                    sp.dma_start(tab5[k], aggs[k][0:N, :].rearrange("(p j) c -> p j c", p=P)).then_inc(aggs_loaded, 16)
                sp.wait_ge(cleared5, 1)
                ld = lambda a, b: weights5_loaded(sp.dma_start(a, b, allow_slow_non_contiguous=True))
                for name, at, n, v in (("wu000", 0, Q0 // 128, CS), ("wu110", Q0 // 128, Q1 // 128, CV)):
                    us = w[name].rearrange("(c a) v w -> a v c w", a=128 // v)
                    for k in range(128 // v):
                        ld(wQ[k * v:(k + 1) * v, at * CS:(at + n) * CS].rearrange("p (c w) -> p c w", c=n), us[k])
                ld(wY[0:CS, 0:YW // 2], w["wu011"].rearrange("u v w -> u (v w)"))
                ld(wY[CS:2 * CS, YW // 2:YW].rearrange("p (u w) -> p u w", u=CV), w["wu101"].rearrange("u v w -> v u w"))
                ld(wLA[0:CS, 0:CS], w["lu0"])
                for k in range(3):
                    ld(wLB[k * CV:(k + 1) * CV, CS + k * CV:CS + (k + 1) * CV], w["lu1"])
                sp.wait_ge(stored, 1)
                sp.dma_start(out.rearrange("(p j) c -> p j c", p=P), xs[:, :, :]).then_inc(stored, 16)
                sp.wait_ge(stored, 17)

            @block.gpsimd
            def _(pool):
                nc.gpsimd.memset(room[:, w5_at:w5_end], 0.0).then_inc(cleared5, 1)
                pool.wait_ge(cats_made, 7)

                def body(j):
                    for k in (1, 2):
                        wait(pool, q110_made, j.back(1))
                        l, r = outer_product(of(x1, j, slice(k * CV, (k + 1) * CV)),
                                             a1x1[:, bass.ds(j.number(1), 1), k, 0:CV].rearrange("p o c -> p (o c)"))
                        nc.gpsimd.tensor_tensor(q_part[k - 1].rearrange("p (u v) -> p u v", u=CV), l, r,
                                                ALU.mult).then_inc(q_rest.sem, 1)
                    wait(pool, q_rest, j, 1)
                    nc.gpsimd.tensor_tensor(q_part[0], q_part[0], q_part[1], ALU.add).then_inc(q_rest.sem, 1)
                    for k in range(3):
                        zk = zbuf[k % 2]
                        wait(pool, z_made, j, k)
                        nc.gpsimd.tensor_tensor(zk[:, 0:YW // 2], zk[:, 0:YW // 2], zk[:, YW // 2:YW],
                                                ALU.add).then_inc(z_halved.sem, 1)

                tiles(pool, body)

            @block.vector
            def _(dve):
                dv = Count(dve5)
                dve.wait_ge(aggs_loaded, 16 * T)
                agg = tab5[0]
                for k in range(1, T):
                    dv(nc.vector.tensor_tensor(agg, agg, tab5[k], ALU.add))
                    dv.wait(dve)
                nc.vector.tensor_copy(x0a0[:, :, CS:2 * CS], agg[:, :, 0:CS]).then_inc(cats_made, 1)
                for k in range(3):
                    nc.vector.tensor_copy(a1x1[:, :, k, 0:CV], agg[:, :, CS + k * CV:CS + (k + 1) * CV]).then_inc(cats_made, 1)
                dve.wait_ge(x_copied, 1 + 3)
                for k in range(3):
                    nc.vector.tensor_copy(a1x1[:, :, k, CV:2 * CV], x1[:, :, k * CV:(k + 1) * CV]).then_inc(cats_made, 1)
                dv(nc.vector.tensor_tensor(xs[:, :, :], xs[:, :, :], hs[:, :, :], ALU.add))
                dve.wait_ge(cats_made, 7)

                def q000(j, half):
                    n = CS // 2
                    if half == 0:
                        wait(dve, q_turned, j.back(1))
                    l, r = outer_product(of(x0a0, j, slice(n * half, n * half + n)), of(x0a0, j, slice(CS, 2 * CS)))
                    nc.vector.tensor_tensor(q[:, n * CS * half:n * CS * (half + 1)].rearrange("p (u v) -> p u v", u=n),
                                            l, r, ALU.mult).then_inc(q000_made.sem, 1)

                def terms(j, k):
                    if k == 0:
                        wait(dve, y_made, j)
                    if k < 2:
                        wait(dve, z_summed, j.back(1), 2 if k == 0 else 1)
                    else:
                        wait(dve, z_summed, j, 0)
                    factor = a1x1[:, bass.ds(j.number(1), 1), k, :].rearrange("p o c -> p (o c)")
                    nc.vector.tensor_tensor(zbuf[k % 2].rearrange("p (s w) -> p s w", w=CV),
                                            ps[0:P, 0:4, :].rearrange("p b (s w) -> p (b s) w", w=CV),
                                            factor.unsqueeze(2).broadcast_to([P, 2 * CV, CV]), ALU.mult).then_inc(z_made.sem, 1)

                def total(j, k):
                    wait(dve, z_halved, j, k)
                    nc.vector.tensor_reduce(slots[:, bass.ds(j.number(1), 1), k, :],
                                            zbuf[k % 2][:, 0:YW // 2].rearrange("p (s w) -> p w s", w=CV).unsqueeze(1),
                                            AX.X, ALU.add).then_inc(z_summed.sem, 1)

                def body(j):
                    q000(j, 0)
                    if j.back(1).exists():
                        total(j.back(1), 2)
                    q000(j, 1)
                    wait(dve, q110_made, j.back(1))
                    l, r = outer_product(of(x1, j, slice(0, CV)),
                                         a1x1[:, bass.ds(j.number(1), 1), 0, 0:CV].rearrange("p o c -> p (o c)"))
                    nc.vector.tensor_tensor(q[:, Q0:Q0 + Q1].rearrange("p (u v) -> p u v", u=CV), l, r,
                                            ALU.mult).then_inc(q_started.sem, 1)
                    terms(j, 0)
                    terms(j, 1)
                    wait(dve, q_started, j)
                    wait(dve, q_rest, j)
                    nc.vector.tensor_tensor(q[:, Q0:Q0 + Q1], q[:, Q0:Q0 + Q1], q_part[0], ALU.add).then_inc(q110_made.sem, 1)
                    total(j, 0)
                    terms(j, 2)
                    total(j, 1)

                tiles(dve, body)
                total(Group(0, NT - 1, 1), 2)
                dve.wait_ge(z_summed.sem, 3 * NT)
                dve.wait_ge(tile_kept.sem, NT)
                dv.wait(dve)
                dv(nc.vector.tensor_tensor(outs[:, :, CS:D], outs[:, :, CS:D], slots.rearrange("p j k w -> p j (k w)"), ALU.add))
                dv(nc.vector.tensor_tensor(xs[:, :, 0:CS], xs[:, :, 0:CS], outs[:, :, 0:CS], ALU.add))
                dv.wait(dve)
                v = xs[:, :, CS:D].rearrange("p j (c k) -> p j c k", k=3)
                for k in range(3):
                    dv(nc.vector.tensor_tensor(v[:, :, :, k], v[:, :, :, k], outs[:, :, CS + k * CV:CS + (k + 1) * CV], ALU.add))
                dve.wait_ge(dve5, dv.n)
                dve.sem_inc(stored, 1)

            @block.scalar
            def _(act):
                nc.scalar.activation(x0a0[:, :, 0:CS], hs[:, :, 0:CS], ACT.Copy).then_inc(x_copied, 1)
                v = hs[:, :, CS:D].rearrange("p j (c k) -> p k j c", k=3)
                for k in range(3):
                    nc.scalar.activation(x1[:, :, k * CV:(k + 1) * CV], v[:, k], ACT.Copy).then_inc(x_copied, 1)
                for r in (0, 64):
                    nc.scalar.activation(both[r:r + CS, :], ident[r:r + CS, r:r + CS], ACT.Copy).then_inc(both_made, 1)
                act.wait_ge(cats_made, 7)
                act.wait_ge(weights5_loaded.sem, weights5_loaded.n)
                for t, f in ((wQ[:, 0:Q0 // 2], K0), (wQ[:, Q0 // 2:], K0 * S3), (wY, K1), (wLA, CS ** -0.5), (wLB, CV ** -0.5)):
                    nc.scalar.mul(t, t, f).then_inc(scaled5, 1)

                def keep(out_, in_, ev):
                    nc.scalar.activation(out_, in_, ACT.Copy).then_inc(ev.sem, 1)

                def take(j):
                    wait(act, cat_turned, j.back(1))
                    keep(cat_tile, of(x0a0, j, slice(0, 2 * CS)), tile_taken)
                    keep(x1_tile, of(x1, j, slice(0, 3 * CV)), tile_taken)
                    wait(act, cat_turned, j)
                    wait(act, y_made, j.back(1))
                    wait(act, tile_made, j.back(1))
                    keep(catT, ps[:, 7, 0:P], cat_kept)
                    keep(x1T[0:96, :], ps[0:96, 7, 128:128 + P], cat_kept)

                def body(j):
                    take(j)
                    for k in range(QUADS):
                        wait(act, q_turned, j, k)
                        if k >= 3:
                            wait(act, q_used, j, k - 3)
                        else:
                            wait(act, q_used, j.back(1), QUADS - 3 + k)
                        keep(qT[k % 3], ps[:, 4 + k % 2, 0:W], q_kept)
                    wait(act, q_used, j)
                    wait(act, tile_made, j.back(1))
                    keep(sumT, ps[:, 6, 0:P], sum_kept)
                    wait(act, tile_made, j)
                    keep(outs[:, bass.ds(j.number(1), 1), :], ps[0:P, 7:8, 256:256 + D], tile_kept)

                tiles(act, body)

            @block.tensor
            def _(pe):
                pe.wait_ge(scaled5, 5)
                pe.wait_ge(both_made, 2)
                pe.wait_ge(cats_made, 7)

                def turn_quad(j, k):
                    if k in (0, 4):
                        wait(pe, q000_made, j, k // 4)
                    if k == 8:
                        wait(pe, q110_made, j)
                    if k >= 2:
                        wait(pe, q_kept, j, k - 2)
                    else:
                        wait(pe, q_kept, j.back(1), QUADS - 2 + k)
                    for c in range(4):
                        at = 128 * (4 * k + c)
                        ins = nc.tensor.transpose(ps[:, 4 + k % 2, c * P:(c + 1) * P], q[:, at:at + 128], ident[0:P, 0:P])
                    ins.then_inc(q_turned.sem, 1)

                def add_quad(j, k):
                    wait(pe, q_kept, j, k)
                    if k == 0:
                        wait(pe, sum_kept, j.back(1))
                    for c in range(4):
                        n, r = 4 * k + c, CS * (c % 2)
                        ins = nc.tensor.matmul(ps[r:r + CS, 6, 0:P], wQ[:, n * CS:(n + 1) * CS], qT[k % 3][:, c * P:(c + 1) * P],
                                               start=(n < 2), stop=True, skip_group_check=True)
                    ins.then_inc(q_used.sem, 1)

                def body(j):
                    wait(pe, tile_kept, j.back(1))
                    wait(pe, tile_taken, j)
                    nc.tensor.transpose(ps[:, 7, 0:P], cat_tile, ident[0:P, 0:P]).then_inc(cat_turned.sem, 1)
                    nc.tensor.transpose(ps[0:96, 7, 128:128 + P], x1_tile, ident[0:P, 0:P]).then_inc(cat_turned.sem, 1)
                    wait(pe, cat_kept, j)
                    wait(pe, z_made, j.back(1))
                    for k in range(YW // 512):
                        ins = nc.tensor.matmul(ps[0:P, k, :], catT, wY[:, 512 * k:512 * (k + 1)], start=True, stop=True)
                    ins.then_inc(y_made.sem, 1)
                    turn_quad(j, 0)
                    for k in range(QUADS):
                        if k + 1 < QUADS:
                            turn_quad(j, k + 1)
                        add_quad(j, k)
                    o = ps[0:P, 7, 256:256 + D]
                    nc.tensor.matmul(o, catT, wLA, start=True, stop=False)
                    nc.tensor.matmul(o, x1T[0:96, :], wLB[0:96, :], start=False, stop=True)
                    wait(pe, sum_kept, j)
                    nc.tensor.matmul(o[:, 0:CS], sumT, both, start=False, stop=True, skip_group_check=True).then_inc(tile_made.sem, 1)

                tiles(pe, body)


WEIGHTS = {
    "L0_gnn_": ["gamma_s", "beta_s", "gamma_v", "Ws_src", "Wv_src", "Ws_dst", "Wv_dst", "W_rbf", "W_alpha",
                "alpha_dot", "Ws_val", "Wv_val", "Wg", "w2_ss", "w2_sv", "w2_vs", "w2_vv0", "w2_vv1",
                "Ws_vlin", "Wv_vlin", "Wps", "Wpv"],
    "L1_gnn_": ["wm000", "wm011", "wm101", "wm110", "lm0", "lm1", "wu000", "wu011", "wu101", "wu110", "lu0", "lu1"],
}


def kernel(**inputs):
    import numpy as np
    import concourse.bacc as bacc
    from concourse.bass_utils import run_bass_kernel_spmd

    nc = bacc.Bacc("TRN2", target_bir_lowering=False, num_devices=1)
    arrays = {}

    def given(name):
        a = np.ascontiguousarray(inputs[name])
        arrays[f"in_{name}"] = a
        return nc.dram_tensor(f"in_{name}", a.shape, mybir.dt.from_np(a.dtype), kind="ExternalInput").ap()

    args = [given(n) for n in ("x", "src", "dst", "edge_attr_16", "edge_attr_4")]
    weights = {n: given(prefix + n) for prefix, names in WEIGHTS.items() for n in names}
    out = nc.dram_tensor("out_x", (N, D), F32, kind="ExternalOutput").ap()
    build(nc, *args, weights, out)
    r = run_bass_kernel_spmd(nc, [arrays], core_ids=[0])
    return r.results[0]["out_x"]
```

```python
from contextlib import ExitStack

import concourse.bass as bass
from concourse import mybir

F32 = mybir.dt.float32
I32 = mybir.dt.int32
ALU = mybir.AluOpType
ACT = mybir.ActivationFunctionType
AX = mybir.AxisListType

N, E = 3125, 53125
CS, CV = 64, 32
D = CS + 3 * CV
H = 4
NB = 16
P = 125
NT = N // P
ET = E // P
T = 4
G = -(-ET // T)
LEFT = ET - T * (G - 1)
W = T * P
ROWS = 26 * P
AC = D + 2 * H
PW = 544
LOW = -1.0e30
EPS = 1e-5
S2, S3 = 2.0 ** -0.5, 3.0 ** -0.5
R96 = 96.0 ** -0.5
K0, K1 = (CS * CS + CV * CV) ** -0.5, (2 * CS * CV) ** -0.5

O_BANK, F_BANK, L_BANK, D_BANK = 0, (1, 0, 1, 0), (5, 1, 0, 5, 0), 1

V0, V1, SC, V2 = 0, 32, 64, 128
HEADS = ((V0, CV // H), (V1, CV // H), (SC, CS // H), (V2, CV // H))
HW = D + 2 * CV
RUNS = ((V2, 3 * CV), (V1, 2 * CV + CS), (SC, 2 * CV + CS), (V0, 2 * CV + CS))
U_AT = (0, 96, 224, 352)
UW = 480
SUMS = [(2 * p + t, c) for p in range(T // 2) for c in range(4) for t in range(2)]
SUM_NO = {s: n for n, s in enumerate(SUMS)}
U_BANK = (3, 4, 3, 4)

class Event:

    def __init__(self, sem, per):
        self.sem, self.per = sem, per

    def value(self, g, k=None):
        return g.number(self.per, self.per if k is None else k + 1)

class Pair:

    def __init__(self, sems, per):
        self.sems, self.per = sems, per

class Group:

    def __init__(self, i, off, stride=2):
        self.i, self.off, self.stride = i, off, stride
        self.b = off % 2

    def back(self, n):
        return Group(self.i, self.off - n, self.stride)

    def ahead(self, n):
        return self.back(-n)

    def number(self, per, plus=0):
        return self.i * (self.stride * per) + (self.off * per + plus)

    def pair(self, per):
        return self.i * per + (self.off // 2 + 1) * per

    def exists(self):
        return not (isinstance(self.i, int) and not 0 <= self.off < G)

def wait(eng, event, g, k=None):
    if not g.exists():
        return
    if isinstance(event, Pair):
        eng.wait_ge(event.sems[g.b], g.pair(event.per))
    else:
        eng.wait_ge(event.sem, event.value(g, k))

class Count:

    def __init__(self, sem, step=1):
        self.sem, self.step, self.n = sem, step, 0

    def __call__(self, ins):
        self.n += self.step
        ins.then_inc(self.sem, self.step)
        return self.n

    def wait(self, eng, n=None):
        eng.wait_ge(self.sem, self.n if n is None else n)

def build(nc, x, src, dst, edge16, edge4, w, out):
    ctx = ExitStack()
    with ctx:
        def sb(name, shape, dt=F32):
            return ctx.enter_context(nc.sbuf_tensor(name, shape, dt))

        def sem(name):
            return ctx.enter_context(nc.semaphore(name))

        def event(name, per=1):
            return Event(sem(name), per)

        def pair(name, per):
            return Pair([sem(f"{name}_even"), sem(f"{name}_odd")], per)

        def dram(name, shape, dt=F32):
            return nc.dram_tensor(name, shape, dt, kind="Internal").ap()

        src_rows = dram("src_rows", (N, D))
        dst_rows = dram("dst_rows", (ROWS, D))
        sums = [dram(f"sums{k}", (ROWS, AC)) for k in range(T)]
        proj_rows = dram("proj_rows", (N, PW))
        aggs = [dram(f"aggs{k}", (ROWS, D)) for k in range(T)]

        ps = ctx.enter_context(nc.psum_tensor("ps", [128, 8, 512], F32))

        xs = sb("xs", [P, NT, D])
        hs = sb("hs", [P, NT, D])
        ident = sb("ident", [128, 128])
        before = sb("before", [P, P])
        pcol = sb("pcol", [P, 1])
        pcol_i = sb("pcol_i", [P, 1], I32)
        room = sb("room", [128, 42000])
        cut = {"at": 0}

        def part(width, dt=F32):
            a = cut["at"]
            cut["at"] = a + width
            assert cut["at"] <= 42000, cut["at"]
            v = room[:, a:a + width]
            return v if dt == F32 else v.bitcast(dt)

        stage = part(NT * 2 * D)[0:P].rearrange("p (j c) -> p j c", j=NT)
        nn = part(NT * D)[0:P].rearrange("p (j c) -> p j c", j=NT)
        tmp = part(NT * D)[0:P].rearrange("p (j c) -> p j c", j=NT)
        stat = part(8 * NT)[0:P].rearrange("p (k j) -> p k j", k=8)
        n_tile = [part(D)[0:P] for _ in range(2)]
        nA = [part(128) for _ in range(2)]
        nB = [part(128) for _ in range(2)]
        gam = part(CS + CV + CS)
        wA = part(2 * D)
        wB = part(2 * D)
        init_row = part(26 * AC)[0:P].rearrange("p (j c) -> p j c", j=26)
        node_end = cut["at"]

        cut["at"] = 0
        e_src = [part(T, I32)[0:P] for _ in range(2)]
        e_dst = [part(T, I32)[0:P] for _ in range(2)]
        e_rbf = [part(T * NB)[0:P] for _ in range(2)]
        e_y = [part(T * 4)[0:P] for _ in range(2)]
        pad_dst = part(T, I32)[0:P]
        g_src = [part(T * D)[0:P] for _ in range(2)]
        g_dst = [part(T * D)[0:P] for _ in range(2)]
        outer = [part(T * 128)[0:P].rearrange("p (t c) -> p t c", t=T) for _ in range(2)]
        y_kept = [part(T * 4)[0:P] for _ in range(2)]
        dst_kept = [part(T, I32)[0:P] for _ in range(2)]
        dst_f = [part(T)[0:P] for _ in range(2)]
        feat = part(T * 256)[0:P].rearrange("p (t c) -> p t c", t=T)
        oT = part(W)
        fT = [part(W) for _ in range(4)]
        prod = [part(W) for _ in range(5)]
        xv = part(W)
        rl = part(W)
        sg = part(W)
        tg = part(W)[0:96]
        gv = part(W)[0:96]
        logit = part(T * H)[0:P].rearrange("p (t h) -> p t h", t=T)
        same = [part(W)[0:P].rearrange("p (t e) -> p t e", t=T) for _ in range(2)]
        apart = [part(W)[0:P].rearrange("p (t e) -> p t e", t=T) for _ in range(2)]
        early = part(W)[0:P].rearrange("p (t e) -> p t e", t=T)
        masked = [part(W)[0:P].rearrange("p (t e) -> p t e", t=T) for _ in range(2)]
        cnt = part(T)[0:P]
        away = part(T)[0:P]
        moved = part(T)[0:P]
        first = [part(T, I32)[0:P] for _ in range(2)]
        rows = [part(T * AC)[0:P].rearrange("p (t c) -> p t c", t=T) for _ in range(2)]
        gmax = part(T * H)[0:P].rearrange("p (t h) -> p t h", t=T)
        newmax = part(T * H)[0:P].rearrange("p (t h) -> p t h", t=T)
        shift = part(2 * T * H)[0:P].rearrange("p (k t h) -> p k t h", k=2, t=T)
        scale = part(2 * T * H)[0:P].rearrange("p (k t h) -> p k t h", k=2, t=T)
        ht = part(T * HW)[0:P].rearrange("p (t c) -> p t c", t=T)
        vx = part(T * (D + H))[0:P].rearrange("p (t c) -> p t c", t=T)
        edge_end = cut["at"]
        cut["at"] = w_at = max(node_end, edge_end)
        wl_all = part(5 * 128)
        wL = [wl_all[:, k * 128:(k + 1) * 128] for k in range(5)]
        wX0, wX4 = part(128), part(128)
        wV = [part(32) for _ in range(3)]
        wV4 = part(96)
        wG = part(96)
        wLr = part(H)
        wUg, wUs = part(UW), part(CS + CV)
        w2col = part(8)
        l0_end = cut["at"]

        inputs_loaded = sem("inputs_loaded")
        cleared = sem("cleared")
        weights_loaded = Count(sem("weights_loaded"), 16)
        dve_step, pool_step = sem("dve_step"), sem("pool_step")
        weights_scaled = sem("weights_scaled")
        var_ready, std_ready = sem("var_ready"), sem("std_ready")
        consts_made = sem("consts_made")
        nn_ready = sem("nn_ready")
        nn_taken, nodes_turned, turned_kept = event("nn_taken"), event("nodes_turned", 2), event("turned_kept", 2)
        projected, projection_kept = event("projected"), event("projection_kept")
        tables_stored = sem("tables_stored")
        edge_places_cleared = sem("edge_places_cleared")
        pad_copied = sem("pad_copied")
        settled = [sem("pool_settled"), sem("sync_settled")]

        edges_loaded = pair("edges_loaded", 64)
        nodes_gathered = pair("nodes_gathered", 2 * T * 16)
        rows_gathered = pair("rows_gathered", T * 16)
        rows_scattered = pair("rows_scattered", T * 16)
        outer_built = event("outer_built", 4)
        copies_made = event("copies_made", 3)
        feat_added, feat_dup = event("feat_added"), event("feat_dup", 2)
        outer_turned, outer_kept = event("outer_turned"), event("outer_kept")
        f_turned, f_kept = event("f_turned", 4), event("f_kept", 4)
        l_made, prod_made = event("l_made", 5), event("prod_made", 5)
        x_made, v_made, xv_kept = event("x_made"), event("v_made"), event("xv_kept", 3)
        g_made, tg_made, sg_made = event("g_made"), event("tg_made"), event("sg_made", 2)
        gv_made = event("gv_made")
        lg_made, lg_kept = event("lg_made"), event("lg_kept")
        d_made, same_made, early_made = event("d_made"), event("same_made"), event("early_made")
        apart_made, early_counted = event("apart_made"), event("early_counted", T)
        firsts_made = event("firsts_made", 4)
        a_made, a_masked, a_max = event("a_made", 4), event("a_masked", 4), event("a_max", 4)
        shift_made, exp_made = event("shift_made", 3), event("exp_made")
        us_made, u_made, zeroed = event("us_made"), event("u_made", T), event("zeroed")
        t0_made, comb, folded = event("t0_made", 4 * T), event("comb", 4 * T), event("folded")
        vx_made, sm_made = event("vx_made", 5), event("sm_made", 2)
        rows_scaled, rows_added = event("rows_scaled", 5), event("rows_added", 3)

        def settle(eng, k):
            eng.sem_inc(settled[k], 1)

        def fold(ap):
            return ap.rearrange("(p t) c -> p (t c)", p=P)

        src_v, dst_v = src.rearrange("(p t) -> p t", p=P), dst.rearrange("(p t) -> p t", p=P)
        rbf_v, y_v = fold(edge16), fold(edge4)

        def norm(dve, dv, raw, res, c, root, relu, stat, tmp, var_ready, std_ready):
            bc = lambda k: stat[:, k, :].unsqueeze(2).broadcast_to([P, NT, c])
            dv(nc.vector.tensor_reduce(stat[:, 0, :], raw, AX.X, ALU.add))
            dv.wait(dve)
            dv(nc.vector.tensor_scalar(stat[:, 1, :], stat[:, 0, :], 1.0 / c, None, ALU.mult))
            dv.wait(dve)
            dv(nc.vector.tensor_tensor(res, raw, bc(1), ALU.subtract))
            dv.wait(dve)
            dv(nc.vector.tensor_tensor(tmp[:, :, 0:c], res, res, ALU.mult))
            dv.wait(dve)
            dv(nc.vector.tensor_reduce(stat[:, 2, :], tmp[:, :, 0:c], AX.X, ALU.add))
            dv.wait(dve)
            nc.vector.tensor_scalar(stat[:, 3, :], stat[:, 2, :], 1.0 / c, EPS, ALU.mult, ALU.add).then_inc(var_ready, 1)
            dve.wait_ge(std_ready, root)
            dv(nc.vector.reciprocal(stat[:, 5, :], stat[:, 4, :]))
            dv.wait(dve)
            dv(nc.vector.tensor_tensor(res, res, bc(5), ALU.mult))
            dv.wait(dve)
            if relu:
                dv(nc.vector.tensor_scalar(res, res, 0.0, None, ALU.max))
                dv.wait(dve)

        def root_of(act, root):
            act.wait_ge(var_ready, root)
            nc.scalar.activation(stat[:, 4, :], stat[:, 3, :], ACT.Sqrt).then_inc(std_ready, 1)

        def to_rows(dst_ap, vecs):
            v = vecs.rearrange("p j (c k) -> p j c k", k=3)
            return [(dst_ap[:, :, at:at + CV], v[:, :, :, k]) for k, at in enumerate((V0, V1, V2))]

        def node_steps(eng, body):
            for j in range(3):
                body(Group(0, j), True, j > 0)
            with eng.Fori(0, (NT - 3) // 2) as i:
                for u in range(2):
                    body(Group(i, u + 3), True, True)
            body(Group(0, NT), False, True)

        def take_tiles(pool, tile, source, taken, turned):
            def body(j, new, old):
                if new:
                    wait(pool, turned, j.back(2))
                    nc.gpsimd.tensor_copy(tile[j.b], source[:, bass.ds(j.number(1), 1), :].rearrange("p o c -> p (o c)")
                                          ).then_inc(taken.sem, 1)

            node_steps(pool, body)

        def turn(pe, j, tile, taken, turned, kept):
            b = j.b
            wait(pe, taken, j)
            wait(pe, kept, j.back(2))
            nc.tensor.transpose(ps[:, b, 0:P], tile[b][:, 0:128], ident[0:P, 0:P]).then_inc(turned.sem, 1)
            nc.tensor.transpose(ps[0:32, b, 128:128 + P], tile[b][:, 128:D], ident[0:P, 0:P]).then_inc(turned.sem, 1)

        def keep_turned(act, j, left, right, turned, kept, used):
            b = j.b
            wait(act, turned, j)
            wait(act, used, j.back(2))
            nc.scalar.activation(left[b][:, 0:P], ps[:, b, 0:P], ACT.Copy).then_inc(kept.sem, 1)
            nc.scalar.activation(right[b][0:32, 0:P], ps[0:32, b, 128:128 + P], ACT.Copy).then_inc(kept.sem, 1)

        with nc.Block() as block:
            @block.sync
            def _(sp):
                sp.dma_start(xs[:, :, :], x.rearrange("(p j) c -> p j c", p=P)).then_inc(inputs_loaded, 16)
                sp.dma_start(gam[0:P, 0:CS], w["gamma_s"].partition_broadcast(P)).then_inc(inputs_loaded, 16)
                sp.dma_start(gam[0:P, CS:2 * CS], w["beta_s"].partition_broadcast(P)).then_inc(inputs_loaded, 16)
                sp.dma_start(gam[0:P, 2 * CS:2 * CS + CV], w["gamma_v"].partition_broadcast(P)).then_inc(inputs_loaded, 16)
                sp.wait_ge(cleared, 3)
                ld = lambda a, b: weights_loaded(sp.dma_start(a, b, allow_slow_non_contiguous=True))
                for k, (ws, wv) in enumerate(((w["Ws_src"], w["Wv_src"]), (w["Ws_dst"], w["Wv_dst"]))):
                    ld(wA[V0:V0 + 32, k * D + V0:k * D + V0 + 32], wv)
                    ld(wA[V1:V1 + 32, k * D + V1:k * D + V1 + 32], wv)
                    ld(wA[SC:SC + 64, k * D + SC:k * D + SC + 64], ws)
                    ld(wB[0:32, k * D + V2:k * D + V2 + 32], wv)
                Wr = w["W_rbf"]
                r_ss, r_sv = Wr[:, 0:64], Wr[:, 64:128]
                r_vs, r_vv0, r_vv1 = Wr[:, 128:160], Wr[:, 160:192], Wr[:, 192:224]
                lw = [[(0, 1, r_vv0), (32, 2, r_vv0), (64, 0, r_ss)],
                      [(0, 0, r_vs), (32, 3, r_vv1), (64, 1, r_sv)],
                      [(0, 0, r_vs), (32, 2, r_sv), (96, 1, r_vv1)],
                      [(0, 3, r_sv), (64, 0, r_vs), (96, 2, r_vv1)],
                      [(0, 2, r_vv1), (32, 3, r_vv1), (64, 1, r_vv1), (96, 3, r_vv0)]]
                for k in range(5):
                    for col, c, b in lw[k]:
                        ld(wL[k][16 * c:16 * c + 16, col:col + b.shape[1]], b)
                for col, m in ((0, w["W_alpha"]), (64, w["Ws_val"])):
                    ld(wX0[0:32, col:col + 64], m[64:96, :])
                    ld(wX0[32:64, col:col + 64], m[64:96, :])
                    ld(wX0[64:128, col:col + 64], m[0:64, :])
                    ld(wX4[96:128, col:col + 64], m[64:96, :])
                Wv = w["Wv_val"]
                for k, (s_at, vs_at, c_at) in enumerate(((64, 0, 32), (32, 0, 96), (0, 64, 96))):
                    ld(wV[k][s_at:s_at + 64, :], Wv[0:64, :])
                    ld(wV[k][vs_at:vs_at + 32, :], Wv[64:96, :])
                    ld(wV[k][c_at:c_at + 32, :], Wv[96:128, :])
                for k in range(3):
                    ld(wV4[32 * k:32 * k + 32, 32 * k:32 * k + 32], Wv[96:128, :])
                    ld(wG[64:128, 32 * k:32 * k + 32], w["Wg"])
                for h in range(H):
                    a = w["alpha_dot"][0, h, :].rearrange("(a o) -> a o", o=1)
                    for r in (0, CS):
                        ld(wLr[r + h * CS // H:r + (h + 1) * CS // H, h:h + 1], a)
                Wh, Wl = w["Wv_vlin"], w["Ws_vlin"]

                for k, to in ((2, 0), (0, 1), (1, 2)):
                    ld(wUg[32 * k:32 * k + 32, to * CV:(to + 1) * CV], Wh[64:96, :])
                for j, (s_at, plus, minus) in enumerate(((32, 0, 96), (0, 64, 96), (64, 0, 32))):
                    a, b, at = (j + 1) % 3, (j + 2) % 3, U_AT[1 + j]
                    ld(wUg[32 * j:32 * j + 32, at + s_at:at + s_at + CS], Wl[64:96, :])
                    ld(wUg[32 * b:32 * b + 32, at + plus:at + plus + CV], Wh[96:128, :])
                    ld(wUg[32 * a:32 * a + 32, at + minus:at + minus + CV], Wh[96:128, :])
                    for k, name in enumerate(("w2_vs", "w2_vv0", "w2_vv1")):
                        ld(w2col[32 * j:32 * j + 32, k:k + 1], w[name].rearrange("(a o) -> a o", o=1))
                ld(wUs[64:128, 0:CS], Wl[0:64, :])
                ld(wUs[64:128, CS:CS + CV], Wh[0:64, :])
                for k, name in enumerate(("w2_ss", "w2_sv")):
                    ld(w2col[64:128, 3 + k:4 + k], w[name].rearrange("(a o) -> a o", o=1))
                sp.wait_ge(consts_made, 5)
                for k in range(T):
                    sp.dma_start(sums[k].rearrange("(p j) c -> p j c", p=P), init_row).then_inc(tables_stored, 16)
                sp.dma_start(dst_rows[N:ROWS, :], init_row[:, 0, 0:D]).then_inc(tables_stored, 16)
                sp.wait_ge(projection_kept.sem, NT)
                sp.dma_start(src_rows.rearrange("(p j) c -> p j c", p=P), stage[:, :, 0:D]).then_inc(tables_stored, 16)
                sp.dma_start(dst_rows[0:N, :].rearrange("(p j) c -> p j c", p=P), stage[:, :, D:2 * D]).then_inc(tables_stored, 16)
                sp.wait_ge(tables_stored, 16 * (T + 3))
                sp.wait_ge(weights_loaded.sem, weights_loaded.n)

            @block.gpsimd
            def _(pool):
                nc.gpsimd.memset(room[:, w_at:l0_end], 0.0).then_inc(cleared, 1)
                nc.gpsimd.memset(wA, 0.0).then_inc(cleared, 1)
                nc.gpsimd.memset(wB, 0.0).then_inc(cleared, 1)
                nc.gpsimd.memset(ident[:, :], 0.0).then_inc(pool_step, 1)
                nc.gpsimd.memset(before[:, :], 1.0).then_inc(pool_step, 1)
                nc.gpsimd.memset(init_row[:, :, 0:D + H], 0.0).then_inc(consts_made, 1)
                nc.gpsimd.memset(init_row[:, :, D + H:AC], LOW).then_inc(consts_made, 1)
                nc.gpsimd.iota(pcol_i[:, :], pattern=[[0, 1]], base=N, channel_multiplier=1).then_inc(pool_step, 1)
                pool.wait_ge(pool_step, 3)
                nc.gpsimd.tensor_copy(pcol[:, :], pcol_i[:, :]).then_inc(consts_made, 1)
                nc.gpsimd.affine_select(out=ident[:, :], in_=ident[:, :], compare_op=ALU.not_equal, fill=1.0,
                                        base=0, pattern=[[-1, 128]], channel_multiplier=1).then_inc(consts_made, 1)
                nc.gpsimd.affine_select(out=before[:, :], in_=before[:, :], compare_op=ALU.is_gt, fill=0.0,
                                        base=0, pattern=[[-1, P]], channel_multiplier=1).then_inc(consts_made, 1)
                pool.wait_ge(nn_ready, 4)
                take_tiles(pool, n_tile, nn, nn_taken, nodes_turned)

            @block.vector
            def _(dve):
                dv = Count(dve_step)
                dve.wait_ge(inputs_loaded, 64)
                norm(dve, dv, xs[:, :, :], hs[:, :, :], D, 1, True, stat, tmp, var_ready, std_ready)
                sn = stage[:, :, 0:CS]
                norm(dve, dv, hs[:, :, 0:CS], sn, CS, 2, False, stat, tmp, var_ready, std_ready)
                row = lambda a, b: gam[0:P, a:b].unsqueeze(1).broadcast_to([P, NT, b - a])
                dv(nc.vector.tensor_tensor(sn, sn, row(0, CS), ALU.mult))
                dv.wait(dve)
                nc.vector.tensor_tensor(nn[:, :, SC:SC + CS], sn, row(CS, 2 * CS), ALU.add).then_inc(nn_ready, 1)
                vec = hs[:, :, CS:D]
                dv(nc.vector.tensor_tensor(tmp[:, :, 0:3 * CV], vec, vec, ALU.mult))
                dv.wait(dve)
                dv(nc.vector.tensor_reduce(stat[:, 2, :], tmp[:, :, 0:3 * CV], AX.X, ALU.add))
                dv.wait(dve)
                nc.vector.tensor_scalar(stat[:, 3, :], stat[:, 2, :], 1.0 / CV, EPS, ALU.mult, ALU.add).then_inc(var_ready, 1)
                dve.wait_ge(std_ready, 3)
                dv(nc.vector.reciprocal(stat[:, 5, :], stat[:, 4, :]))
                dv.wait(dve)
                dv(nc.vector.tensor_tensor(tmp[:, :, 0:3 * CV], vec,
                                           stat[:, 5, :].unsqueeze(2).broadcast_to([P, NT, 3 * CV]), ALU.mult))
                dv.wait(dve)
                for o, i in to_rows(nn, tmp[:, :, 0:3 * CV]):
                    nc.vector.tensor_tensor(o, i, row(2 * CS, 2 * CS + CV), ALU.mult).then_inc(nn_ready, 1)
                dve.wait_ge(weights_loaded.sem, weights_loaded.n)
                sc = []
                mul = lambda ap, f, g=None: sc.append(
                    nc.vector.tensor_scalar(ap, ap, f, g, ALU.mult, ALU.mult) if g is not None
                    else nc.vector.tensor_scalar(ap, ap, f, None, ALU.mult))
                mul(wX0[0:64, :], S3)
                mul(wX4[96:128, :], S3)
                for k, c_at in enumerate((32, 96, 96)):
                    mul(wV[k][c_at:c_at + 32, :], S2)
                mul(wV4[0:96, :], -S2)
                mul(wLr[0:64, :], 0.2)
                mul(wLr[64:128, :], 0.8)
                mul(wUs[64:128, 0:CS], w2col[64:128, 3:4], 0.5)
                mul(wUs[64:128, CS:CS + CV], w2col[64:128, 4:5], 0.5)
                mul(wUg[0:96, 0:96], w2col[0:96, 0:1], 0.5)
                for j, (s_at, plus, minus) in enumerate(((32, 0, 96), (0, 64, 96), (64, 0, 32))):
                    a, b, at = (j + 1) % 3, (j + 2) % 3, U_AT[1 + j]
                    for r, c, n, k, f in ((j, s_at, CS, 1, 0.5 * S3), (b, plus, CV, 2, 0.5 * S2), (a, minus, CV, 2, -0.5 * S2)):
                        mul(wUg[32 * r:32 * r + 32, at + c:at + c + n], w2col[32 * r:32 * r + 32, k:k + 1], f)
                for ins in sc:
                    ins.then_inc(weights_scaled, 1)
                dve.wait_ge(weights_scaled, len(sc))

            @block.scalar
            def _(act):
                for r in (1, 2, 3):
                    root_of(act, r)
                act.wait_ge(weights_loaded.sem, weights_loaded.n)

                def body(j, new, old):
                    g = j.back(1)
                    if new:
                        keep_turned(act, j, nA, nB, nodes_turned, turned_kept, projected)
                    if old:
                        wait(act, projected, g)
                        nc.scalar.activation(stage[:, bass.ds(g.number(1), 1), :], ps[0:P, 2 + g.b:3 + g.b, 0:2 * D],
                                             ACT.Copy).then_inc(projection_kept.sem, 1)

                node_steps(act, body)

            @block.tensor
            def _(pe):
                pe.wait_ge(consts_made, 5)
                pe.wait_ge(nn_ready, 4)
                pe.wait_ge(weights_loaded.sem, weights_loaded.n)

                def body(j, new, old):
                    g = j.back(1)
                    if new:
                        turn(pe, j, n_tile, nn_taken, nodes_turned, turned_kept)
                    if old:
                        wait(pe, turned_kept, g)
                        wait(pe, projection_kept, g.back(2))
                        o = ps[0:P, 2 + g.b, 0:2 * D]
                        nc.tensor.matmul(o, nA[g.b][:, 0:P], wA, start=True, stop=True)
                        for a in (V2, D + V2):
                            ins = nc.tensor.matmul(o[:, a:a + CV], nB[g.b][0:32, 0:P], wB[0:32, a:a + CV],
                                                   start=False, stop=True, skip_group_check=True)
                        ins.then_inc(projected.sem, 1)

                node_steps(pe, body)

        def steps(eng, body):
            for j in range(3):
                body(Group(0, j))
            with eng.Fori(0, (G - 5) // 2) as i:
                for u in range(2):
                    body(Group(i, u + 3))
            for j in range(G - 2, G + 1):
                body(Group(0, j))

        def halves(j):
            return j.exists(), j.back(1).exists()

        with nc.Block() as block:
            @block.sync
            def _(sp):
                def load_edges(g):
                    b, eds = g.b, edges_loaded.sems[g.b]
                    wait(sp, outer_built, g.back(2))
                    settle(sp, 1)
                    wait(sp, copies_made, g.back(2))
                    wait(sp, nodes_gathered, g.back(2))
                    settle(sp, 1)
                    last = isinstance(g.i, int) and g.off == G - 1
                    n = LEFT if last else T
                    if last:
                        sp.dma_start(e_dst[b][:, n:T], pad_dst[:, n:T]).then_inc(pad_copied, 16)
                        sp.wait_ge(pad_copied, 16)
                    sp.dma_start(e_src[b][:, 0:n], src_v[:, bass.ds(g.number(T), n)], allow_slow_non_contiguous=True).then_inc(eds, 16)
                    sp.dma_start(e_dst[b][:, 0:n], dst_v[:, bass.ds(g.number(T), n)], allow_slow_non_contiguous=True).then_inc(eds, 16)
                    sp.dma_start(e_rbf[b][:, 0:n * NB], rbf_v[:, bass.ds(g.number(T * NB), n * NB)]).then_inc(eds, 16)
                    sp.dma_start(e_y[b][:, 0:n * 4], y_v[:, bass.ds(g.number(T * 4), n * 4)]).then_inc(eds, 16)

                sp.wait_ge(edge_places_cleared, 4)
                for g in range(4):
                    load_edges(Group(0, g))
                with sp.Fori(0, (G - 5) // 2) as i:
                    for u in range(2):
                        load_edges(Group(i, u + 4))
                load_edges(Group(0, G - 1))

            @block.gpsimd
            def _(pool):
                nc.gpsimd.memset(outer[0], 0.0).then_inc(edge_places_cleared, 1)
                nc.gpsimd.memset(outer[1], 0.0).then_inc(edge_places_cleared, 1)
                nc.gpsimd.memset(sg, 0.0).then_inc(edge_places_cleared, 1)
                nc.gpsimd.memset(pad_dst, N).then_inc(edge_places_cleared, 1)
                pool.wait_ge(edge_places_cleared, 4)

                def gather(g, first, last):
                    b = g.b
                    if first == 0:
                        wait(pool, edges_loaded, g)
                        wait(pool, feat_added, g.back(2))
                        settle(pool, 0)
                    for t in range(first, last):
                        nc.gpsimd.indirect_dma_start(g_src[b][:, t * D:(t + 1) * D], None, src_rows,
                                                     bass.IndirectOffsetOnAxis(ap=e_src[b][:, t:t + 1], axis=0)
                                                     ).then_inc(nodes_gathered.sems[b], 16)
                        nc.gpsimd.indirect_dma_start(g_dst[b][:, t * D:(t + 1) * D], None, dst_rows,
                                                     bass.IndirectOffsetOnAxis(ap=e_dst[b][:, t:t + 1], axis=0)
                                                     ).then_inc(nodes_gathered.sems[b], 16)

                def radial(g):
                    b = g.b
                    wait(pool, outer_turned, g.back(2))
                    wait(pool, edges_loaded, g)
                    y = e_y[b].rearrange("p (t c) -> p t c", c=4)
                    for c in range(4):
                        nc.gpsimd.tensor_tensor(outer[b][:, :, NB * c:NB * c + NB],
                                                e_rbf[b].rearrange("p (t r) -> p t r", r=NB),
                                                y[:, :, c:c + 1].broadcast_to([P, T, NB]),
                                                ALU.mult).then_inc(outer_built.sem, 1)

                def read_tables(g):
                    wait(pool, copies_made, g)
                    wait(pool, rows_scattered, g.back(1))
                    settle(pool, 0)
                    for t in range(T):
                        nc.gpsimd.indirect_dma_start(rows[g.b][:, t, :], None, sums[t],
                                                     bass.IndirectOffsetOnAxis(ap=dst_kept[g.b][:, t:t + 1], axis=0)
                                                     ).then_inc(rows_gathered.sems[g.b], 16)

                def write_tables(g):
                    b, rw = g.b, rows[g.b]
                    wait(pool, rows_gathered, g)
                    wait(pool, exp_made, g)
                    for a, n in HEADS + ((D, 1),):
                        v = rw[:, :, a:a + H * n].rearrange("p t (h a) -> p t h a", h=H)
                        nc.gpsimd.tensor_tensor(v, v, scale[:, 0, :, :].unsqueeze(3).broadcast_to([P, T, H, n]),
                                                ALU.mult).then_inc(rows_scaled.sem, 1)
                    wait(pool, rows_added, g)
                    wait(pool, firsts_made, g)
                    settle(pool, 0)
                    for t in range(T):
                        nc.gpsimd.indirect_dma_start(sums[t], bass.IndirectOffsetOnAxis(ap=first[b][:, t:t + 1], axis=0),
                                                     rw[:, t, :], None, bounds_check=N - 1, oob_is_err=False
                                                     ).then_inc(rows_scattered.sems[b], 16)

                def body(m):
                    n = m.ahead(3)
                    if n.exists():
                        gather(n, 0, 1)
                    read_tables(m)
                    if n.exists():
                        gather(n, 1, T)
                        radial(n)
                    write_tables(m)

                for g in range(3):
                    gather(Group(0, g), 0, T)
                    radial(Group(0, g))
                body(Group(0, 0))
                with pool.Fori(0, (G - 5) // 2) as i:
                    for u in range(2):
                        body(Group(i, u + 1))
                for g in range(G - 4, G):
                    body(Group(0, g))
                wait(pool, rows_scattered, Group(0, G - 2))
                wait(pool, rows_scattered, Group(0, G - 1))

            @block.vector
            def _(dve):
                def take(j):
                    wait(dve, edges_loaded, j)
                    wait(dve, d_made, j.back(2))
                    wait(dve, firsts_made, j.back(2))
                    nc.vector.tensor_copy(dst_f[j.b], e_dst[j.b]).then_inc(copies_made.sem, 1)

                def keep_dst(j):
                    wait(dve, rows_gathered, j.back(2))
                    nc.vector.tensor_copy(dst_kept[j.b], e_dst[j.b]).then_inc(copies_made.sem, 1)

                def features(j):
                    b = j.b
                    wait(dve, comb, j.back(2))
                    wait(dve, t0_made, j.back(2))
                    nc.vector.tensor_copy(y_kept[b], e_y[b]).then_inc(copies_made.sem, 1)
                    wait(dve, nodes_gathered, j)
                    wait(dve, f_turned, j.back(1))
                    nc.vector.tensor_tensor(feat[:, :, 0:D], g_src[b].rearrange("p (t c) -> p t c", t=T),
                                            g_dst[b].rearrange("p (t c) -> p t c", t=T),
                                            ALU.add).then_inc(feat_added.sem, 1)

                def same_destination(j):
                    b = j.b
                    wait(dve, d_made, j)
                    wait(dve, sm_made, j.back(2))
                    col = dst_f[b].unsqueeze(2).broadcast_to([P, T, P])
                    nc.vector.tensor_tensor(same[b], ps[0:P, D_BANK, 0:W].rearrange("p (t e) -> p t e", t=T), col,
                                            ALU.is_equal).then_inc(same_made.sem, 1)

                def masks(j):
                    wait(dve, early_counted, j.back(1))
                    wait(dve, same_made, j)
                    nc.vector.tensor_tensor(early, same[j.b], before[:, :].unsqueeze(1).broadcast_to([P, T, P]),
                                            ALU.mult).then_inc(early_made.sem, 1)
                    wait(dve, firsts_made, j.back(1))
                    nc.vector.tensor_scalar(away, dst_f[j.b], -1.0, pcol[:, 0:1], ALU.mult, ALU.add).then_inc(firsts_made.sem, 1)

                def firsts(j, step):
                    if step == 0:
                        wait(dve, early_counted, j)
                        nc.vector.tensor_scalar(cnt, cnt, 0.5, None, ALU.is_gt).then_inc(firsts_made.sem, 1)
                    elif step == 1:
                        wait(dve, firsts_made, j, 1)
                        nc.vector.tensor_tensor(moved, away, cnt, ALU.mult).then_inc(firsts_made.sem, 1)
                    else:
                        wait(dve, firsts_made, j, 2)
                        wait(dve, rows_scattered, j.back(2))
                        nc.vector.tensor_tensor(first[j.b], moved, dst_f[j.b], ALU.add).then_inc(firsts_made.sem, 1)

                def only_same(g, h):
                    wait(dve, a_made, g, h)
                    wait(dve, apart_made, g)
                    if h >= 2:
                        wait(dve, a_max, g, h - 2)
                    else:
                        wait(dve, a_max, g.back(1))
                    nc.vector.tensor_tensor(masked[h % 2], ps[0:P, 6 + h % 2, 0:W].rearrange("p (t e) -> p t e", t=T),
                                            apart[g.b], ALU.add).then_inc(a_masked.sem, 1)

                def largest(g, h):
                    wait(dve, a_masked, g, h)
                    nc.vector.tensor_reduce(gmax[:, :, h], masked[h % 2], AX.X, ALU.max).then_inc(a_max.sem, 1)

                def combine(g, t, c):
                    if c == 0:
                        wait(dve, u_made, g, t)
                        wait(dve, t0_made, g, 4 * t + 3)
                    else:
                        wait(dve, comb, g, SUM_NO[t, c - 1])
                    if c == 1:
                        wait(dve, zeroed, g)
                    at, n = RUNS[c]
                    nc.vector.scalar_tensor_tensor(
                        ht[:, t, at:at + n], ps[0:P, U_BANK[t], U_AT[c]:U_AT[c] + n],
                        y_kept[g.b][:, 4 * t + c:4 * t + c + 1], ht[:, t, at:at + n],
                        ALU.mult, ALU.add).then_inc(comb.sem, 1)

                def product(j, k):
                    wait(dve, l_made, j, k)
                    f = (0, 0, 1, 2, 3)[k]
                    wait(dve, f_kept, j, f)
                    nc.vector.tensor_tensor(prod[k], ps[:, L_BANK[k], 0:W], fT[f], ALU.mult).then_inc(prod_made.sem, 1)

                def new_maxima(g, step):
                    old_max = rows[g.b][:, :, D + H:AC]
                    if step == 0:
                        wait(dve, rows_gathered, g)
                        wait(dve, a_max, g)
                        wait(dve, rows_added, g.back(1))
                        nc.vector.tensor_tensor(newmax, gmax, old_max, ALU.max).then_inc(shift_made.sem, 1)
                    elif step == 1:
                        wait(dve, shift_made, g, 0)
                        wait(dve, exp_made, g.back(1))
                        nc.vector.tensor_tensor(shift[:, 0], old_max, newmax, ALU.subtract).then_inc(shift_made.sem, 1)
                    else:
                        wait(dve, lg_kept, g)
                        nc.vector.tensor_tensor(shift[:, 1], logit, newmax, ALU.subtract).then_inc(shift_made.sem, 1)

                def weigh(g):
                    wait(dve, folded, g)
                    wait(dve, exp_made, g)
                    wait(dve, sm_made, g.back(1))
                    ex = scale[:, 1, :, :]
                    for a, n in HEADS:
                        nc.vector.tensor_tensor(
                            vx[:, :, a:a + H * n].rearrange("p t (h a) -> p t h a", h=H),
                            ht[:, :, a:a + H * n].rearrange("p t (h a) -> p t h a", h=H),
                            ex.unsqueeze(3).broadcast_to([P, T, H, n]), ALU.mult).then_inc(vx_made.sem, 1)
                    nc.vector.tensor_copy(vx[:, :, D:D + H], ex).then_inc(vx_made.sem, 1)

                def add_rows(g):
                    wait(dve, rows_scaled, g)
                    for k in range(2):
                        wait(dve, sm_made, g, k)
                        r = rows[g.b][:, 2 * k:2 * k + 2, 0:D + H]
                        nc.vector.tensor_tensor(r, r, ps[0:P, 6 + k, 0:2 * (D + H)].rearrange("p (t c) -> p t c", t=2),
                                                ALU.add).then_inc(rows_added.sem, 1)
                    wait(dve, shift_made, g)
                    nc.vector.tensor_copy(rows[g.b][:, :, D + H:AC], newmax).then_inc(rows_added.sem, 1)

                def body(j):
                    new, old = halves(j)
                    g, n = j.back(1), j.ahead(1)
                    if n.exists():
                        take(n)
                    if old:
                        only_same(g, 0)
                        only_same(g, 1)
                        largest(g, 0)
                        only_same(g, 2)
                        largest(g, 1)
                        only_same(g, 3)
                        wait(dve, vx_made, g.back(1))
                        nc.vector.memset(ht[:, :, V0:V0 + 2 * CV], 0.0).then_inc(zeroed.sem, 1)
                        largest(g, 2)
                        largest(g, 3)
                    if new:
                        wait(dve, x_made, j.back(1))
                        wait(dve, v_made, j.back(1))
                        for k in range(3):
                            product(j, k)
                    if old:
                        for t, c in SUMS[0:8]:
                            combine(g, t, c)
                    if new:
                        product(j, 3)
                        firsts(j, 0)
                        product(j, 4)
                        firsts(j, 1)
                        firsts(j, 2)
                    if n.exists():
                        keep_dst(n)
                    if old:
                        for t, c in SUMS[8:13]:
                            combine(g, t, c)
                        for k in range(3):
                            new_maxima(g, k)
                            combine(g, *SUMS[13 + k])
                        wait(dve, comb, g)
                        v = ht[:, :, V0:V0 + 2 * CV]
                        nc.vector.tensor_tensor(v, v, ht[:, :, D:HW], ALU.add).then_inc(folded.sem, 1)
                    if n.exists():
                        features(n)
                    if old:
                        weigh(g)
                    if new:
                        wait(dve, tg_made, j)
                        wait(dve, v_made, j)
                        wait(dve, u_made, j.back(1))
                        nc.vector.scalar_tensor_tensor(gv[:, :], tg[:, :], 1.0, ps[0:96, 5, 0:W],
                                                       ALU.add, ALU.mult).then_inc(gv_made.sem, 1)
                    if old:
                        add_rows(g)
                    if n.exists():
                        same_destination(n)
                        masks(n)

                take(Group(0, 0))
                keep_dst(Group(0, 0))
                features(Group(0, 0))
                same_destination(Group(0, 0))
                masks(Group(0, 0))
                steps(dve, body)

            @block.scalar
            def _(act):
                def keep(out_, in_, ev):
                    nc.scalar.activation(out_, in_, ACT.Copy).then_inc(ev.sem, 1)

                def apart_and_count(j):
                    wait(act, same_made, j)
                    wait(act, a_masked, j.back(2))
                    nc.scalar.activation(apart[j.b], same[j.b], ACT.Copy, scale=-LOW, bias=LOW).then_inc(apart_made.sem, 1)
                    wait(act, early_made, j)
                    wait(act, firsts_made, j.back(1), 2)
                    for t in range(T):
                        nc.scalar.activation(early[:, t, :], early[:, t, :], ACT.Copy,
                                             accum_out=cnt[:, t:t + 1]).then_inc(early_counted.sem, 1)

                def double(j):
                    wait(act, feat_added, j)
                    wait(act, f_turned, j.back(1))
                    keep(feat[:, :, D:D + 64], feat[:, :, V0:V0 + 64], feat_dup)
                    keep(feat[:, :, D + 64:D + 96], feat[:, :, V2:V2 + 32], feat_dup)

                act.wait_ge(edge_places_cleared, 4)

                def body(j):
                    new, old = halves(j)
                    g = j.back(1)
                    if new:
                        wait(act, outer_turned, j)
                        wait(act, l_made, j.back(1))
                        keep(oT, ps[:, O_BANK, 0:W], outer_kept)
                        for k in range(4):
                            wait(act, f_turned, j, k)
                            wait(act, prod_made, j.back(1))
                            keep(fT[k], ps[:, F_BANK[k], 0:W], f_kept)
                    if old:
                        wait(act, vx_made, g.back(1))
                        wait(act, us_made, g)
                        for t in range(T):
                            for c, to, at, n in ((0, SC, 0, CS), (1, D, CS, CV), (2, D + CV, CS, CV), (3, V2, CS, CV)):
                                nc.scalar.activation(ht[:, t, to:to + n], ps[0:P, 2, t * 96 + at:t * 96 + at + n], ACT.Copy,
                                                     scale=y_kept[g.b][:, 4 * t + c:4 * t + c + 1]).then_inc(t0_made.sem, 1)
                    if new:
                        apart_and_count(j)
                        wait(act, x_made, j)
                        wait(act, lg_made, j.back(1))
                        wait(act, g_made, j.back(1))
                        wait(act, sg_made, j.back(1))
                        keep(xv[64:128, :], ps[64:128, 2, 0:W], xv_kept)
                    if old:
                        wait(act, shift_made, g)
                        wait(act, rows_scaled, g.back(1))
                        nc.scalar.activation(scale, shift, ACT.Exp).then_inc(exp_made.sem, 1)
                    if new:
                        keep(rl[0:64, :], ps[0:64, 2, 0:W], xv_kept)
                        nc.scalar.activation(rl[64:128, :], ps[0:64, 2, 0:W], ACT.Relu).then_inc(xv_kept.sem, 1)
                        wait(act, xv_kept, j, 0)
                        wait(act, us_made, j.back(1))
                        nc.scalar.activation(sg[64:128, :], xv[64:128, :], ACT.Tanh, scale=0.5).then_inc(sg_made.sem, 1)
                        wait(act, g_made, j)
                        wait(act, gv_made, j.back(1))
                        nc.scalar.activation(tg[:, :], ps[0:96, 6, 0:W], ACT.Tanh, scale=0.5).then_inc(tg_made.sem, 1)
                        wait(act, lg_made, j)
                        wait(act, shift_made, j.back(1))
                        wait(act, a_made, j.back(1))
                        keep(logit, ps[0:P, 7, 0:T * H].rearrange("p (t h) -> p t h", t=T), lg_kept)
                        wait(act, sg_made, j, 0)
                        nc.scalar.activation(sg[64:128, :], sg[64:128, :], ACT.Copy, bias=1.0).then_inc(sg_made.sem, 1)
                    if j.ahead(1).exists():
                        double(j.ahead(1))

                double(Group(0, 0))
                steps(act, body)

            @block.tensor
            def _(pe):
                tr = nc.tensor.transpose
                mm = nc.tensor.matmul
                idP = ident[0:P, 0:P]

                def destinations(j):
                    wait(pe, copies_made, j, 0)
                    wait(pe, prod_made, j.back(1), 1)
                    for t in range(T):
                        ins = tr(ps[0:P, D_BANK, t * P:(t + 1) * P],
                                 dst_f[j.b][:, t:t + 1].broadcast_to([P, P]), idP)
                    ins.then_inc(d_made.sem, 1)

                def over_edges(g, h):
                    bank = 6 + h % 2
                    if h >= 2:
                        wait(pe, a_masked, g, h - 2)
                    else:
                        if h == 0:
                            wait(pe, lg_kept, g)
                        wait(pe, rows_added, g.back(1), h)
                    for t in range(T):
                        ins = tr(ps[0:P, bank, t * P:(t + 1) * P], logit[:, t, h:h + 1].broadcast_to([P, P]), idP)
                    ins.then_inc(a_made.sem, 1)

                def weights_of(j, k):
                    if k == 0:
                        wait(pe, gv_made, j.back(1))
                    elif k < 3:
                        wait(pe, f_kept, j, 1 + k)
                    else:
                        wait(pe, prod_made, j, (0, 2)[k - 3])
                    mm(ps[:, L_BANK[k], 0:W], wL[k], oT, start=True, stop=True).then_inc(l_made.sem, 1)

                def scalars_terms(g):
                    wait(pe, sg_made, g)
                    for t in range(T):
                        ins = mm(ps[0:P, 2, t * 96:(t + 1) * 96], sg[:, t * P:(t + 1) * P], wUs, start=True, stop=True)
                    ins.then_inc(us_made.sem, 1)

                def vectors_terms(g, t):
                    if t == 0:
                        wait(pe, gv_made, g)
                        wait(pe, comb, g.back(1))
                    if t >= 2:
                        wait(pe, comb, g, SUM_NO[t - 2, 3])
                    mm(ps[0:P, U_BANK[t], 0:UW], gv[:, t * P:(t + 1) * P], wUg[0:96, :], start=True, stop=True).then_inc(u_made.sem, 1)

                def body(j):
                    new, old = halves(j)
                    g = j.back(1)
                    if new:
                        wait(pe, outer_built, j)
                        wait(pe, prod_made, j.back(1))
                        for t in range(T):
                            ins = tr(ps[:, O_BANK, t * P:(t + 1) * P], outer[j.b][:, t, :], idP)
                        ins.then_inc(outer_turned.sem, 1)
                    if old:
                        over_edges(g, 0)
                        over_edges(g, 1)
                    if new:
                        wait(pe, feat_added, j)
                        for k, a in enumerate((0, 32, 64, 128)):
                            if k == 2 and old:
                                scalars_terms(g)
                            if k == 0:
                                wait(pe, same_made, j)
                            elif k == 1:
                                wait(pe, outer_kept, j)
                            else:
                                wait(pe, f_kept, j, k - 2)
                            if k == 2:
                                wait(pe, feat_dup, j)
                            for t in range(T):
                                ins = tr(ps[:, F_BANK[k], t * P:(t + 1) * P], feat[:, t, a:a + 128], idP)
                            ins.then_inc(f_turned.sem, 1)
                    elif old:
                        scalars_terms(g)
                    if old:
                        over_edges(g, 2)
                    if new:
                        wait(pe, outer_kept, j)
                        weights_of(j, 0)
                    if old:
                        over_edges(g, 3)
                    if new:
                        weights_of(j, 1)
                        weights_of(j, 2)
                    if old:
                        vectors_terms(g, 0)
                        vectors_terms(g, 1)
                    if new:
                        weights_of(j, 3)
                        weights_of(j, 4)
                    if j.ahead(1).exists():
                        destinations(j.ahead(1))
                    if old:
                        vectors_terms(g, 2)
                        vectors_terms(g, 3)
                    if new:
                        wait(pe, t0_made, j.back(1))
                        wait(pe, prod_made, j)
                        mm(ps[:, 2, 0:W], wX0, prod[0], start=True, stop=False)
                        mm(ps[:, 2, 0:W], wX4, prod[4], start=False, stop=True).then_inc(x_made.sem, 1)
                        mm(ps[0:96, 5, 0:W], wV4, prod[4], start=True, stop=True)
                        for k in range(3):
                            ins = mm(ps[32 * k:32 * k + 32, 5, 0:W], wV[k], prod[1 + k], start=False, stop=True,
                                     skip_group_check=True)
                        ins.then_inc(v_made.sem, 1)
                        wait(pe, xv_kept, j, 0)
                        wait(pe, a_masked, j.back(1))
                        mm(ps[0:96, 6, 0:W], wG[64:128, :], xv[64:128, :], start=True, stop=True).then_inc(g_made.sem, 1)
                        wait(pe, xv_kept, j)
                        for t in range(T):
                            ins = mm(ps[0:P, 7, t * H:(t + 1) * H], rl[:, t * P:(t + 1) * P], wLr, start=True, stop=True)
                        ins.then_inc(lg_made.sem, 1)
                    if old:
                        wait(pe, vx_made, g)
                        for k in range(2):
                            if new:
                                wait(pe, *((tg_made, j), (lg_kept, j))[k])
                            else:
                                wait(pe, a_masked, g, 2 + k)
                            for t in range(2):
                                ins = mm(ps[0:P, 6 + k, t * (D + H):(t + 1) * (D + H)], same[g.b][:, 2 * k + t, :],
                                         vx[:, 2 * k + t, :], start=True, stop=True)
                            ins.then_inc(sm_made.sem, 1)

                pe.wait_ge(edge_places_cleared, 4)
                destinations(Group(0, 0))
                steps(pe, body)

        cut["at"] = 0
        tabs = [part(NT * AC)[0:P].rearrange("p (j c) -> p j c", j=NT) for _ in range(T)]
        top = part(NT * H)[0:P].rearrange("p (j h) -> p j h", j=NT)
        nn3 = part(NT * D)[0:P].rearrange("p (j c) -> p j c", j=NT)
        stage3 = part(2 * PW)[0:P].rearrange("p (j c) -> p j c", j=2)
        a_tile = [part(D)[0:P] for _ in range(2)]
        aA, aB = [part(128) for _ in range(2)], [part(128) for _ in range(2)]
        w3_at = cut["at"]
        wPs, wPv = part(D), part(D)
        wMA, wMB = part(PW), part(PW)
        w3_end = cut["at"]
        zeros = part(26 * D)[0:P]
        total = tabs[0][:, 0:NT, :]
        scratch = tabs[1][:, 0:NT, 0:D]
        weights3_loaded = Count(sem("weights3_loaded"), 16)
        cleared3, scaled3 = sem("cleared3"), sem("scaled3")
        tabs_loaded = sem("tabs_loaded")
        dve3 = sem("dve3")
        tab_shift, tab_exp = sem("tab_shift"), sem("tab_exp")
        agg_ready, h1_ready = sem("agg_ready"), sem("h1_ready")
        agg_taken, agg_turned, agg_kept = event("agg_taken"), event("agg_turned", 2), event("agg_kept", 2)
        out_made, out_kept = event("out_made"), event("out_kept", 2)
        h1_taken, h1_turned, h1_kept = event("h1_taken"), event("h1_turned", 2), event("h1_kept", 2)
        proj_made, proj_kept, proj_stored = event("proj_made"), event("proj_kept", 2), pair("proj_stored", 16)
        aggs_cleared = sem("aggs_cleared")
        stat3 = part(8 * NT)[0:P].rearrange("p (k j) -> p k j", k=8)
        var3, std3 = sem("var3"), sem("std3")

        P_ONE, P_DIST, P_DIR, P_VEC = 0, D, 2 * D, 2 * D + 3 * CS

        with nc.Block() as block:
            @block.sync
            def _(sp):
                for k in range(T):
                    sp.dma_start(tabs[k], sums[k][0:N, :].rearrange("(p j) c -> p j c", p=P)).then_inc(tabs_loaded, 16)
                sp.wait_ge(cleared3, 2)
                ld = lambda a, b: weights3_loaded(sp.dma_start(a, b, allow_slow_non_contiguous=True))
                ld(wPs[SC:SC + CS, 0:CS], w["Wps"])
                for k, (t, r) in enumerate(((wPs, V0), (wPs, V1), (wPv, 0))):
                    ld(t[r:r + CV, CS + k * CV:CS + (k + 1) * CV], w["Wpv"])
                m = {n: w[n].rearrange("u o w -> (u o) w") for n in ("wm000", "wm011", "wm101", "wm110")}
                ld(wMA[SC:SC + CS, P_ONE:P_ONE + CS], w["lm0"])
                ld(wMA[SC:SC + CS, P_DIST:P_DIST + CS], m["wm000"])
                ld(wMA[SC:SC + CS, P_VEC:P_VEC + CV], m["wm011"])
                for k, (t, r) in enumerate(((wMA, V0), (wMA, V1), (wMB, 0))):
                    ld(t[r:r + CV, P_ONE + CS + k * CV:P_ONE + CS + (k + 1) * CV], w["lm1"])
                    ld(t[r:r + CV, P_DIST + CS + k * CV:P_DIST + CS + (k + 1) * CV], m["wm101"])
                    ld(t[r:r + CV, P_DIR + k * CS:P_DIR + (k + 1) * CS], m["wm110"])
                for k in range(T):
                    sp.dma_start(aggs[k].rearrange("(p j) c -> p (j c)", p=P), zeros).then_inc(aggs_cleared, 16)
                rows_v = proj_rows.rearrange("(p j) c -> p j c", p=P)

                def store(j, new, old):
                    g = j.back(1)
                    if old:
                        wait(sp, proj_kept, g)
                        settle(sp, 1)
                        sp.dma_start(rows_v[:, bass.ds(g.number(1), 1), :], stage3[:, g.b:g.b + 1, :]
                                     ).then_inc(proj_stored.sems[g.b], 16)

                node_steps(sp, store)
                wait(sp, proj_stored, Group(0, NT - 2))
                wait(sp, proj_stored, Group(0, NT - 1))
                sp.wait_ge(aggs_cleared, 16 * T)
                sp.wait_ge(weights3_loaded.sem, weights3_loaded.n)

            @block.gpsimd
            def _(pool):
                nc.gpsimd.memset(room[:, w3_at:w3_end], 0.0).then_inc(cleared3, 1)
                nc.gpsimd.memset(zeros, 0.0).then_inc(cleared3, 1)
                pool.wait_ge(agg_ready, 1)
                take_tiles(pool, a_tile, nn3, agg_taken, agg_turned)
                pool.wait_ge(h1_ready, 4)
                pool.wait_ge(agg_turned.sem, 2 * NT)
                take_tiles(pool, a_tile, nn3, h1_taken, h1_turned)

            @block.vector
            def _(dve):
                dv = Count(dve3)
                dve.wait_ge(tabs_loaded, 16 * T)
                mx = [tabs[k][:, 0:NT, D + H:AC] for k in range(T)]
                dv(nc.vector.tensor_tensor(top, mx[0], mx[1], ALU.max))
                for k in (2, 3):
                    dv.wait(dve)
                    dv(nc.vector.tensor_tensor(top, top, mx[k], ALU.max))
                dv.wait(dve)
                for k in range(T):
                    nc.vector.tensor_tensor(mx[k], mx[k], top, ALU.subtract).then_inc(tab_shift, 1)
                dve.wait_ge(tab_exp, T)
                for k in range(T):
                    for h in range(H):
                        f = tabs[k][:, 0:NT, D + H + h:D + H + h + 1]
                        for a, n in HEADS + ((D, 1),):
                            v = tabs[k][:, 0:NT, a + h * n:a + (h + 1) * n]
                            dv(nc.vector.tensor_tensor(v, v, f.broadcast_to([P, NT, n]), ALU.mult))
                dv.wait(dve)
                for k in range(1, T):
                    dv(nc.vector.tensor_tensor(total[:, :, 0:D + H], total[:, :, 0:D + H], tabs[k][:, 0:NT, 0:D + H], ALU.add))
                    dv.wait(dve)
                den = total[:, :, D:D + H]
                dv(nc.vector.tensor_scalar(den, den, 1e-16, None, ALU.add))
                dv.wait(dve)
                dv(nc.vector.reciprocal(top, den))
                dv.wait(dve)
                for h in range(H):
                    f = top[:, :, h:h + 1]
                    for a, n in HEADS:
                        v = total[:, :, a + h * n:a + (h + 1) * n]
                        dv(nc.vector.tensor_tensor(v, v, f.broadcast_to([P, NT, n]), ALU.mult))
                dv.wait(dve)
                nc.vector.tensor_copy(nn3, total[:, :, 0:D]).then_inc(agg_ready, 1)
                dv(nc.vector.tensor_tensor(xs[:, :, :], xs[:, :, :], hs[:, :, :], ALU.add))
                dv.wait(dve)

                def add_out(j, new, old):
                    g = j.back(1)
                    if old:
                        wait(dve, out_made, g)
                        row, made = xs[:, bass.ds(g.number(1), 1), :], ps[0:P, 4 + g.b:5 + g.b, :]
                        s = row[:, :, 0:CS]
                        nc.vector.tensor_tensor(s, s, made[:, :, 0:CS], ALU.add).then_inc(out_kept.sem, 1)
                        v = row[:, :, CS:D].rearrange("p o (c k) -> p (o k) c", k=3)
                        nc.vector.tensor_tensor(v, v, made[:, :, CS:D].rearrange("p o (k c) -> p (o k) c", k=3),
                                                ALU.add).then_inc(out_kept.sem, 1)

                node_steps(dve, add_out)
                dve.wait_ge(out_kept.sem, 2 * NT)
                dve.wait_ge(agg_taken.sem, NT)
                norm(dve, dv, xs[:, :, :], hs[:, :, :], D, 1, True, stat3, scratch, var3, std3)
                nc.vector.tensor_copy(nn3[:, :, SC:SC + CS], hs[:, :, 0:CS]).then_inc(h1_ready, 1)
                for o, i in to_rows(nn3, hs[:, :, CS:D]):
                    nc.vector.tensor_copy(o, i).then_inc(h1_ready, 1)
                dve.wait_ge(weights3_loaded.sem, weights3_loaded.n)
                nc.vector.tensor_scalar(wMA[0:64, P_ONE:P_ONE + D], wMA[0:64, P_ONE:P_ONE + D], 32.0 ** -0.5, None, ALU.mult).then_inc(scaled3, 1)
                nc.vector.tensor_scalar(wMA[64:128, P_ONE:P_ONE + D], wMA[64:128, P_ONE:P_ONE + D], 0.125, None, ALU.mult).then_inc(scaled3, 1)
                nc.vector.tensor_scalar(wMB[0:32, P_ONE:P_ONE + D], wMB[0:32, P_ONE:P_ONE + D], 32.0 ** -0.5, None, ALU.mult).then_inc(scaled3, 1)
                for t, n in ((wMA, 128), (wMB, 32)):
                    for a, b, f in ((P_DIST, P_DIR, R96), (P_DIR, P_VEC, R96 * S3), (P_VEC, PW, R96)):
                        nc.vector.tensor_scalar(t[0:n, a:b], t[0:n, a:b], f, None, ALU.mult).then_inc(scaled3, 1)

            @block.scalar
            def _(act):
                act.wait_ge(tab_shift, T)
                for k in range(T):
                    m = tabs[k][:, 0:NT, D + H:AC]
                    nc.scalar.activation(m, m, ACT.Exp).then_inc(tab_exp, 1)
                def turn_sums(j, new, old):
                    if new:
                        keep_turned(act, j, aA, aB, agg_turned, agg_kept, out_made)

                node_steps(act, turn_sums)
                act.wait_ge(out_made.sem, NT)
                act.wait_ge(var3, 1)
                nc.scalar.activation(stat3[:, 4, :], stat3[:, 3, :], ACT.Sqrt).then_inc(std3, 1)
                def keep_projections(j, new, old):
                    g = j.back(1)
                    if new:
                        keep_turned(act, j, aA, aB, h1_turned, h1_kept, proj_made)
                    if old:
                        wait(act, proj_made, g)
                        wait(act, proj_stored, g.back(2))
                        nc.scalar.activation(stage3[:, g.b, 0:320], ps[0:P, 4 + 2 * g.b, 0:320], ACT.Copy).then_inc(proj_kept.sem, 1)
                        nc.scalar.activation(stage3[:, g.b, 320:PW], ps[0:P, 5 + 2 * g.b, 0:PW - 320], ACT.Copy
                                             ).then_inc(proj_kept.sem, 1)

                node_steps(act, keep_projections)

            @block.tensor
            def _(pe):
                pe.wait_ge(agg_ready, 1)
                pe.wait_ge(weights3_loaded.sem, weights3_loaded.n)

                def output(j, new, old):
                    g = j.back(1)
                    if new:
                        turn(pe, j, a_tile, agg_taken, agg_turned, agg_kept)
                    if old:
                        wait(pe, agg_kept, g)
                        wait(pe, out_kept, g.back(2))
                        o = ps[0:P, 4 + g.b, 0:D]
                        nc.tensor.matmul(o, aA[g.b][:, 0:P], wPs, start=True, stop=True)
                        nc.tensor.matmul(o[:, D - CV:D], aB[g.b][0:32, 0:P], wPv[0:32, D - CV:D], start=False, stop=True,
                                         skip_group_check=True).then_inc(out_made.sem, 1)

                node_steps(pe, output)
                pe.wait_ge(scaled3, 9)
                pe.wait_ge(out_kept.sem, 2 * NT)
                pe.wait_ge(agg_kept.sem, 2 * NT)

                def projections(j, new, old):
                    g = j.back(1)
                    if new:
                        turn(pe, j, a_tile, h1_taken, h1_turned, h1_kept)
                    if old:
                        wait(pe, h1_kept, g)
                        wait(pe, proj_kept, g.back(2))
                        for k, (a, e, thirds) in enumerate(((0, 320, ((P_ONE + D - CV, CV), (P_DIST + D - CV, CV))),
                                                            (320, PW, ((P_DIR + 2 * CS, CS),)))):
                            o = ps[0:P, 4 + 2 * g.b + k, 0:e - a]
                            nc.tensor.matmul(o, aA[g.b][:, 0:P], wMA[:, a:e], start=True, stop=True)
                            for c, n in thirds:
                                last = nc.tensor.matmul(o[:, c - a:c - a + n], aB[g.b][0:32, 0:P], wMB[0:32, c:c + n],
                                                        start=False, stop=True, skip_group_check=True)
                        last.then_inc(proj_made.sem, 1)

                node_steps(pe, projections)

        cut["at"] = 0
        m_src = [part(T, I32)[0:P] for _ in range(2)]
        m_first = [part(T, I32)[0:P] for _ in range(2)]
        m_early = part(W)[0:P].rearrange("p (t e) -> p t e", t=T)
        m_cnt, m_away, m_moved = part(T)[0:P], part(T)[0:P], part(T)[0:P]
        m_dst = [part(T, I32)[0:P] for _ in range(2)]
        m_y = [part(T * 4)[0:P] for _ in range(2)]
        m_src_f = [part(T)[0:P] for _ in range(2)]
        m_pad = part(T, I32)[0:P]
        m_rows = [part(T * PW)[0:P].rearrange("p (t c) -> p t c", t=T) for _ in range(2)]
        m_same = [part(W)[0:P].rearrange("p (t e) -> p t e", t=T) for _ in range(2)]
        m_edge = [part(T * D)[0:P].rearrange("p (t c) -> p t c", t=T) for _ in range(2)]
        m_vec = part(T * 3 * CV)[0:P].rearrange("p (t k c) -> p t k c", t=T, k=3)
        m_msg = [part(T * D)[0:P].rearrange("p (t c) -> p t c", t=T) for _ in range(2)]
        m_loaded = pair("m_loaded", 48)
        m_gathered, m_scattered = pair("m_gathered", 16 * T), pair("m_scattered", 16 * T)
        m_pad_made, m_pad_copied = sem("m_pad_made"), sem("m_pad_copied")
        m_copied, m_turned, m_masked = event("m_copied"), event("m_turned"), event("m_masked")
        m_early_made, m_counted, m_firsts_made = event("m_early_made"), event("m_counted"), event("m_firsts_made", 4)
        m_combined = event("m_combined", 4 * T + 2)
        m_summed, m_kept = event("m_summed", 2), event("m_kept", 2)

        with nc.Block() as block:
            @block.sync
            def _(sp):
                def load(g):
                    b, eds = g.b, m_loaded.sems[g.b]
                    wait(sp, m_copied, g.back(2))
                    settle(sp, 1)
                    wait(sp, m_combined, g.back(2))
                    settle(sp, 1)
                    wait(sp, m_gathered, g.back(2))
                    settle(sp, 1)
                    last = isinstance(g.i, int) and g.off == G - 1
                    n = LEFT if last else T
                    if last:
                        sp.dma_start(m_src[b][:, n:T], m_pad[:, n:T]).then_inc(m_pad_copied, 16)
                        sp.wait_ge(m_pad_copied, 16)
                    sp.dma_start(m_src[b][:, 0:n], src_v[:, bass.ds(g.number(T), n)], allow_slow_non_contiguous=True).then_inc(eds, 16)
                    sp.dma_start(m_dst[b][:, 0:n], dst_v[:, bass.ds(g.number(T), n)], allow_slow_non_contiguous=True).then_inc(eds, 16)
                    sp.dma_start(m_y[b][:, 0:n * 4], y_v[:, bass.ds(g.number(T * 4), n * 4)]).then_inc(eds, 16)

                sp.wait_ge(m_pad_made, 1)
                for g in range(2):
                    load(Group(0, g))
                with sp.Fori(0, (G - 3) // 2) as i:
                    for u in range(2):
                        load(Group(i, u + 2))
                load(Group(0, G - 1))

            @block.gpsimd
            def _(pool):
                nc.gpsimd.memset(m_pad, N).then_inc(m_pad_made, 1)

                def gather(g):
                    b = g.b
                    wait(pool, m_loaded, g)
                    wait(pool, m_combined, g.back(2))
                    settle(pool, 0)
                    for t in range(T):
                        nc.gpsimd.indirect_dma_start(m_rows[b][:, t, :], None, proj_rows,
                                                     bass.IndirectOffsetOnAxis(ap=m_dst[b][:, t:t + 1], axis=0)
                                                     ).then_inc(m_gathered.sems[b], 16)

                def add(g):
                    b = g.b
                    wait(pool, m_kept, g)
                    wait(pool, m_firsts_made, g)
                    wait(pool, m_scattered, g.back(1))
                    settle(pool, 0)
                    for t in range(T):
                        nc.gpsimd.indirect_dma_start(aggs[t], bass.IndirectOffsetOnAxis(ap=m_first[b][:, t:t + 1], axis=0),
                                                     m_msg[b][:, t, :], None, compute_op=ALU.add
                                                     ).then_inc(m_scattered.sems[b], 16)

                gather(Group(0, 0))
                gather(Group(0, 1))
                gather(Group(0, 2))
                add(Group(0, 0))
                with pool.Fori(0, (G - 3) // 2) as i:
                    for u in range(2):
                        gather(Group(i, u + 3))
                        add(Group(i, u + 1))
                for g in range(G - 2, G):
                    add(Group(0, g))
                wait(pool, m_scattered, Group(0, G - 2))
                wait(pool, m_scattered, Group(0, G - 1))

            @block.vector
            def _(dve):
                def copy_src(j):
                    b = j.b
                    wait(dve, m_loaded, j)
                    wait(dve, m_turned, j.back(2))
                    wait(dve, m_firsts_made, j.back(2))
                    nc.vector.tensor_copy(m_src_f[b], m_src[b]).then_inc(m_copied.sem, 1)

                def masks(j):
                    b = j.b
                    wait(dve, m_turned, j)
                    wait(dve, m_copied, j)
                    wait(dve, m_summed, j.back(2))
                    wait(dve, m_early_made, j.back(2))
                    nc.vector.tensor_tensor(m_same[b], ps[0:P, b, 0:W].rearrange("p (t e) -> p t e", t=T),
                                            m_src_f[b].unsqueeze(2).broadcast_to([P, T, P]), ALU.is_equal).then_inc(m_masked.sem, 1)
                    wait(dve, m_firsts_made, j.back(1))
                    nc.vector.tensor_scalar(m_away, m_src_f[b], -1.0, pcol[:, 0:1], ALU.mult, ALU.add).then_inc(m_firsts_made.sem, 1)
                    wait(dve, m_masked, j)
                    wait(dve, m_counted, j.back(1))
                    nc.vector.tensor_tensor(m_early, m_same[b], before[:, :].unsqueeze(1).broadcast_to([P, T, P]),
                                            ALU.mult).then_inc(m_early_made.sem, 1)
                    wait(dve, m_early_made, j)
                    nc.vector.tensor_reduce(m_cnt, m_early, AX.X, ALU.add).then_inc(m_counted.sem, 1)
                    wait(dve, m_counted, j)
                    nc.vector.tensor_scalar(m_cnt, m_cnt, 0.5, None, ALU.is_gt).then_inc(m_firsts_made.sem, 1)
                    wait(dve, m_firsts_made, j, 1)
                    nc.vector.tensor_tensor(m_moved, m_away, m_cnt, ALU.mult).then_inc(m_firsts_made.sem, 1)

                def table_rows(j):
                    wait(dve, m_firsts_made, j, 2)
                    wait(dve, m_scattered, j.back(2))
                    nc.vector.tensor_tensor(m_first[j.b], m_moved, m_src_f[j.b], ALU.add).then_inc(m_firsts_made.sem, 1)

                def messages(g):
                    b = g.b
                    y, r, o = m_y[b], m_rows[b], m_edge[b]
                    wait(dve, m_gathered, g)
                    wait(dve, m_summed, g.back(2))
                    for t in range(T):
                        nc.vector.scalar_tensor_tensor(o[:, t, :], r[:, t, P_DIST:P_DIST + D], y[:, 4 * t + 3:4 * t + 4],
                                                       r[:, t, P_ONE:P_ONE + D], ALU.mult, ALU.add).then_inc(m_combined.sem, 1)
                    wait(dve, m_combined, g.back(1))
                    nc.vector.tensor_tensor(m_vec, r[:, :, P_VEC:PW].unsqueeze(2).broadcast_to([P, T, 3, CV]),
                                            y.rearrange("p (t c) -> p t c", c=4)[:, :, 0:3].unsqueeze(3).broadcast_to([P, T, 3, CV]),
                                            ALU.mult).then_inc(m_combined.sem, 1)
                    for k in range(3):
                        for t in range(T):
                            wait(dve, m_combined, g, t if k == 0 else T + 1 + T * (k - 1) + t)
                            v = o[:, t, 0:CS]
                            nc.vector.scalar_tensor_tensor(v, r[:, t, P_DIR + k * CS:P_DIR + (k + 1) * CS],
                                                           y[:, 4 * t + k:4 * t + k + 1], v, ALU.mult, ALU.add
                                                           ).then_inc(m_combined.sem, 1)
                    v = o[:, :, CS:D].rearrange("p t (k c) -> p t k c", k=3)
                    nc.vector.tensor_tensor(v, v, m_vec, ALU.add).then_inc(m_combined.sem, 1)

                def body(j):
                    new, old = halves(j)
                    if new:
                        copy_src(j)
                    if old:
                        messages(j.back(1))
                        table_rows(j.back(1))
                    if new:
                        masks(j)

                steps(dve, body)

            @block.tensor
            def _(pe):
                def body(j):
                    new, old = halves(j)
                    if new:
                        wait(pe, m_copied, j)
                        wait(pe, m_masked, j.back(2))
                        for t in range(T):
                            ins = nc.tensor.transpose(ps[0:P, j.b, t * P:(t + 1) * P],
                                                      m_src_f[j.b][:, t:t + 1].broadcast_to([P, P]), ident[0:P, 0:P])
                        ins.then_inc(m_turned.sem, 1)
                    if old:
                        g = j.back(1)
                        b = g.b
                        wait(pe, m_masked, g)
                        wait(pe, m_combined, g)
                        for t in range(T):
                            if t % 2 == 0:
                                wait(pe, m_kept, g.back(2), t // 2)
                            ins = nc.tensor.matmul(ps[0:P, 2 + 2 * b + t // 2, (t % 2) * D:(t % 2 + 1) * D],
                                                   m_same[b][:, t, :], m_edge[b][:, t, :], start=True, stop=True)
                            if t % 2:
                                ins.then_inc(m_summed.sem, 1)

                steps(pe, body)

            @block.scalar
            def _(act):
                def body(j):
                    new, old = halves(j)
                    if not old:
                        return
                    g = j.back(1)
                    wait(act, m_scattered, g.back(2))
                    for k in range(2):
                        wait(act, m_summed, g, k)
                        nc.scalar.activation(m_msg[g.b][:, 2 * k:2 * k + 2, :],
                                             ps[0:P, 2 + 2 * g.b + k, 0:2 * D].rearrange("p (t c) -> p t c", t=2),
                                             ACT.Copy).then_inc(m_kept.sem, 1)

                steps(act, body)

        cut["at"] = 0
        Q0, Q1 = CS * CS, CV * CV
        CHUNKS = (Q0 + Q1) // 128
        QUADS = CHUNKS // 4
        YW = 2 * CV * CV
        x0a0 = part(NT * 2 * CS)[0:P].rearrange("p (j c) -> p j c", j=NT)
        a1x1 = part(NT * 6 * CV)[0:P].rearrange("p (j k c) -> p j k c", j=NT, k=3)
        x1 = part(NT * 3 * CV)[0:P].rearrange("p (j c) -> p j c", j=NT)
        w5_at = cut["at"]
        wQ, wY = part(CHUNKS * CS), part(YW)
        wLA, wLB = part(D), part(D)
        w5_end = cut["at"]
        both = part(CS)
        outs = part(NT * D)[0:P].rearrange("p (j c) -> p j c", j=NT)
        slots = part(NT * 3 * CV)[0:P].rearrange("p (j k w) -> p j k w", j=NT, k=3)
        catT, x1T, sumT = part(P), part(P), part(P)
        cat_tile, x1_tile = part(2 * CS)[0:P], part(3 * CV)[0:P]
        qT = [part(W) for _ in range(3)]
        tabs_at = cut["at"]
        q = part(Q0 + Q1)[0:P]
        q_part = [part(Q1)[0:P] for _ in range(2)]
        zbuf = [part(YW)[0:P] for _ in range(2)]
        cut["at"] = tabs_at
        tab5 = [part(NT * D)[0:P].rearrange("p (j c) -> p j c", j=NT) for _ in range(T)]
        cleared5, scaled5, aggs_loaded = sem("cleared5"), sem("scaled5"), sem("aggs_loaded")
        weights5_loaded = Count(sem("weights5_loaded"), 16)
        dve5, x_copied, both_made, cats_made = sem("dve5"), sem("x_copied"), sem("both_made"), sem("cats_made")
        tile_taken = event("tile_taken", 2)
        cat_turned, cat_kept, y_made = event("cat_turned", 2), event("cat_kept", 2), event("y_made")
        q000_made, q_started, q_rest, q110_made = event("q000_made", 2), event("q_started"), event("q_rest", 3), event("q110_made")
        q_turned, q_kept, q_used = event("q_turned", QUADS), event("q_kept", QUADS), event("q_used", QUADS)
        sum_kept, tile_made, tile_kept = event("sum_kept"), event("tile_made"), event("tile_kept")
        z_made, z_halved, z_summed = event("z_made", 3), event("z_halved", 3), event("z_summed", 3)
        stored = sem("stored")

        def tiles(eng, body):
            body(Group(0, 0, 1))
            with eng.Fori(0, NT - 1) as i:
                body(Group(i, 1, 1))

        def of(array, j, *at):
            v = array[(slice(None), bass.ds(j.number(1), 1)) + at]
            return v.rearrange("p o c -> p (o c)")

        def outer_product(left, right):
            m, n = left.shape[-1], right.shape[-1]
            return left.unsqueeze(2).broadcast_to([P, m, n]), right.unsqueeze(1).broadcast_to([P, m, n])

        with nc.Block() as block:
            @block.sync
            def _(sp):
                for k in range(T):
                    sp.dma_start(tab5[k], aggs[k][0:N, :].rearrange("(p j) c -> p j c", p=P)).then_inc(aggs_loaded, 16)
                sp.wait_ge(cleared5, 1)
                ld = lambda a, b: weights5_loaded(sp.dma_start(a, b, allow_slow_non_contiguous=True))
                for name, at, n, v in (("wu000", 0, Q0 // 128, CS), ("wu110", Q0 // 128, Q1 // 128, CV)):
                    us = w[name].rearrange("(c a) v w -> a v c w", a=128 // v)
                    for k in range(128 // v):
                        ld(wQ[k * v:(k + 1) * v, at * CS:(at + n) * CS].rearrange("p (c w) -> p c w", c=n), us[k])
                ld(wY[0:CS, 0:YW // 2], w["wu011"].rearrange("u v w -> u (v w)"))
                ld(wY[CS:2 * CS, YW // 2:YW].rearrange("p (u w) -> p u w", u=CV), w["wu101"].rearrange("u v w -> v u w"))
                ld(wLA[0:CS, 0:CS], w["lu0"])
                for k in range(3):
                    ld(wLB[k * CV:(k + 1) * CV, CS + k * CV:CS + (k + 1) * CV], w["lu1"])
                sp.wait_ge(stored, 1)
                sp.dma_start(out.rearrange("(p j) c -> p j c", p=P), xs[:, :, :]).then_inc(stored, 16)
                sp.wait_ge(stored, 17)

            @block.gpsimd
            def _(pool):
                nc.gpsimd.memset(room[:, w5_at:w5_end], 0.0).then_inc(cleared5, 1)
                pool.wait_ge(cats_made, 7)

                def body(j):
                    for k in (1, 2):
                        wait(pool, q110_made, j.back(1))
                        l, r = outer_product(of(x1, j, slice(k * CV, (k + 1) * CV)),
                                             a1x1[:, bass.ds(j.number(1), 1), k, 0:CV].rearrange("p o c -> p (o c)"))
                        nc.gpsimd.tensor_tensor(q_part[k - 1].rearrange("p (u v) -> p u v", u=CV), l, r,
                                                ALU.mult).then_inc(q_rest.sem, 1)
                    wait(pool, q_rest, j, 1)
                    nc.gpsimd.tensor_tensor(q_part[0], q_part[0], q_part[1], ALU.add).then_inc(q_rest.sem, 1)
                    for k in range(3):
                        zk = zbuf[k % 2]
                        wait(pool, z_made, j, k)
                        nc.gpsimd.tensor_tensor(zk[:, 0:YW // 2], zk[:, 0:YW // 2], zk[:, YW // 2:YW],
                                                ALU.add).then_inc(z_halved.sem, 1)

                tiles(pool, body)

            @block.vector
            def _(dve):
                dv = Count(dve5)
                dve.wait_ge(aggs_loaded, 16 * T)
                agg = tab5[0]
                for k in range(1, T):
                    dv(nc.vector.tensor_tensor(agg, agg, tab5[k], ALU.add))
                    dv.wait(dve)
                nc.vector.tensor_copy(x0a0[:, :, CS:2 * CS], agg[:, :, 0:CS]).then_inc(cats_made, 1)
                for k in range(3):
                    nc.vector.tensor_copy(a1x1[:, :, k, 0:CV], agg[:, :, CS + k * CV:CS + (k + 1) * CV]).then_inc(cats_made, 1)
                dve.wait_ge(x_copied, 1 + 3)
                for k in range(3):
                    nc.vector.tensor_copy(a1x1[:, :, k, CV:2 * CV], x1[:, :, k * CV:(k + 1) * CV]).then_inc(cats_made, 1)
                dv(nc.vector.tensor_tensor(xs[:, :, :], xs[:, :, :], hs[:, :, :], ALU.add))
                dve.wait_ge(cats_made, 7)

                def q000(j, half):
                    n = CS // 2
                    if half == 0:
                        wait(dve, q_turned, j.back(1))
                    l, r = outer_product(of(x0a0, j, slice(n * half, n * half + n)), of(x0a0, j, slice(CS, 2 * CS)))
                    nc.vector.tensor_tensor(q[:, n * CS * half:n * CS * (half + 1)].rearrange("p (u v) -> p u v", u=n),
                                            l, r, ALU.mult).then_inc(q000_made.sem, 1)

                def terms(j, k):
                    if k == 0:
                        wait(dve, y_made, j)
                    if k < 2:
                        wait(dve, z_summed, j.back(1), 2 if k == 0 else 1)
                    else:
                        wait(dve, z_summed, j, 0)
                    factor = a1x1[:, bass.ds(j.number(1), 1), k, :].rearrange("p o c -> p (o c)")
                    nc.vector.tensor_tensor(zbuf[k % 2].rearrange("p (s w) -> p s w", w=CV),
                                            ps[0:P, 0:4, :].rearrange("p b (s w) -> p (b s) w", w=CV),
                                            factor.unsqueeze(2).broadcast_to([P, 2 * CV, CV]), ALU.mult).then_inc(z_made.sem, 1)

                def total(j, k):
                    wait(dve, z_halved, j, k)
                    nc.vector.tensor_reduce(slots[:, bass.ds(j.number(1), 1), k, :],
                                            zbuf[k % 2][:, 0:YW // 2].rearrange("p (s w) -> p w s", w=CV).unsqueeze(1),
                                            AX.X, ALU.add).then_inc(z_summed.sem, 1)

                def body(j):
                    q000(j, 0)
                    if j.back(1).exists():
                        total(j.back(1), 2)
                    q000(j, 1)
                    wait(dve, q110_made, j.back(1))
                    l, r = outer_product(of(x1, j, slice(0, CV)),
                                         a1x1[:, bass.ds(j.number(1), 1), 0, 0:CV].rearrange("p o c -> p (o c)"))
                    nc.vector.tensor_tensor(q[:, Q0:Q0 + Q1].rearrange("p (u v) -> p u v", u=CV), l, r,
                                            ALU.mult).then_inc(q_started.sem, 1)
                    terms(j, 0)
                    terms(j, 1)
                    wait(dve, q_started, j)
                    wait(dve, q_rest, j)
                    nc.vector.tensor_tensor(q[:, Q0:Q0 + Q1], q[:, Q0:Q0 + Q1], q_part[0], ALU.add).then_inc(q110_made.sem, 1)
                    total(j, 0)
                    terms(j, 2)
                    total(j, 1)

                tiles(dve, body)
                total(Group(0, NT - 1, 1), 2)
                dve.wait_ge(z_summed.sem, 3 * NT)
                dve.wait_ge(tile_kept.sem, NT)
                dv.wait(dve)
                dv(nc.vector.tensor_tensor(outs[:, :, CS:D], outs[:, :, CS:D], slots.rearrange("p j k w -> p j (k w)"), ALU.add))
                dv(nc.vector.tensor_tensor(xs[:, :, 0:CS], xs[:, :, 0:CS], outs[:, :, 0:CS], ALU.add))
                dv.wait(dve)
                v = xs[:, :, CS:D].rearrange("p j (c k) -> p j c k", k=3)
                for k in range(3):
                    dv(nc.vector.tensor_tensor(v[:, :, :, k], v[:, :, :, k], outs[:, :, CS + k * CV:CS + (k + 1) * CV], ALU.add))
                dve.wait_ge(dve5, dv.n)
                dve.sem_inc(stored, 1)

            @block.scalar
            def _(act):
                nc.scalar.activation(x0a0[:, :, 0:CS], hs[:, :, 0:CS], ACT.Copy).then_inc(x_copied, 1)
                v = hs[:, :, CS:D].rearrange("p j (c k) -> p k j c", k=3)
                for k in range(3):
                    nc.scalar.activation(x1[:, :, k * CV:(k + 1) * CV], v[:, k], ACT.Copy).then_inc(x_copied, 1)
                for r in (0, 64):
                    nc.scalar.activation(both[r:r + CS, :], ident[r:r + CS, r:r + CS], ACT.Copy).then_inc(both_made, 1)
                act.wait_ge(cats_made, 7)
                act.wait_ge(weights5_loaded.sem, weights5_loaded.n)
                for t, f in ((wQ[:, 0:Q0 // 2], K0), (wQ[:, Q0 // 2:], K0 * S3), (wY, K1), (wLA, CS ** -0.5), (wLB, CV ** -0.5)):
                    nc.scalar.mul(t, t, f).then_inc(scaled5, 1)

                def keep(out_, in_, ev):
                    nc.scalar.activation(out_, in_, ACT.Copy).then_inc(ev.sem, 1)

                def take(j):
                    wait(act, cat_turned, j.back(1))
                    keep(cat_tile, of(x0a0, j, slice(0, 2 * CS)), tile_taken)
                    keep(x1_tile, of(x1, j, slice(0, 3 * CV)), tile_taken)
                    wait(act, cat_turned, j)
                    wait(act, y_made, j.back(1))
                    wait(act, tile_made, j.back(1))
                    keep(catT, ps[:, 7, 0:P], cat_kept)
                    keep(x1T[0:96, :], ps[0:96, 7, 128:128 + P], cat_kept)

                def body(j):
                    take(j)
                    for k in range(QUADS):
                        wait(act, q_turned, j, k)
                        if k >= 3:
                            wait(act, q_used, j, k - 3)
                        else:
                            wait(act, q_used, j.back(1), QUADS - 3 + k)
                        keep(qT[k % 3], ps[:, 4 + k % 2, 0:W], q_kept)
                    wait(act, q_used, j)
                    wait(act, tile_made, j.back(1))
                    keep(sumT, ps[:, 6, 0:P], sum_kept)
                    wait(act, tile_made, j)
                    keep(outs[:, bass.ds(j.number(1), 1), :], ps[0:P, 7:8, 256:256 + D], tile_kept)

                tiles(act, body)

            @block.tensor
            def _(pe):
                pe.wait_ge(scaled5, 5)
                pe.wait_ge(both_made, 2)
                pe.wait_ge(cats_made, 7)

                def turn_quad(j, k):
                    if k in (0, 4):
                        wait(pe, q000_made, j, k // 4)
                    if k == 8:
                        wait(pe, q110_made, j)
                    if k >= 2:
                        wait(pe, q_kept, j, k - 2)
                    else:
                        wait(pe, q_kept, j.back(1), QUADS - 2 + k)
                    for c in range(4):
                        at = 128 * (4 * k + c)
                        ins = nc.tensor.transpose(ps[:, 4 + k % 2, c * P:(c + 1) * P], q[:, at:at + 128], ident[0:P, 0:P])
                    ins.then_inc(q_turned.sem, 1)

                def add_quad(j, k):
                    wait(pe, q_kept, j, k)
                    if k == 0:
                        wait(pe, sum_kept, j.back(1))
                    for c in range(4):
                        n, r = 4 * k + c, CS * (c % 2)
                        ins = nc.tensor.matmul(ps[r:r + CS, 6, 0:P], wQ[:, n * CS:(n + 1) * CS], qT[k % 3][:, c * P:(c + 1) * P],
                                               start=(n < 2), stop=True, skip_group_check=True)
                    ins.then_inc(q_used.sem, 1)

                def body(j):
                    wait(pe, tile_kept, j.back(1))
                    wait(pe, tile_taken, j)
                    nc.tensor.transpose(ps[:, 7, 0:P], cat_tile, ident[0:P, 0:P]).then_inc(cat_turned.sem, 1)
                    nc.tensor.transpose(ps[0:96, 7, 128:128 + P], x1_tile, ident[0:P, 0:P]).then_inc(cat_turned.sem, 1)
                    wait(pe, cat_kept, j)
                    wait(pe, z_made, j.back(1))
                    for k in range(YW // 512):
                        ins = nc.tensor.matmul(ps[0:P, k, :], catT, wY[:, 512 * k:512 * (k + 1)], start=True, stop=True)
                    ins.then_inc(y_made.sem, 1)
                    turn_quad(j, 0)
                    for k in range(QUADS):
                        if k + 1 < QUADS:
                            turn_quad(j, k + 1)
                        add_quad(j, k)
                    o = ps[0:P, 7, 256:256 + D]
                    nc.tensor.matmul(o, catT, wLA, start=True, stop=False)
                    nc.tensor.matmul(o, x1T[0:96, :], wLB[0:96, :], start=False, stop=True)
                    wait(pe, sum_kept, j)
                    nc.tensor.matmul(o[:, 0:CS], sumT, both, start=False, stop=True, skip_group_check=True).then_inc(tile_made.sem, 1)

                tiles(pe, body)

WEIGHTS = {
    "L0_gnn_": ["gamma_s", "beta_s", "gamma_v", "Ws_src", "Wv_src", "Ws_dst", "Wv_dst", "W_rbf", "W_alpha",
                "alpha_dot", "Ws_val", "Wv_val", "Wg", "w2_ss", "w2_sv", "w2_vs", "w2_vv0", "w2_vv1",
                "Ws_vlin", "Wv_vlin", "Wps", "Wpv"],
    "L1_gnn_": ["wm000", "wm011", "wm101", "wm110", "lm0", "lm1", "wu000", "wu011", "wu101", "wu110", "lu0", "lu1"],
}

def kernel(**inputs):
    import numpy as np
    import concourse.bacc as bacc
    from concourse.bass_utils import run_bass_kernel_spmd

    nc = bacc.Bacc("TRN2", target_bir_lowering=False, num_devices=1)
    arrays = {}

    def given(name):
        a = np.ascontiguousarray(inputs[name])
        arrays[f"in_{name}"] = a
        return nc.dram_tensor(f"in_{name}", a.shape, mybir.dt.from_np(a.dtype), kind="ExternalInput").ap()

    args = [given(n) for n in ("x", "src", "dst", "edge_attr_16", "edge_attr_4")]
    weights = {n: given(prefix + n) for prefix, names in WEIGHTS.items() for n in names}
    out = nc.dram_tensor("out_x", (N, D), F32, kind="ExternalOutput").ap()
    build(nc, *args, weights, out)
    r = run_bass_kernel_spmd(nc, [arrays], core_ids=[0])
    return r.results[0]["out_x"]
```
